# Optimizing a Trainium2 kernel written in Bass

```python
import numpy as np
import jax
import jax.numpy as jnp

def _softmax(x, axis=-1):
    return jax.nn.softmax(x, axis=axis)

def _gelu(x):
    return jax.nn.gelu(x, approximate=True)

def _silu(x):
    return jax.nn.silu(x)

def _sigmoid(x):
    return jax.nn.sigmoid(x)

def _layernorm(x, axis=-1, eps=1e-05):
    m = jnp.mean(x, axis=axis, keepdims=True)
    v = jnp.var(x, axis=axis, keepdims=True)
    return (x - m) / jnp.sqrt(v + eps)

def _scatter_add(tgt, idx, src, axis=0):
    return tgt.at[idx].add(src)

def _segment_sum(src, seg, n):
    return jax.ops.segment_sum(src, seg, n)
kernel_name = 'mk_early_fusion_embed_d1_tok_img768_r4_80bb74'

def setup_inputs(seed: int=0):
    np.random.seed(seed)
    _w = jnp.asarray

    def _rec_inputs():
        import jax
        import jax.numpy as jnp
        _rk = jax.random.key(seed)
        x = -0.000348323 + 0.999952 * jax.random.normal(jax.random.fold_in(_rk, 1), (32, 3, 96, 96), jnp.float32)
        x_txt = jax.random.randint(jax.random.fold_in(_rk, 51), (32, 32), 0, 12564, jnp.int32)
        return (x, x_txt)
    x, x_txt = _rec_inputs()

    def _L0_tok_setup():
        import jax, jax.numpy as jnp
        import numpy as np
        PATCH = 16

        def _patchify(x, p):
            B, C, H, W = x.shape
            nH, nW = (H // p, W // p)
            t = x.reshape(B, C, nH, p, nW, p)
            t = t.transpose(0, 2, 4, 3, 5, 1)
            return t.reshape(B, nH * nW, p * p * C)
        key = jax.random.key(seed)
        kx, kw = jax.random.split(key)
        B, C, H, W = (32, 3, 96, 96)
        embed_dim = 192
        in_feat = PATCH * PATCH * C * 5
        x = jax.random.normal(kx, (B, C, H, W), dtype=jnp.float32)
        Wm = jax.random.normal(kw, (embed_dim, in_feat), dtype=jnp.float32) * 0.02
        b = jnp.zeros((embed_dim,), dtype=jnp.float32)
        gamma = jnp.ones((embed_dim,), dtype=jnp.float32)
        beta = jnp.zeros((embed_dim,), dtype=jnp.float32)
        return {'x': x, 'W': Wm, 'b': b, 'gamma': gamma, 'beta': beta}
    _L0_tok_all = _L0_tok_setup()
    _L0_tok_in = {k: v for k, v in _L0_tok_all.items() if k in ('W', 'b', 'gamma', 'beta')}
    del _L0_tok_all

    def _L0_txt_setup():
        import jax, jax.numpy as jnp
        import numpy as np
        VOCAB = 50257
        DIM = 192
        B, S = (8, 512)
        key = jax.random.key(seed)
        k1, k2 = jax.random.split(key)
        x = jax.random.randint(k1, (B, S), 0, VOCAB, dtype=jnp.int64 if jax.config.jax_enable_x64 else jnp.int32)
        weight = jax.random.normal(k2, (VOCAB, DIM), dtype=jnp.float32)
        return {'x': x, 'weight': weight}
    _L0_txt_all = _L0_txt_setup()
    _L0_txt_in = {k: v for k, v in _L0_txt_all.items() if k in ('weight',)}
    del _L0_txt_all

    def _L0_attn_setup():
        import jax, jax.numpy as jnp
        import numpy as np
        NUM_HEADS = 12
        TOP_K = 32

        def _ex_quant(t):
            a = jnp.abs(t)
            e = jnp.floor(jnp.log2(jnp.where(a > 0, a, jnp.ones_like(a))))
            return jnp.where(a > 0, jnp.sign(t) * jnp.exp2(e), jnp.zeros_like(t))
        key = jax.random.key(seed)
        k0, k1, k2 = jax.random.split(key, 3)
        B, N, C = (8, 256, 192)
        x = jax.random.normal(k0, (B, N, C), jnp.float32)
        qkv_w = jax.random.normal(k1, (3 * C, C), jnp.float32) * 0.02
        qkv_b = jnp.zeros((3 * C,), jnp.float32)
        proj_w = jax.random.normal(k2, (C, C), jnp.float32) * 0.02
        proj_b = jnp.zeros((C,), jnp.float32)
        return {'x': x, 'qkv_w': qkv_w, 'qkv_b': qkv_b, 'proj_w': proj_w, 'proj_b': proj_b}
    _L0_attn_all = _L0_attn_setup()
    _L0_attn_in = {k: v for k, v in _L0_attn_all.items() if k in ('qkv_w', 'qkv_b', 'proj_w', 'proj_b')}
    del _L0_attn_all

    def _L0_ffn_setup():
        import jax, jax.numpy as jnp
        import numpy as np
        B, S, D = (2, 256, 192)
        NF, NR, R, DS, K = (128, 128, 128, 64, 4)

        @jax.checkpoint
        def feature_fn(x, neurons, weights):
            all_h = jnp.einsum('bsd,ndr->bsnr', x, neurons)
            return jnp.einsum('bsnr,bsn->bsr', all_h, weights)

        @jax.checkpoint
        def restore_fn(h, neurons, weights):
            all_out = jnp.einsum('bsr,nrd->bsnd', h, neurons)
            return jnp.einsum('bsnd,bsn->bsd', all_out, weights)

        def topk_sparsify(weights, k):
            topk_vals, topk_idx = jax.lax.top_k(weights, k)
            N = weights.shape[-1]
            one_hot_mask = jax.nn.one_hot(topk_idx, N, dtype=weights.dtype)
            sparse = (one_hot_mask * topk_vals[..., jnp.newaxis]).sum(axis=-2)
            sparse = sparse / (sparse.sum(axis=-1, keepdims=True) + 1e-08)
            return (sparse, topk_idx)
        key = jax.random.key(seed)
        ks = jax.random.split(key, 8)
        x = jax.random.normal(ks[0], (B, S, D), jnp.float32)
        f_know = jax.random.normal(ks[1], (NF, D, R), jnp.float32) * 0.02
        r_know = jax.random.normal(ks[2], (NR, R, D), jnp.float32) * 0.02
        W_fk = jax.random.normal(ks[3], (D, DS), jnp.float32) * 0.02
        b_fk = jnp.zeros((DS,), jnp.float32)
        W_rk = jax.random.normal(ks[4], (D, DS), jnp.float32) * 0.02
        b_rk = jnp.zeros((DS,), jnp.float32)
        emb_fk = jax.random.normal(ks[5], (NF, DS), jnp.float32) * 0.02
        emb_rk = jax.random.normal(ks[6], (NR, DS), jnp.float32) * 0.02
        return {'x': x, 'f_know': f_know, 'r_know': r_know, 'W_fk': W_fk, 'b_fk': b_fk, 'W_rk': W_rk, 'b_rk': b_rk, 'emb_fk': emb_fk, 'emb_rk': emb_rk}
    _L0_ffn_all = _L0_ffn_setup()
    _L0_ffn_in = {k: v for k, v in _L0_ffn_all.items() if k in ('f_know', 'r_know', 'W_fk', 'b_fk', 'W_rk', 'b_rk', 'emb_fk', 'emb_rk')}
    del _L0_ffn_all
    return {'x': x, 'x_txt': x_txt, 'L0_tok_W': _L0_tok_in['W'], 'L0_tok_b': _L0_tok_in['b'], 'L0_tok_gamma': _L0_tok_in['gamma'], 'L0_tok_beta': _L0_tok_in['beta'], 'L0_txt_weight': _L0_txt_in['weight'], 'L0_attn_qkv_w': _L0_attn_in['qkv_w'], 'L0_attn_qkv_b': _L0_attn_in['qkv_b'], 'L0_attn_proj_w': _L0_attn_in['proj_w'], 'L0_attn_proj_b': _L0_attn_in['proj_b'], 'L0_ffn_f_know': _L0_ffn_in['f_know'], 'L0_ffn_r_know': _L0_ffn_in['r_know'], 'L0_ffn_W_fk': _L0_ffn_in['W_fk'], 'L0_ffn_b_fk': _L0_ffn_in['b_fk'], 'L0_ffn_W_rk': _L0_ffn_in['W_rk'], 'L0_ffn_b_rk': _L0_ffn_in['b_rk'], 'L0_ffn_emb_fk': _L0_ffn_in['emb_fk'], 'L0_ffn_emb_rk': _L0_ffn_in['emb_rk']}

def reference(x, x_txt, L0_tok_W, L0_tok_b, L0_tok_gamma, L0_tok_beta, L0_txt_weight, L0_attn_qkv_w, L0_attn_qkv_b, L0_attn_proj_w, L0_attn_proj_b, L0_ffn_f_know, L0_ffn_r_know, L0_ffn_W_fk, L0_ffn_b_fk, L0_ffn_W_rk, L0_ffn_b_rk, L0_ffn_emb_fk, L0_ffn_emb_rk):
    import jax
    import jax.numpy as jnp

    def _L0_tok_ref(x, W, b, gamma, beta):
        import jax, jax.numpy as jnp
        import numpy as np
        PATCH = 16

        def _patchify(x, p):
            B, C, H, W = x.shape
            nH, nW = (H // p, W // p)
            t = x.reshape(B, C, nH, p, nW, p)
            t = t.transpose(0, 2, 4, 3, 5, 1)
            return t.reshape(B, nH * nW, p * p * C)
        p = PATCH
        s = p // 2
        shifts = [(0, 0), (-s, -s), (-s, s), (s, -s), (s, s)]
        pats = [_patchify(jnp.roll(x, (dx, dy), axis=(2, 3)), p) for dx, dy in shifts]
        tokens = jnp.concatenate(pats, axis=-1)
        tokens = jnp.einsum('bnf,ef->bne', tokens, W) + b
        mean = jnp.mean(tokens, axis=-1, keepdims=True)
        var = jnp.var(tokens, axis=-1, keepdims=True)
        tokens = (tokens - mean) * jax.lax.rsqrt(var + 1e-05) * gamma + beta
        return tokens

    def _L0_txt_ref(x, weight):
        import jax, jax.numpy as jnp
        import numpy as np
        VOCAB = 50257
        DIM = 192
        B, S = (8, 512)
        return weight[x]

    def _L0_attn_ref(x, qkv_w, qkv_b, proj_w, proj_b):
        import jax, jax.numpy as jnp
        import numpy as np
        NUM_HEADS = 12
        TOP_K = 32

        def _ex_quant(t):
            a = jnp.abs(t)
            e = jnp.floor(jnp.log2(jnp.where(a > 0, a, jnp.ones_like(a))))
            return jnp.where(a > 0, jnp.sign(t) * jnp.exp2(e), jnp.zeros_like(t))
        B, N, C = x.shape
        H = NUM_HEADS
        d = C // H
        scale = 1.0 / jnp.sqrt(jnp.float32(d))
        qkv = x @ qkv_w.T + qkv_b
        qkv = qkv.reshape(B, N, 3, H, d).transpose(2, 0, 3, 1, 4)
        q, k, v = (qkv[0], qkv[1], qkv[2])
        true_scores = jnp.einsum('bhnd,bhmd->bhnm', q, k) * scale
        eq = _ex_quant(q)
        ek = _ex_quant(k)
        pred_scores = jnp.einsum('bhnd,bhmd->bhnm', eq, ek)
        _, idx = jax.lax.top_k(pred_scores, TOP_K)
        vals = jnp.take_along_axis(true_scores, idx, axis=-1)
        topk_attn = jax.nn.softmax(vals, axis=-1)
        bi = jnp.arange(B)[:, None, None, None]
        hi = jnp.arange(H)[None, :, None, None]
        ni = jnp.arange(N)[None, None, :, None]
        attn = jnp.zeros_like(true_scores).at[bi, hi, ni, idx].set(topk_attn)
        out = jnp.einsum('bhnm,bhmd->bhnd', attn, v)
        out = out.transpose(0, 2, 1, 3).reshape(B, N, C)
        out = out @ proj_w.T + proj_b
        return out

    def _L0_ffn_ref(x, f_know, r_know, W_fk, b_fk, W_rk, b_rk, emb_fk, emb_rk):
        import jax, jax.numpy as jnp
        import numpy as np
        B, S, D = (2, 256, 192)
        NF, NR, R, DS, K = (128, 128, 128, 64, 4)

        @jax.checkpoint
        def feature_fn(x, neurons, weights):
            all_h = jnp.einsum('bsd,ndr->bsnr', x, neurons)
            return jnp.einsum('bsnr,bsn->bsr', all_h, weights)

        @jax.checkpoint
        def restore_fn(h, neurons, weights):
            all_out = jnp.einsum('bsr,nrd->bsnd', h, neurons)
            return jnp.einsum('bsnd,bsn->bsd', all_out, weights)

        def topk_sparsify(weights, k):
            topk_vals, topk_idx = jax.lax.top_k(weights, k)
            N = weights.shape[-1]
            one_hot_mask = jax.nn.one_hot(topk_idx, N, dtype=weights.dtype)
            sparse = (one_hot_mask * topk_vals[..., jnp.newaxis]).sum(axis=-2)
            sparse = sparse / (sparse.sum(axis=-1, keepdims=True) + 1e-08)
            return (sparse, topk_idx)
        emb_fk_n = emb_fk / (jnp.linalg.norm(emb_fk, axis=-1, keepdims=True) + 1e-08)
        emb_rk_n = emb_rk / (jnp.linalg.norm(emb_rk, axis=-1, keepdims=True) + 1e-08)
        logits_fk = jnp.einsum('bsd,nd->bsn', x @ W_fk + b_fk, emb_fk_n)
        logits_rk = jnp.einsum('bsd,nd->bsn', x @ W_rk + b_rk, emb_rk_n)
        w_fk, _ = topk_sparsify(jax.nn.softmax(logits_fk, axis=-1), K)
        w_rk, _ = topk_sparsify(jax.nn.softmax(logits_rk, axis=-1), K)
        h = feature_fn(x, f_know, w_fk)
        out = restore_fn(h, r_know, w_rk)
        return out
    h = _L0_tok_ref(x, L0_tok_W, L0_tok_b, L0_tok_gamma, L0_tok_beta)
    h = jnp.concatenate([h, _L0_txt_ref(x_txt, L0_txt_weight)], axis=1)
    h = h + _L0_attn_ref(_layernorm(h, axis=-1), L0_attn_qkv_w, L0_attn_qkv_b, L0_attn_proj_w, L0_attn_proj_b)
    h = h + _L0_ffn_ref(_layernorm(h, axis=-1), L0_ffn_f_know, L0_ffn_r_know, L0_ffn_W_fk, L0_ffn_b_fk, L0_ffn_W_rk, L0_ffn_b_rk, L0_ffn_emb_fk, L0_ffn_emb_rk)
    return h

_drawn_inputs = setup_inputs


def setup_inputs(seed=0):
    import zlib

    import numpy as np

    out = dict(_drawn_inputs(seed))
    spreads = {'L0_tok_b': (0.0, 0.1),
     'L0_tok_gamma': (1.0, 0.2),
     'L0_tok_beta': (0.0, 0.1),
     'L0_attn_qkv_b': (0.0, 0.296),
     'L0_attn_proj_b': (0.0, 0.1),
     'L0_ffn_b_fk': (0.0, 0.671),
     'L0_ffn_b_rk': (0.0, 0.663)}
    factors = {'L0_attn_qkv_w': 3.818,
     'L0_ffn_f_know': 3.694,
     'L0_ffn_r_know': 3.695,
     'L0_ffn_W_fk': 3.788,
     'L0_ffn_W_rk': 3.805,
     'L0_ffn_emb_fk': 3.785,
     'L0_ffn_emb_rk': 3.753}
    for name, (base, spread) in spreads.items():
        noise = np.random.default_rng([zlib.crc32(name.encode()), seed]).standard_normal(out[name].shape)
        drawn = base * np.exp(spread * noise) if base else spread * noise
        out[name] = jnp.asarray(drawn.astype(out[name].dtype))
    for name, factor in factors.items():
        out[name] = (out[name] * factor).astype(out[name].dtype)
    return out
```

```python
from contextlib import ExitStack

import numpy as np

import concourse.bass as bass
from concourse import mybir

F32 = mybir.dt.float32
BF16 = mybir.dt.bfloat16
I32 = mybir.dt.int32
U32 = mybir.dt.uint32
U16 = mybir.dt.uint16
ALU = mybir.AluOpType
ACT = mybir.ActivationFunctionType
AX = mybir.AxisListType

BATCH, CHANNELS, IMAGE, PATCH = 32, 3, 96, 16
D = 192
HALF = D // 2
HALO = 2 * (IMAGE // PATCH) + 2
GRID = IMAGE // PATCH
NPATCH = GRID * GRID
NTEXT = 32
S = NPATCH + NTEXT
T = BATCH * S
PAIRS = BATCH // 2
BLOCK_F = 8 * 8 * CHANNELS
HEADS, HD, TOPK = 12, 16, 32
HH = HEADS // 2
ROWS = HH * S // 4
EPS = 1e-5
SCALE = 0.25
TAKEN = -3.0e38
BIG = 1.0e30
NE, R, DS, K4 = 128, 128, 64, 4
P = 128
NT = T // P
TILES = T * K4 // P + NE
SLOTS = TILES * P
N_ZERO = -(-TILES * D // 2048) - (-TILES * R // 2048)
DEPTH = 4


def build(nc, a_x, l_x, text_ids, w_shift_a, w_shift_l, w_mid_a, w_mid_l, tok_vec, tok_bias, vocab,
          w_qkv, qk_bias, row_vec, w_proj, f_know, r_know, w_route, route_bias, emb, out):
    ctx = ExitStack()
    with ctx:
        def sb(name, shape, dt=F32):
            return ctx.enter_context(nc.sbuf_tensor(name, shape, dt))

        sem = {}

        def S_(name):
            sem[name] = ctx.enter_context(nc.semaphore(name))

        def dram(name, shape, dt=F32):
            return nc.dram_tensor(name, shape, dt, kind="Internal").ap()

        h0 = dram("h0", [T, D])
        h1 = dram("h1", [T, D])
        xn2 = dram("xn2", [T, D])
        slots_x = dram("slots_x", [SLOTS, D])
        slots_h = dram("slots_h", [SLOTS, R])
        slots_g = dram("slots_g", [SLOTS, R])
        slots_y = dram("slots_y", [SLOTS, D])

        ident = sb("ident", [P, P])
        ones_f = sb("ones_f", [P, P])
        ones_b = sb("ones_b", [P, P], BF16)
        upper_b = sb("upper_b", [P, P], BF16)
        upper_f = sb("upper_f", [P, P])
        upper_in = sb("upper_in", [P, P])
        eps_col = sb("eps_col", [P, 1])
        minus_half = sb("minus_half", [P, 1])
        iota_e = sb("iota_e", [P, NE])
        iota_t = sb("iota_t", [P, TILES])
        head_mask = sb("head_mask", [HALF, HH])
        wa = sb("wa", [P, 16, D])
        wl = sb("wl", [P, 8, D])
        wma = sb("wma", [P, 4, D])
        wml = sb("wml", [P, 2, D])
        tok_row = sb("tok_row", [P, 2, D])
        tok_b = sb("tok_b", [HALF, 2])
        qkv = sb("qkv", [HALF, 2, 3 * D])
        qk_b = sb("qk_b", [HALF, 4])
        row_b = sb("row_b", [P, 2, D])
        wp = sb("wp", [HALF, 2, D])
        w_rt = sb("w_rt", [HALF, 2, P])
        rt_b = sb("rt_b", [P, 1])
        emb_n = sb("emb_n", [P, 2, DS])
        emb_t = sb("emb_t", [P, 2 * NE])
        zero = sb("zero", [P, 2048])

        ids = sb("ids", [P, 8], I32)
        text = sb("text", [P, 8, D])
        xa = sb("xa", [P, 2, HALO, HALO])
        xl = sb("xl", [P, 2, HALO, HALO // 2])
        tokT = sb("tokT", [HALF, 2, 2 * NPATCH])
        tok = sb("tok", [2 * NPATCH, D])
        tok2 = sb("tok2", [2 * NPATCH, D])
        tstat = sb("tstat", [2 * NPATCH, 8])
        tmv = sb("tmv", [2 * NPATCH, 4])

        hb = sb("hb", [S, 2, D])
        hbp = sb("hbp", [S, 2, D])
        stat = sb("stat", [S, 8])
        mv = sb("mv", [S, 4])
        xn = sb("xn", [S, D])
        xnT = sb("xnT", [HALF, 2, S])
        qk = sb("qk", [HALF, 2, 4, S])
        ek = sb("ek", [HALF, 2, S], BF16)
        qbd = sb("qbd", [HALF, 2, HH, S])
        eqbd = sb("eqbd", [HALF, 2, HH, S], BF16)
        vm = sb("vm", [S, 2, HEADS, HALF])
        work = sb("work", [ROWS, 2, 8, S])
        tru = sb("tru", [ROWS, 2, 8, S])
        top8 = sb("top8", [ROWS, 8, 8])
        sc1 = sb("sc1", [ROWS, 8, S])
        sc2 = sb("sc2", [ROWS, 8, S])
        smax = sb("smax", [ROWS, 8])
        ssum = sb("ssum", [ROWS, 8])
        srec = sb("srec", [ROWS, 8])
        pT = sb("pT", [S, 2, HH * S])
        oT = sb("oT", [HALF, 2, S])
        h1b = sb("h1b", [S, 2, D])

        t_h = sb("t_h", [P, 2, D])
        t_stat = sb("t_stat", [P, 8])
        t_mv = sb("t_mv", [P, 4])
        t_xn = sb("t_xn", [P, 2, D])
        t_xT = sb("t_xT", [HALF, 2, P])
        t_q = sb("t_q", [P, P])
        t_e = sb("t_e", [P, 2, NE])
        t_p = sb("t_p", [P, 2, NE])
        t_m = sb("t_m", [P, 8])
        t_top = sb("t_top", [P, 2, 8])
        t_idx = sb("t_idx", [P, 2, 8], U32)
        t_idf = sb("t_idf", [P, 2, 8])
        weights = sb("weights", [P, NT, 2, K4])
        pick = sb("pick", [P, NT, 2, K4, NE], BF16)
        place = sb("place", [P, NT, 2, NE])
        count = sb("count", [P, 2, NE])
        emb_s = sb("emb_s", [P, 2, DS])
        emb_m = sb("emb_m", [P, 8])
        ntile_i = sb("ntile_i", [P, 4], I32)
        ntile = sb("ntile", [P, 2])
        ntile_b = sb("ntile_b", [P, 2, NE])
        base = sb("base", [P, 2, NE])
        ends = sb("ends", [P, 2])
        ended = sb("ended", [P, 2, TILES])
        tile_e = sb("tile_e", [P, 2 * TILES], I32)
        s_at = sb("s_at", [P, NE])
        s_prod = sb("s_prod", [P, K4, NE])
        s_f = sb("s_f", [P, K4])
        s_idx = sb("s_idx", [P, 2, K4], I32)
        s_all = sb("s_all", [P, 2, NT, K4], I32)
        g_idx = sb("g_idx", [P, 2, K4], I32)
        g_in = sb("g_in", [P, 2, K4, D])
        g_sum = sb("g_sum", [P, 2, D])
        m_w = sb("m_w", [P, DEPTH, 2 * P])
        m_x = sb("m_x", [P, DEPTH, D])
        m_xT = sb("m_xT", [P, 2, 2 * P])
        m_y = sb("m_y", [P, DEPTH, D])

        bank = [ctx.enter_context(nc.psum_tensor(f"bank{i}", [P, 512], F32)) for i in range(8)]
        ps_pred = bank[0:2]
        ps_true = bank[2:4]
        ps_front, ps_vp, ps_pt, ps_eo = bank[4], bank[5], bank[6], bank[7]

        for name in (
            "consts", "weights_in", "biases_in", "mid_in", "zeroed", "slots_zeroed", "ids_in", "text_in", "text_out",
            "c_memset", "c_select", "c_iota", "w_sum",
            "x_in", "emb_mm", "emb_turned", "emb_copied", "emb_bias", "emb_stat", "emb_aggr", "emb_rstd", "emb_eps", "ln_eps", "emb_norm", "emb_gamma", "emb_done", "emb_out",
            "hb_in0", "hb_in1", "ln_stat", "ln_aggr", "ln_rstd", "ln_done", "hbp_done", "xt_mm", "xt_copied", "qk_mm", "v_mm",
            "qk_copied", "ek_done", "qbd_done", "eqbd_done", "v_done", "score_mm", "score_copied",
            "topk", "dve_steps", "gap_done", "masked", "smax_done", "shifted", "exp_done", "ssum_done", "srec_done", "prob_done",
            "pt_mm", "pt_copied", "ot_mm", "ot_copied", "proj_mm", "h1_done", "h1_out0", "h1_out1",
            "emb_sq", "emb_ss", "emb_root", "emb_eps2", "emb_rec", "emb_scaled", "emb_flip", "emb_ready",
            "t_in0", "t_in1", "t_stat", "t_aggr", "t_eps", "t_rstd", "t_norm", "xn_out0", "xn_out1", "t_turn", "t_xt", "t_qmm",
            "t_qd", "t_logit", "t_max", "t_shift", "t_exp", "route", "t_pick", "t_pos", "t_placed", "fresh", "base_steps",
            "count_turn", "base_mm", "ends_mm", "ended_mm", "tiles_known",
            "slot_steps0", "slot_steps1", "slot_ready0", "slot_ready1", "stg_in0", "stg_in1", "sent0", "sent1", "back_ready1", "back_ready2",
            "got0_1", "got1_1", "got0_2", "got1_2", "sum_steps1", "sum_steps2", "summed1", "summed2",
            "resent0", "resent1", "res_in0", "res_in1", "out_done0", "out_done1", "pool_steps",
            *[f"m_in{r}{d}" for r in range(2) for d in range(DEPTH)],
            *[f"m_out{r}{d}" for r in range(2) for d in range(DEPTH)],
            *[f"{n}{r}" for r in range(2) for n in ("m_turn", "m_xt", "m_mm", "m_done")],
        ):
            S_(name)

        block = ctx.enter_context(nc.Block())

        def own16(b, par):
            return b * 8 + (16 - 8 * par)

        def slots_of(eng, slot):
            slot(0, 0)
            slot(1, 1)
            with eng.Fori(2, BATCH - 2, 2) as b:
                slot(b, 0)
                slot(b + 1, 1)
            for b in range(BATCH - 2, BATCH + 2):
                slot(b, b % 2)

        def is_static(b):
            return isinstance(b, int)

        def runs(b, lo, hi):
            return not is_static(b) or lo <= b <= hi

        def tiles_of(eng, body):
            body(0, 0)
            body(1, 1)
            with eng.Fori(2, NT - 2, 2) as i:
                body(i, 0)
                body(i + 1, 1)
            body(NT - 1, 0)

        def tiles_ahead(eng, ahead, body):
            ahead(0, 0)
            ahead(1, 1)
            body(0, 0)
            ahead(2, 0)
            body(1, 1)
            with eng.Fori(2, NT - 2, 2) as i:
                ahead(i + 1, 1)
                body(i, 0)
                ahead(i + 2, 0)
                body(i + 1, 1)
            body(NT - 1, 0)

        def own(i, par, each):
            return i * (each // 2) + (each - each // 2 * par)

        def matmuls_of(eng, body):
            for d in range(DEPTH):
                body(d, d)
            with eng.Fori(DEPTH, TILES - DEPTH, DEPTH) as j:
                for d in range(DEPTH):
                    body(j + d, d)
            for d in range(DEPTH):
                body(TILES - DEPTH + d, d)

        def own_m(j, d, each):
            return j * (each // DEPTH) + (each - each // DEPTH * d)

        class Steps:

            def __init__(self, eng, name, per_tile):
                self.eng, self.sem, self.per, self.at, self.base = eng, sem[name], per_tile, per_tile, 0

            def start(self, i):
                assert self.at == self.per, self.at
                self.base, self.at = i * self.per, 0

            def done(self, ins):
                ins.then_inc(self.sem, 1)
                self.at += 1

            def wait(self):
                self.eng.wait_ge(self.sem, self.base + self.at)

        h0_pairs = h0.rearrange("(q s) d -> q s d", s=S)

        @block.sync
        def _(sp):
            sp.dma_start(ids[:], text_ids).then_inc(sem["ids_in"], 16)
            sp.dma_start(wa[:], w_shift_a).then_inc(sem["weights_in"], 16)
            sp.dma_start(wl[:], w_shift_l).then_inc(sem["weights_in"], 16)
            sp.dma_start(wma[:], w_mid_a).then_inc(sem["mid_in"], 16)
            sp.dma_start(wml[:], w_mid_l).then_inc(sem["mid_in"], 16)

            def load_images(p):
                sp.wait_ge(sem["emb_mm"], p)
                sp.dma_start(xa[:], a_x[p] if is_static(p) else a_x[bass.ds(p, 1)].squeeze(0)).then_inc(sem["x_in"], 16)
                sp.dma_start(xl[:], l_x[p] if is_static(p) else l_x[bass.ds(p, 1)].squeeze(0)).then_inc(sem["x_in"], 16)

            def store_patches(p):
                sp.wait_ge(sem["emb_done"], p + 1)
                for j in range(2):
                    row = (2 * p + j) * S
                    sp.dma_start(h0[bass.ds(row, NPATCH), :], tok2[j * NPATCH:(j + 1) * NPATCH, :]).then_inc(sem["emb_out"], 16)

            def load_h0(b, par):
                sp.wait_ge(sem["emb_out"], 32 * (b // 2 + 1) if is_static(b) else (b - par) * 16 + 32)
                if runs(b, 2, BATCH):
                    sp.wait_ge(sem["hbp_done"], b - 1)
                    sp.wait_ge(sem["ln_done"], b - 1)
                sp.dma_start(hb[:, par, :], h0[bass.ds(b * S, S), :]).then_inc(sem[f"hb_in{par}"], 16)

            load_images(0)
            sp.dma_start(tok_row[:], tok_vec).then_inc(sem["biases_in"], 16)
            sp.dma_start(tok_b[:], tok_bias).then_inc(sem["biases_in"], 16)
            sp.dma_start(qkv[:], w_qkv).then_inc(sem["biases_in"], 16)
            sp.dma_start(qk_b[:], qk_bias).then_inc(sem["biases_in"], 16)
            sp.dma_start(row_b[:], row_vec).then_inc(sem["biases_in"], 16)
            sp.dma_start(wp[:], w_proj).then_inc(sem["biases_in"], 16)
            sp.dma_start(w_rt[:], w_route).then_inc(sem["biases_in"], 16)
            sp.dma_start(rt_b[:], route_bias).then_inc(sem["biases_in"], 16)
            sp.dma_start(emb_n[:], emb).then_inc(sem["biases_in"], 16)
            store_patches(0)
            sp.wait_ge(sem["text_out"], 16 * 32)
            load_h0(0, 0)

            def slot(b, par):
                if runs(b, 0, BATCH - 2):
                    load_h0(b + 1, 1 - par)
                embeds = par == 0 and runs(b, 0, BATCH - 3)
                if embeds:
                    load_images(b // 2 + 1)
                if runs(b, 2, BATCH + 1):
                    sp.wait_ge(sem["h1_done"], b - 1)
                    sp.dma_start(h1[bass.ds((b - 2) * S, S), :], h1b[:, par, :]).then_inc(sem[f"h1_out{par}"], 16)
                if embeds:
                    store_patches(b // 2 + 1)

            slots_of(sp, slot)

            for par in range(2):
                sp.wait_ge(sem[f"h1_out{par}"], 16 * (BATCH // 2))

            def load_h1(i, par):
                if not is_static(i) or i >= 2:
                    sp.wait_ge(sem["t_norm"], i - 1)
                sp.dma_start(t_h[:, par, :], h1[bass.ds(i * P, P), :]).then_inc(sem[f"t_in{par}"], 16)

            def store_xn(i, par):
                sp.wait_ge(sem["t_norm"], i + 1)
                sp.dma_start(xn2[bass.ds(i * P, P), :], t_xn[:, par, :]).then_inc(sem[f"xn_out{par}"], 16)

            load_h1(0, 0)
            load_h1(1, 1)
            with sp.Fori(0, NT - 3, 2) as i:
                store_xn(i, 0)
                load_h1(i + 2, 0)
                store_xn(i + 1, 1)
                load_h1(i + 3, 1)
            store_xn(NT - 3, 0)
            load_h1(NT - 1, 0)
            store_xn(NT - 2, 1)
            store_xn(NT - 1, 0)

            sp.wait_ge(sem["xn_out0"], 16 * 9)
            sp.wait_ge(sem["xn_out1"], 16 * 8)
            sp.wait_ge(sem["t_turn"], NT)

            def load_xn(i, par):
                if not is_static(i) or i >= 2:
                    sp.wait_ge(sem[f"sent{par}"], own(i - 2, par, 16 * K4))
                sp.dma_start(t_xn[:, par, :], xn2[bass.ds(i * P, P), :]).then_inc(sem[f"stg_in{par}"], 16)

            load_xn(0, 0)
            load_xn(1, 1)
            with sp.Fori(2, NT - 1, 2) as i:
                load_xn(i, 0)
                load_xn(i + 1, 1)
            load_xn(NT - 1, 0)

            def load_tiles(r, matrices, rows, arrays, width):
                def body(j, d):
                    if not is_static(j) or j >= DEPTH:
                        sp.wait_ge(sem[f"m_mm{r}"], j - DEPTH + 1)
                    e = sp.value_load(tile_e[0:1, bass.ds(j + r * TILES, 1)], min_val=0, max_val=NE - 1)
                    sp.dma_start(m_w[0:rows, d, 0:matrices.shape[2]], matrices[bass.ds(e, 1)].rearrange("e p f -> (e p) f")).then_inc(sem[f"m_in{r}{d}"], 16)
                    sp.dma_start(m_x[:, d, 0:width], arrays[bass.ds(j * P, P), :]).then_inc(sem[f"m_in{r}{d}"], 16)
                matmuls_of(sp, body)

            sp.wait_ge(sem["tiles_known"], 1)
            sp.wait_ge(sem["slots_zeroed"], 16 * N_ZERO)
            sp.wait_ge(sem["sent0"], 16 * K4 * 9)
            sp.wait_ge(sem["sent1"], 16 * K4 * 8)
            load_tiles(0, f_know.rearrange("e (p c) r -> e p (c r)", c=2), HALF, slots_x, D)
            sp.wait_ge(sem["resent0"], 16 * K4 * 9)
            sp.wait_ge(sem["resent1"], 16 * K4 * 8)
            load_tiles(1, r_know, P, slots_g, R)

            out_rows = out.rearrange("b s d -> (b s) d")

            def load_res(i, par):
                if not is_static(i) or i >= 2:
                    sp.wait_ge(sem["summed2"], i - 1)
                sp.dma_start(t_h[:, par, :], h1[bass.ds(i * P, P), :]).then_inc(sem[f"res_in{par}"], 16)

            def store_out(i, par):
                sp.wait_ge(sem["summed2"], i + 1)
                sp.dma_start(out_rows[bass.ds(i * P, P), :], g_sum[:, par, :]).then_inc(sem[f"out_done{par}"], 16)

            load_res(0, 0)
            load_res(1, 1)
            with sp.Fori(0, NT - 3, 2) as i:
                store_out(i, 0)
                load_res(i + 2, 0)
                store_out(i + 1, 1)
                load_res(i + 3, 1)
            store_out(NT - 3, 0)
            load_res(NT - 1, 0)
            store_out(NT - 2, 1)
            store_out(NT - 1, 0)
            sp.wait_ge(sem["out_done0"], 16 * 9)
            sp.wait_ge(sem["out_done1"], 16 * 8)

        @block.gpsimd
        def _(pool):
            nc.gpsimd.memset(ident[:], 0.0)
            nc.gpsimd.memset(minus_half[:], -0.5)
            nc.gpsimd.memset(eps_col[:], EPS)
            nc.gpsimd.memset(ones_f[:], 1.0)
            nc.gpsimd.memset(ones_b[:], 1.0)
            nc.gpsimd.memset(upper_b[:], 1.0)
            nc.gpsimd.memset(upper_f[:], 1.0)
            nc.gpsimd.memset(upper_in[:], 1.0)
            nc.gpsimd.memset(head_mask[:], 1.0).then_inc(sem["c_memset"], 1)
            pool.wait_ge(sem["c_memset"], 1)
            nc.gpsimd.affine_select(out=ident[:], in_=ident[:], compare_op=ALU.not_equal, fill=1.0, base=0,
                                    pattern=[[-1, P]], channel_multiplier=1)
            for m in (upper_b, upper_f):
                nc.gpsimd.affine_select(out=m[:], in_=m[:], compare_op=ALU.is_ge, fill=0.0, base=-1,
                                        pattern=[[1, P]], channel_multiplier=-1)
            nc.gpsimd.affine_select(out=upper_in[:], in_=upper_in[:], compare_op=ALU.is_ge, fill=0.0, base=0,
                                    pattern=[[1, P]], channel_multiplier=-1)
            nc.gpsimd.affine_select(out=head_mask[:], in_=head_mask[:], compare_op=ALU.is_ge, fill=0.0, base=0,
                                    pattern=[[-HD, HH]], channel_multiplier=1).then_inc(sem["c_select"], 1)
            pool.wait_ge(sem["c_select"], 1)
            nc.gpsimd.affine_select(out=head_mask[:], in_=head_mask[:], compare_op=ALU.is_ge, fill=0.0, base=HD - 1,
                                    pattern=[[HD, HH]], channel_multiplier=-1)
            nc.gpsimd.iota(iota_e[:], pattern=[[1, NE]], base=0, channel_multiplier=0,
                           allow_small_or_imprecise_dtypes=True)
            nc.gpsimd.iota(iota_t[:], pattern=[[1, TILES]], base=0, channel_multiplier=0,
                           allow_small_or_imprecise_dtypes=True).then_inc(sem["consts"], 1)

            pool.wait_ge(sem["ids_in"], 16)
            for g in range(8):
                nc.gpsimd.indirect_dma_start(text[:, g, :], None, vocab,
                                             bass.IndirectOffsetOnAxis(ids[:, g:g + 1], 0)).then_inc(sem["text_in"], 16)
            pool.wait_ge(sem["text_in"], 16 * 8)
            for g in range(8):
                for j in range(4):
                    pool.dma_start(h0_pairs[4 * g + j, NPATCH:S, :], text[32 * j:32 * j + 32, g, :]).then_inc(sem["text_out"], 16)
            pool.wait_ge(sem["zeroed"], 1)
            for arr, width in ((slots_x, D), (slots_g, R)):
                flat = arr.rearrange("(p s) d -> p (s d)", p=P)
                total = TILES * width
                for c in range(0, total, 2048):
                    w = min(2048, total - c)
                    pool.dma_start(flat[:, c:c + w], zero[:, 0:w]).then_inc(sem["slots_zeroed"], 16)

            def residual(b, par):
                pool.wait_ge(sem[f"hb_in{par}"], own16(b, par))
                if runs(b, 2, BATCH):
                    pool.wait_ge(sem["h1_done"], b - 1)
                nc.gpsimd.tensor_tensor(hbp[:, par, :], hb[:, par, :], row_b[0:S, 1, :], ALU.add).then_inc(sem["hbp_done"], 1)

            def spread(b, par):
                pool.wait_ge(sem["qk_copied"], b + 1)
                if runs(b, 1, BATCH):
                    pool.wait_ge(sem["score_mm"], b)
                for g in range(2):
                    last = nc.gpsimd.tensor_tensor(
                        qbd[:, g], qk[:, par, g, :].unsqueeze(1).to_broadcast([HALF, HH, S]),
                        head_mask[:].unsqueeze(2).to_broadcast([HALF, HH, S]), ALU.mult)
                last.then_inc(sem["qbd_done"], 1)

            def embed_rstd(p):
                pool.wait_ge(sem["emb_aggr"], p + 1)
                nc.gpsimd.tensor_tensor(tmv[:, 2:3], tmv[:, 1:2], eps_col[0:tmv.shape[0], :], ALU.add).then_inc(sem["emb_eps"], 1)
                pool.wait_ge(sem["emb_eps"], p + 1)
                nc.gpsimd.tensor_tensor(tmv[:, 3:4], tmv[:, 2:3], minus_half[0:tmv.shape[0], :], ALU.pow).then_inc(sem["emb_rstd"], 1)

            def rstd(b):
                pool.wait_ge(sem["ln_aggr"], b + 1)
                nc.gpsimd.tensor_tensor(mv[:, 2:3], mv[:, 1:2], eps_col[0:mv.shape[0], :], ALU.add).then_inc(sem["ln_eps"], 1)
                pool.wait_ge(sem["ln_eps"], b + 1)
                nc.gpsimd.tensor_tensor(mv[:, 3:4], mv[:, 2:3], minus_half[0:mv.shape[0], :], ALU.pow).then_inc(sem["ln_rstd"], 1)

            pool.wait_ge(sem["biases_in"], 16 * 9)
            embed_rstd(0)
            rstd(0)
            spread(0, 0)

            def slot(b, par):
                if runs(b, 0, BATCH - 2):
                    rstd(b + 1)
                if runs(b, 1, BATCH):
                    pool.wait_ge(sem["gap_done"], b)
                    if runs(b, 2, BATCH):
                        pool.wait_ge(sem["pt_mm"], 2 * b - 2)
                    nc.gpsimd.tensor_tensor(sc1[:], work[:, 1 - par], tru[:, 1 - par], ALU.add).then_inc(sem["masked"], 1)
                if runs(b, 0, BATCH - 2):
                    spread(b + 1, 1 - par)
                if runs(b, 1, BATCH):
                    pool.wait_ge(sem["smax_done"], b)
                    nc.gpsimd.tensor_tensor(sc2[:], sc1[:], smax[:].unsqueeze(2).to_broadcast([ROWS, 8, S]),
                                            ALU.subtract).then_inc(sem["shifted"], 1)
                if par == 0 and runs(b, 0, BATCH - 3):
                    embed_rstd(b // 2 + 1)
                if runs(b, 0, BATCH - 1):
                    residual(b, par)
                if runs(b, 1, BATCH):
                    pool.wait_ge(sem["srec_done"], b)
                    nc.gpsimd.tensor_tensor(sc1[:], sc2[:], srec[:].unsqueeze(2).to_broadcast([ROWS, 8, S]),
                                            ALU.mult).then_inc(sem["prob_done"], 1)

            slots_of(pool, slot)

            def t_rstd(i, par):
                pool.wait_ge(sem["t_aggr"], i + 1)
                nc.gpsimd.tensor_tensor(t_mv[:, 2:3], t_mv[:, 1:2], eps_col[:], ALU.add).then_inc(sem["t_eps"], 1)
                pool.wait_ge(sem["t_eps"], i + 1)
                nc.gpsimd.tensor_tensor(t_mv[:, 3:4], t_mv[:, 2:3], minus_half[:], ALU.pow).then_inc(sem["t_rstd"], 1)

            tiles_of(pool, t_rstd)

            pool.wait_ge(sem["slots_zeroed"], 16 * N_ZERO)

            def scatter(src, dst, width, idx, par, done):
                nc.gpsimd.sem_inc(sem["pool_steps"], 1)
                for k in range(K4):
                    nc.gpsimd.indirect_dma_start(dst, bass.IndirectOffsetOnAxis(idx[:, par, k:k + 1], 0),
                                                 src[:, par, 0:width], None).then_inc(sem[f"{done}{par}"], 16)

            def send(i, par):
                pool.wait_ge(sem["slot_ready0"], i + 1)
                pool.wait_ge(sem[f"stg_in{par}"], own(i, par, 16))
                scatter(t_xn, slots_x, D, s_idx, par, "sent")

            tiles_of(pool, send)

            def fetch(r, src, width):
                def body(i, par):
                    pool.wait_ge(sem[f"back_ready{r}"], i + 1)
                    nc.gpsimd.sem_inc(sem["pool_steps"], 1)
                    for k in range(K4):
                        nc.gpsimd.indirect_dma_start(g_in[:, par, k, 0:width], None, src,
                                                     bass.IndirectOffsetOnAxis(g_idx[:, par, k:k + 1], 0)).then_inc(sem[f"got{par}_{r}"], 16)
                return body

            def resend(i, par):
                pool.wait_ge(sem["slot_ready1"], i + 1)
                pool.wait_ge(sem["summed1"], i + 1)
                scatter(g_sum, slots_g, R, s_idx, par, "resent")

            for d in range(DEPTH):
                pool.wait_ge(sem[f"m_out0{d}"], 16 * (TILES // DEPTH))
            tiles_ahead(pool, fetch(1, slots_h, R), resend)
            for d in range(DEPTH):
                pool.wait_ge(sem[f"m_out1{d}"], 16 * (TILES // DEPTH))
            tiles_of(pool, fetch(2, slots_y, D))

        @block.scalar
        def _(act):
            def copy_xt(b):
                act.wait_ge(sem["xt_mm"], b + 1)
                if runs(b, 1, BATCH):
                    act.wait_ge(sem["v_mm"], b)
                nc.scalar.activation(xnT[:], ps_front[0:HALF, 0:2 * S].rearrange("p (c s) -> p c s", c=2),
                                     ACT.Copy).then_inc(sem["xt_copied"], 1)

            def embed_bias(p):
                act.wait_ge(sem["emb_mm"], p + 1)
                if runs(p, 1, PAIRS):
                    act.wait_ge(sem["emb_turned"], p)
                for e in range(2):
                    last = nc.scalar.activation(tokT[:, e, :], ps_eo[0:HALF, e * 2 * NPATCH:(e + 1) * 2 * NPATCH],
                                                ACT.Identity, bias=tok_b[:, e:e + 1])
                last.then_inc(sem["emb_bias"], 1)

            def embed_copy(p):
                act.wait_ge(sem["emb_turned"], p + 1)
                act.wait_ge(sem["emb_done"], p)
                nc.scalar.activation(tok[:], ps_pt[0:2 * NPATCH, 0:D], ACT.Copy).then_inc(sem["emb_copied"], 1)

            def copy_qk(b, par):
                act.wait_ge(sem["qk_mm"], b + 1)
                for o in range(4):
                    last = nc.scalar.activation(qk[:, par, o, :], ps_front[0:HALF, (2 + o) * S:(3 + o) * S],
                                                ACT.Identity, bias=qk_b[:, o:o + 1])
                last.then_inc(sem["qk_copied"], 1)

            def copy_scores(b, par):
                if runs(b, 2, BATCH):
                    act.wait_ge(sem["masked"], b - 1)
                act.wait_ge(sem["score_mm"], b + 1)
                for g in range(2):
                    nc.scalar.activation(work[:, par, 4 * g:4 * g + 4, :],
                                         ps_pred[g][0:ROWS, 0:4 * S].rearrange("p (c s) -> p c s", c=4), ACT.Copy)
                for g in range(2):
                    last = nc.scalar.activation(tru[:, par, 4 * g:4 * g + 4, :],
                                                ps_true[g][0:ROWS, 0:4 * S].rearrange("p (c s) -> p c s", c=4), ACT.Copy)
                last.then_inc(sem["score_copied"], 1)

            act.wait_ge(sem["biases_in"], 16 * 9)
            embed_bias(0)
            embed_copy(0)
            copy_xt(0)
            copy_qk(0, 0)
            copy_scores(0, 0)

            def slot(b, par):
                if runs(b, 0, BATCH - 2):
                    copy_xt(b + 1)
                    copy_qk(b + 1, 1 - par)
                if par == 0 and runs(b, 0, BATCH - 3):
                    embed_bias(b // 2 + 1)
                if runs(b, 1, BATCH):
                    act.wait_ge(sem["shifted"], b)
                    nc.scalar.activation(sc2[:], sc2[:], ACT.Exp, scale=SCALE).then_inc(sem["exp_done"], 1)
                if runs(b, 0, BATCH - 2):
                    copy_scores(b + 1, 1 - par)
                if par == 0 and runs(b, 0, BATCH - 3):
                    embed_copy(b // 2 + 1)
                if runs(b, 1, BATCH):
                    for g in range(2):
                        act.wait_ge(sem["pt_mm"], (b - 1) * 2 + g + 1)
                        if g == 0 and runs(b, 2, BATCH):
                            act.wait_ge(sem["ot_mm"], b - 1)
                        nc.scalar.activation(pT[:, g, :], ps_pt[0:S, 0:HH * S], ACT.Copy).then_inc(sem["pt_copied"], 1)
                    act.wait_ge(sem["ot_mm"], b)
                    if runs(b, 2, BATCH):
                        act.wait_ge(sem["proj_mm"], b - 1)
                    nc.scalar.activation(oT[:], ps_eo[0:HALF, D:D + 2 * S].rearrange("p (c s) -> p c s", c=2),
                                         ACT.Copy).then_inc(sem["ot_copied"], 1)

            slots_of(act, slot)

            act.wait_ge(sem["emb_ss"], 1)
            nc.scalar.activation(emb_m[:, 2:4], emb_m[:, 0:2], ACT.Sqrt).then_inc(sem["emb_root"], 1)

            def t_turned(i, par):
                act.wait_ge(sem["t_turn"], i + 1)
                nc.scalar.activation(t_xT[:], bank[0][0:HALF, 0:2 * P].rearrange("p (c s) -> p c s", c=2), ACT.Copy).then_inc(sem["t_xt"], 1)
                act.wait_ge(sem["t_qmm"], i + 1)
                nc.scalar.activation(t_q[:], bank[1][:, 0:P], ACT.Identity, bias=rt_b[:, 0:1]).then_inc(sem["t_qd"], 1)

            def t_exped(i, par):
                act.wait_ge(sem["t_shift"], i + 1)
                nc.scalar.activation(t_e[:], t_e[:], ACT.Exp).then_inc(sem["t_exp"], 1)

            tiles_ahead(act, t_turned, t_exped)

            def keep_tiles(r, arrays, width):
                def body(j, d):
                    act.wait_ge(sem[f"m_mm{r}"], j + 1)
                    if not is_static(j) or j >= DEPTH:
                        act.wait_ge(sem[f"m_out{r}{d}"], own_m(j - DEPTH, d, 16))
                    nc.scalar.activation(m_y[:, d, 0:width], bank[2 + d % 2][:, 0:width], ACT.Copy).then_inc(sem[f"m_done{r}"], 1)
                    act.wait_ge(sem[f"m_done{r}"], j + 1)
                    act.dma_start(arrays[bass.ds(j * P, P), :], m_y[:, d, 0:width]).then_inc(sem[f"m_out{r}{d}"], 16)
                matmuls_of(act, body)

            keep_tiles(0, slots_h, R)
            for d in range(DEPTH):
                act.wait_ge(sem[f"m_out0{d}"], 16 * (TILES // DEPTH))
            keep_tiles(1, slots_y, D)

        @block.tensor
        def _(pe):
            def embed(p):
                pe.wait_ge(sem["x_in"], (p + 1) * 32)
                pe.wait_ge(sem["emb_bias"], p)
                for e in range(2):
                    half = ps_eo[0:HALF, e * 2 * NPATCH:(e + 1) * 2 * NPATCH]
                    for a in range(4):
                        for c in range(4):
                            nc.tensor.matmul(half, wa[:, 4 * a + c, e * HALF:(e + 1) * HALF],
                                             xa[:, :, a:a + 2 * GRID - 1:2, c:c + 2 * GRID - 1:2],
                                             start=(a == 0 and c == 0), stop=False)
                        for c in range(2):
                            last = nc.tensor.matmul(half, wl[:, 2 * a + c, e * HALF:(e + 1) * HALF],
                                                    xl[:, :, a:a + 2 * GRID - 1:2, c:c + GRID],
                                                    start=False, stop=(a == 3 and c == 1))
                last.then_inc(sem["emb_mm"], 1)

            def embed_turn(p, b):
                pe.wait_ge(sem["emb_bias"], p + 1)
                if runs(b, 2, BATCH):
                    pe.wait_ge(sem["pt_copied"], 2 * b - 2)
                for e in range(2):
                    last = nc.tensor.transpose(ps_pt[0:2 * NPATCH, e * HALF:(e + 1) * HALF],
                                               tokT[:, e, :], ident[0:HALF, 0:HALF])
                last.then_inc(sem["emb_turned"], 1)

            def project_in(b):
                pe.wait_ge(sem["ln_done"], b + 1)
                if runs(b, 1, BATCH):
                    pe.wait_ge(sem["qk_copied"], b)
                for c in range(2):
                    last = nc.tensor.transpose(ps_front[0:HALF, c * S:(c + 1) * S], xn[:, c * HALF:(c + 1) * HALF],
                                               ident[0:S, 0:S])
                last.then_inc(sem["xt_mm"], 1)
                pe.wait_ge(sem["xt_copied"], b + 1)
                for o in range(4):
                    for c in range(2):
                        last = nc.tensor.matmul(ps_front[0:HALF, (2 + o) * S:(3 + o) * S],
                                                qkv[:, c, o * HALF:(o + 1) * HALF], xnT[:, c, :],
                                                start=(c == 0), stop=(c == 1))
                last.then_inc(sem["qk_mm"], 1)

            def values(b):
                if runs(b, 1, BATCH):
                    pe.wait_ge(sem["v_done"], b)
                if runs(b, 3, BATCH):
                    pe.wait_ge(sem["h1_done"], b - 2)
                for c in range(2):
                    last = nc.tensor.matmul(ps_vp[0:S, 0:D], xnT[:, c, :], qkv[:, c, 2 * D:3 * D],
                                            start=(c == 0), stop=(c == 1))
                last.then_inc(sem["v_mm"], 1)

            def scores(b, par):
                pe.wait_ge(sem["eqbd_done"], b + 1)
                if runs(b, 1, BATCH):
                    pe.wait_ge(sem["score_copied"], b)
                for bank2, lhs in ((ps_pred, eqbd), (ps_true, qbd)):
                    for g in range(2):
                        flat = lhs[:, g].rearrange("p h s -> p (h s)")
                        rhs = ek[:, g, :] if lhs is eqbd else qk[:, par, 2 + g, :]
                        for c in range(4):
                            last = nc.tensor.matmul(bank2[g][0:ROWS, c * S:(c + 1) * S], flat[:, c * ROWS:(c + 1) * ROWS],
                                                    rhs, start=True, stop=True)
                last.then_inc(sem["score_mm"], 1)

            def attend(b, par, embedded):
                pe.wait_ge(sem["prob_done"], b + 1)
                for g in range(2):
                    if g == 1:
                        pe.wait_ge(sem["pt_copied"], 2 * b + 1)
                    if g == 0 and embedded:
                        pe.wait_ge(sem["emb_copied"], (b + 1) // 2 + 2)
                    if g == 0 and runs(b, 1, BATCH):
                        pe.wait_ge(sem["pt_copied"], 2 * b)
                    for c in range(4):
                        last = nc.tensor.transpose(ps_pt[0:S, c * ROWS:(c + 1) * ROWS], sc1[:, 4 * g + c, :],
                                                   ident[0:ROWS, 0:ROWS])
                    last.then_inc(sem["pt_mm"], 1)
                pe.wait_ge(sem["pt_copied"], 2 * b + 2)
                if runs(b, 1, BATCH):
                    pe.wait_ge(sem["ot_copied"], b)
                for g in range(2):
                    for h in range(HH):
                        last = nc.tensor.matmul(ps_eo[0:HALF, D + g * S:D + (g + 1) * S], vm[:, par, HH * g + h, :],
                                                pT[:, g, h * S:(h + 1) * S], start=(h == 0), stop=(h == HH - 1))
                last.then_inc(sem["ot_mm"], 1)
                pe.wait_ge(sem["ot_copied"], b + 1)
                if runs(b, 1, BATCH):
                    pe.wait_ge(sem["h1_done"], b)
                pe.wait_ge(sem["v_done"], b + 3 if runs(b, 0, BATCH - 3) else BATCH)
                for g in range(2):
                    last = nc.tensor.matmul(ps_vp[0:S, D:2 * D], oT[:, g, :], wp[:, g, :], start=(g == 0), stop=(g == 1))
                last.then_inc(sem["proj_mm"], 1)

            pe.wait_ge(sem["consts"], 1)
            pe.wait_ge(sem["biases_in"], 16 * 9)
            pe.wait_ge(sem["w_sum"], 1)
            pe.wait_ge(sem["zeroed"], 2)
            embed(0)
            embed_turn(0, 0)
            project_in(0)
            scores(0, 0)
            values(0)

            def slot(b, par):
                if runs(b, 0, BATCH - 2):
                    project_in(b + 1)
                if par == 0 and runs(b, 0, BATCH - 3):
                    embed(b // 2 + 1)
                if runs(b, 0, BATCH - 2):
                    scores(b + 1, 1 - par)
                    values(b + 1)
                if par == 0 and runs(b, 0, BATCH - 3):
                    embed_turn(b // 2 + 1, b)
                if runs(b, 1, BATCH):
                    attend(b - 1, 1 - par, par == 0 and runs(b, 0, BATCH - 3))

            slots_of(pe, slot)

            pe.wait_ge(sem["emb_scaled"], 1)
            nc.tensor.transpose(bank[5][:, 0:P], emb_s[:].rearrange("p r d -> p (r d)"), ident[:]).then_inc(sem["emb_flip"], 1)
            pe.wait_ge(sem["emb_ready"], 1)

            def t_logits(i, par):
                pe.wait_ge(sem["t_norm"], i + 1)
                if not is_static(i) or i >= 1:
                    pe.wait_ge(sem["t_xt"], i)
                for c in range(2):
                    last = nc.tensor.transpose(bank[0][0:HALF, c * P:(c + 1) * P], t_xn[:, par, c * HALF:(c + 1) * HALF], ident[:])
                last.then_inc(sem["t_turn"], 1)
                pe.wait_ge(sem["t_xt"], i + 1)
                if not is_static(i) or i >= 1:
                    pe.wait_ge(sem["t_qd"], i)
                for c in range(2):
                    last = nc.tensor.matmul(bank[1][:, 0:P], w_rt[:, c, :], t_xT[:, c, :], start=(c == 0), stop=(c == 1))
                last.then_inc(sem["t_qmm"], 1)
                pe.wait_ge(sem["t_qd"], i + 1)
                if not is_static(i) or i >= 1:
                    pe.wait_ge(sem["t_shift"], i)
                nc.tensor.matmul(bank[2][:, 0:2 * NE], t_q[:], emb_t[:], start=True, stop=True).then_inc(sem["t_logit"], 1)

            def t_position(i, par):
                pe.wait_ge(sem["t_pick"], i + 1)
                if not is_static(i) or i >= 1:
                    pe.wait_ge(sem["t_placed"], i)
                for b2, m in ((3, upper_b), (4, ones_b)):
                    for k in range(K4):
                        last = nc.tensor.matmul(bank[b2][:, 0:2 * NE].rearrange("p (r n) -> p r n", r=2), m[:],
                                                pick[:, bass.ds(i, 1), :, k, :].rearrange("p i r n -> p (i r) n"),
                                                start=(k == 0), stop=(k == K4 - 1))
                last.then_inc(sem["t_pos"], 1)

            tiles_ahead(pe, t_logits, t_position)

            pe.wait_ge(sem["t_placed"], NT)
            for r in range(2):
                last = nc.tensor.transpose(bank[0][:, r * P:(r + 1) * P], count[:, r, :], ident[:])
            last.then_inc(sem["count_turn"], 1)
            pe.wait_ge(sem["base_steps"], 4)
            for r in range(2):
                last = nc.tensor.matmul(bank[1][:, r * NE:(r + 1) * NE], ntile_b[:, r, :], upper_f[:], start=True, stop=True)
            last.then_inc(sem["base_mm"], 1)
            nc.tensor.matmul(bank[2][:, 0:2], upper_in[:], ntile[:], start=True, stop=True).then_inc(sem["ends_mm"], 1)
            pe.wait_ge(sem["base_steps"], 8)
            nc.tensor.matmul(bank[3][:, 0:2 * TILES], ones_f[:], ended[:].rearrange("p r t -> p (r t)"), start=True, stop=True).then_inc(sem["ended_mm"], 1)

            def multiply_tiles(r, rows, halves, width):
                def turn(j, d):
                    pe.wait_ge(sem[f"m_in{r}{d}"], own_m(j, d, 32))
                    if not is_static(j) or j >= 2:
                        pe.wait_ge(sem[f"m_xt{r}"], j - 1)
                    for c in range(halves):
                        last = nc.tensor.transpose(bank[d % 2][0:rows, c * P:(c + 1) * P], m_x[:, d, c:halves * rows:halves], ident[:])
                    last.then_inc(sem[f"m_turn{r}"], 1)

                def multiply(j, d):
                    pe.wait_ge(sem[f"m_xt{r}"], j + 1)
                    if not is_static(j) or j >= 2:
                        pe.wait_ge(sem[f"m_done{r}"], j - 1)
                    for c in range(halves):
                        last = nc.tensor.matmul(bank[2 + d % 2][:, 0:width], m_xT[0:rows, d % 2, c * P:(c + 1) * P],
                                                m_w[0:rows, d, c * width:(c + 1) * width], start=(c == 0), stop=(c == halves - 1))
                    last.then_inc(sem[f"m_mm{r}"], 1)

                turn(0, 0)
                for d in range(DEPTH):
                    turn(d + 1, (d + 1) % DEPTH)
                    multiply(d, d)
                with pe.Fori(DEPTH, TILES - DEPTH, DEPTH) as j:
                    for d in range(DEPTH):
                        turn(j + d + 1, (d + 1) % DEPTH)
                        multiply(j + d, d)
                for d in range(DEPTH):
                    j = TILES - DEPTH + d
                    if d < DEPTH - 1:
                        turn(j + 1, d + 1)
                    multiply(j, d)

            pe.wait_ge(sem["tiles_known"], 1)
            multiply_tiles(0, HALF, 2, R)
            multiply_tiles(1, P, 1, D)

        @block.vector
        def _(dve):
            def plain():
                dve.sem_inc(sem["dve_steps"], 1)

            def embed_norm(p):
                n = 2 * NPATCH
                dve.wait_ge(sem["emb_copied"], p + 1)
                nc.vector.bn_stats(tstat[:, 0:6], tok[:]).then_inc(sem["emb_stat"], 1)
                dve.wait_ge(sem["emb_stat"], p + 1)
                plain()
                nc.vector.bn_aggr(tmv[:, 0:2], tstat[:, 0:6]).then_inc(sem["emb_aggr"], 1)

            def embed_scale(p):
                n = 2 * NPATCH
                dve.wait_ge(sem["emb_rstd"], p + 1)
                nc.vector.tensor_scalar(tok[:], tok[:], tmv[:, 0:1], tmv[:, 3:4], ALU.subtract, ALU.mult).then_inc(sem["emb_norm"], 1)
                dve.wait_ge(sem["emb_norm"], p + 1)
                nc.vector.tensor_tensor(tok[:], tok[:], tok_row[0:n, 0, :], ALU.mult).then_inc(sem["emb_gamma"], 1)
                dve.wait_ge(sem["emb_gamma"], p + 1)
                if runs(p, 1, PAIRS):
                    dve.wait_ge(sem["emb_out"], p * 32)
                nc.vector.tensor_tensor(tok2[:], tok[:], tok_row[0:n, 1, :], ALU.add).then_inc(sem["emb_done"], 1)

            def norm(b, par):
                dve.wait_ge(sem[f"hb_in{par}"], own16(b, par))
                nc.vector.bn_stats(stat[:, 0:6], hb[:, par, :]).then_inc(sem["ln_stat"], 1)
                dve.wait_ge(sem["ln_stat"], b + 1)
                plain()
                nc.vector.bn_aggr(mv[:, 0:2], stat[:, 0:6]).then_inc(sem["ln_aggr"], 1)

            def scale(b, par):
                dve.wait_ge(sem["ln_rstd"], b + 1)
                if runs(b, 1, BATCH):
                    dve.wait_ge(sem["xt_mm"], b)
                nc.vector.tensor_scalar(xn[:], hb[:, par, :], mv[:, 0:1], mv[:, 3:4], ALU.subtract, ALU.mult).then_inc(sem["ln_done"], 1)

            def quantise(b, par):
                dve.wait_ge(sem["qk_copied"], b + 1)
                if runs(b, 1, BATCH):
                    dve.wait_ge(sem["score_mm"], b)
                nc.vector.tensor_scalar(ek[:].bitcast(U16), qk[:, par, 2:4, :].bitcast(U16)[:, :, 1::2], 0xFF80, None,
                                        ALU.bitwise_and).then_inc(sem["ek_done"], 1)
                dve.wait_ge(sem["qbd_done"], b + 1)
                nc.vector.tensor_scalar(eqbd[:].rearrange("p g h s -> p (g h s)").bitcast(U16),
                                        qbd[:].rearrange("p g h s -> p (g h s)").bitcast(U16)[:, 1::2], 0xFF80, None,
                                        ALU.bitwise_and).then_inc(sem["eqbd_done"], 1)

            def spread_v(b, par):
                dve.wait_ge(sem["v_mm"], b + 1)
                if runs(b, 2, BATCH):
                    dve.wait_ge(sem["ot_mm"], b - 1)
                for g in range(2):
                    dst = vm[:, par, HH * g:HH * g + HH, :].rearrange("p h c -> p (h c)")
                    dst = dst[:, 0:HH * HALF]
                    dst = strided(dst, HH, HALF + HD, HD)
                    last = nc.vector.tensor_tensor(dst, ps_vp[0:S, g * HALF:(g + 1) * HALF].rearrange("p (h c) -> p h c", h=HH),
                                                   row_b[0:S, 0, g * HALF:(g + 1) * HALF].rearrange("p (h c) -> p h c", h=HH), ALU.add)
                last.then_inc(sem["v_done"], 1)

            def strided(ap, n, step, width):
                pitch = [list(x) for x in ap.ap]
                return bass.AP(ap.tensor, ap.offset, [pitch[0], [step, n], [1, width]])

            def take8(b, par, r):
                base = 8 * b + 2 * r
                if r > 0:
                    dve.wait_ge(sem["topk"], base)
                    plain()
                for c in range(8):
                    last = nc.vector.max(top8[:, c, :], work[:, par, c, :])
                last.then_inc(sem["topk"], 1)
                dve.wait_ge(sem["topk"], base + 1)
                plain()
                for c in range(8):
                    last = nc.vector.match_replace(work[:, par, c, :], top8[:, c, :], work[:, par, c, :], TAKEN)
                last.then_inc(sem["topk"], 1)

            def finish(b, par):
                dve.wait_ge(sem["proj_mm"], b + 1)
                if runs(b, 2, BATCH):
                    dve.wait_ge(sem[f"h1_out{par}"], own16(b - 2, par))
                nc.vector.tensor_tensor(h1b[:, par, :], ps_vp[0:S, D:2 * D], hbp[:, par, :], ALU.add).then_inc(sem["h1_done"], 1)

            nc.vector.memset(zero[:], 0.0).then_inc(sem["zeroed"], 1)
            nc.vector.memset(vm[:], 0.0).then_inc(sem["zeroed"], 1)
            dve.wait_ge(sem["weights_in"], 32)
            dve.wait_ge(sem["mid_in"], 32)
            for a in range(2):
                nc.vector.tensor_tensor(wa[:, 5 + 4 * a:7 + 4 * a, :], wa[:, 5 + 4 * a:7 + 4 * a, :], wma[:, 2 * a:2 * a + 2, :], ALU.add)
                nc.vector.tensor_tensor(wl[64:P, 2 + 2 * a, :], wl[64:P, 2 + 2 * a, :], wml[64:P, a, :], ALU.add)
                last = nc.vector.tensor_tensor(wl[0:64, 3 + 2 * a, :], wl[0:64, 3 + 2 * a, :], wml[0:64, a, :], ALU.add)
            last.then_inc(sem["w_sum"], 1)
            dve.wait_ge(sem["biases_in"], 16 * 9)
            dve.wait_ge(sem["zeroed"], 2)
            embed_norm(0)
            embed_scale(0)
            norm(0, 0)
            scale(0, 0)
            quantise(0, 0)
            spread_v(0, 0)

            def slot(b, par):
                take = runs(b, 0, BATCH - 1)
                front = runs(b, 0, BATCH - 2)
                back = runs(b, 1, BATCH)
                if front:
                    norm(b + 1, 1 - par)
                if back:
                    dve.wait_ge(sem["topk"], b * 8)
                    nc.vector.tensor_scalar(work[:, 1 - par], work[:, 1 - par], TAKEN / 2, -BIG, ALU.is_gt, ALU.mult).then_inc(sem["gap_done"], 1)
                if front:
                    scale(b + 1, 1 - par)
                if take:
                    dve.wait_ge(sem["score_copied"], b + 1)
                    plain()
                    take8(b, par, 0)
                if back:
                    dve.wait_ge(sem["masked"], b)
                    nc.vector.tensor_reduce(smax[:], sc1[:], AX.X, ALU.max).then_inc(sem["smax_done"], 1)
                if runs(b, 2, BATCH + 1):
                    finish(b - 2, par)
                if take:
                    take8(b, par, 1)
                if front:
                    quantise(b + 1, 1 - par)
                if back:
                    dve.wait_ge(sem["exp_done"], b)
                    nc.vector.tensor_reduce(ssum[:], sc2[:], AX.X, ALU.add).then_inc(sem["ssum_done"], 1)
                    dve.wait_ge(sem["ssum_done"], b)
                    nc.vector.reciprocal(srec[:], ssum[:]).then_inc(sem["srec_done"], 1)
                if par == 0 and runs(b, 0, BATCH - 3):
                    embed_norm(b // 2 + 1)
                if take:
                    take8(b, par, 2)
                if par == 0 and runs(b, 0, BATCH - 3):
                    embed_scale(b // 2 + 1)
                if front:
                    spread_v(b + 1, 1 - par)
                if take:
                    take8(b, par, 3)

            slots_of(dve, slot)

            nc.vector.memset(emb_t[:], 0.0).then_inc(sem["fresh"], 1)
            nc.vector.memset(count[:], 0.0).then_inc(sem["fresh"], 1)
            nc.vector.tensor_tensor(emb_s[:], emb_n[:], emb_n[:], ALU.mult).then_inc(sem["emb_sq"], 1)
            dve.wait_ge(sem["emb_sq"], 1)
            nc.vector.tensor_reduce(emb_m[:, 0:2], emb_s[:], AX.X, ALU.add).then_inc(sem["emb_ss"], 1)
            dve.wait_ge(sem["emb_root"], 1)
            nc.vector.tensor_scalar(emb_m[:, 4:6], emb_m[:, 2:4], 1e-8, None, ALU.add).then_inc(sem["emb_eps2"], 1)
            dve.wait_ge(sem["emb_eps2"], 1)
            nc.vector.reciprocal(emb_m[:, 6:8], emb_m[:, 4:6]).then_inc(sem["emb_rec"], 1)
            dve.wait_ge(sem["emb_rec"], 1)
            for r in range(2):
                last = nc.vector.tensor_scalar(emb_s[:, r, :], emb_n[:, r, :], emb_m[:, 6 + r:7 + r], None, ALU.mult)
            last.then_inc(sem["emb_scaled"], 1)
            dve.wait_ge(sem["emb_flip"], 1)
            dve.wait_ge(sem["fresh"], 2)
            nc.vector.tensor_copy(emb_t[0:DS, 0:NE], bank[5][0:DS, 0:P])
            nc.vector.tensor_copy(emb_t[DS:P, NE:2 * NE], bank[5][DS:P, 0:P]).then_inc(sem["emb_ready"], 1)

            def t_norm(i, par):
                dve.wait_ge(sem[f"t_in{par}"], own(i, par, 16))
                nc.vector.bn_stats(t_stat[:, 0:6], t_h[:, par, :]).then_inc(sem["t_stat"], 1)
                dve.wait_ge(sem["t_stat"], i + 1)
                plain()
                nc.vector.bn_aggr(t_mv[:, 0:2], t_stat[:, 0:6]).then_inc(sem["t_aggr"], 1)
                dve.wait_ge(sem["t_rstd"], i + 1)
                if not is_static(i) or i >= 2:
                    dve.wait_ge(sem["t_turn"], i - 1)
                    dve.wait_ge(sem[f"xn_out{par}"], own(i - 2, par, 16))
                nc.vector.tensor_scalar(t_xn[:, par, :], t_h[:, par, :], t_mv[:, 0:1], t_mv[:, 3:4], ALU.subtract, ALU.mult).then_inc(sem["t_norm"], 1)

            route = Steps(dve, "route", 9)

            def t_route(i, par):
                route.start(i)
                logits = bank[2][:, 0:2 * NE].rearrange("p (r n) -> p r n", r=2)
                dve.wait_ge(sem["t_logit"], i + 1)
                nc.vector.tensor_reduce(t_m[:, 0:2], logits, AX.X, ALU.max).then_inc(sem["t_max"], 1)
                dve.wait_ge(sem["t_max"], i + 1)
                nc.vector.tensor_tensor(t_e[:], logits, t_m[:, 0:2].unsqueeze(2).to_broadcast([P, 2, NE]), ALU.subtract).then_inc(sem["t_shift"], 1)
                dve.wait_ge(sem["t_exp"], i + 1)
                route.done(nc.vector.tensor_reduce(t_m[:, 2:4], t_e[:], AX.X, ALU.add))
                route.wait()
                route.done(nc.vector.reciprocal(t_m[:, 4:6], t_m[:, 2:4]))
                route.wait()
                route.done(nc.vector.tensor_tensor(t_p[:], t_e[:], t_m[:, 4:6].unsqueeze(2).to_broadcast([P, 2, NE]), ALU.mult))
                route.wait()
                plain()
                nc.vector.max(t_top[:, 0, :], t_p[:, 0, :])
                route.done(nc.vector.max(t_top[:, 1, :], t_p[:, 1, :]))
                route.wait()
                plain()
                nc.vector.max_index(t_idx[:, 0, :], t_top[:, 0, :], t_p[:, 0, :])
                nc.vector.max_index(t_idx[:, 1, :], t_top[:, 1, :], t_p[:, 1, :])
                route.done(nc.vector.tensor_reduce(t_m[:, 6:8], t_top[:, :, 0:K4], AX.X, ALU.add))
                route.wait()
                route.done(nc.vector.tensor_scalar(t_m[:, 2:4], t_m[:, 6:8], 1e-8, None, ALU.add))
                nc.vector.tensor_copy(t_idf[:], t_idx[:])
                route.wait()
                route.done(nc.vector.reciprocal(t_m[:, 4:6], t_m[:, 2:4]))
                route.wait()
                route.done(nc.vector.tensor_tensor(weights[:, bass.ds(i, 1), :, :].rearrange("p i r k -> p (i r) k"), t_top[:, :, 0:K4],
                                                   t_m[:, 4:6].unsqueeze(2).to_broadcast([P, 2, K4]), ALU.mult))
                for r in range(2):
                    last = nc.vector.tensor_tensor(pick[:, bass.ds(i, 1), r, :, :].rearrange("p i k n -> p (i k) n"),
                                                   iota_e[:].unsqueeze(1).to_broadcast([P, K4, NE]),
                                                   t_idf[:, r, 0:K4].unsqueeze(2).to_broadcast([P, K4, NE]), ALU.is_equal)
                last.then_inc(sem["t_pick"], 1)
                dve.wait_ge(sem["t_pos"], i + 1)
                route.wait()
                nc.vector.tensor_tensor(place[:, bass.ds(i, 1), :, :].rearrange("p i r n -> p (i r) n"),
                                        bank[3][:, 0:2 * NE].rearrange("p (r n) -> p r n", r=2), count[:], ALU.add)
                route.done(nc.vector.tensor_tensor(count[:], bank[4][:, 0:2 * NE].rearrange("p (r n) -> p r n", r=2), count[:], ALU.add))
                route.wait()
                nc.vector.sem_inc(sem["t_placed"], 1)

            tiles_ahead(dve, t_norm, t_route)

            steps = Steps(dve, "base_steps", 9)
            steps.start(0)
            dve.wait_ge(sem["count_turn"], 1)
            steps.done(nc.vector.tensor_scalar(ntile_i[:, 0:2], bank[0][:, 0:2 * P:P], float(P - 1), None, ALU.add))
            steps.wait()
            steps.done(nc.vector.tensor_scalar(ntile_i[:, 2:4], ntile_i[:, 0:2], 7, None, ALU.logical_shift_right))
            steps.wait()
            steps.done(nc.vector.tensor_copy(ntile[:], ntile_i[:, 2:4]))
            steps.wait()
            steps.done(nc.vector.tensor_copy(ntile_b[:], ntile[:].unsqueeze(2).to_broadcast([P, 2, NE])))
            dve.wait_ge(sem["base_mm"], 1)
            steps.done(nc.vector.tensor_scalar(base[:].rearrange("p r n -> p (r n)"), bank[1][:, 0:2 * NE], float(P), None, ALU.mult))
            dve.wait_ge(sem["ends_mm"], 1)
            steps.done(nc.vector.tensor_copy(ends[:], bank[2][:, 0:2]))
            steps.wait()
            for r in range(2):
                steps.done(nc.vector.tensor_scalar(ended[:, r, :], iota_t[:], ends[:, r:r + 1], None, ALU.is_ge))
            dve.wait_ge(sem["ended_mm"], 1)
            steps.done(nc.vector.tensor_scalar(tile_e[:], bank[3][:, 0:2 * TILES], float(NE - 1), None, ALU.min))
            steps.wait()
            nc.vector.sem_inc(sem["tiles_known"], 1)

            slot_steps = [Steps(dve, "slot_steps0", 4), Steps(dve, "slot_steps1", 4)]

            def find_slots(r, i, par, sent):
                st = slot_steps[r]
                st.start(i)
                st.done(nc.vector.tensor_tensor(s_at[:], place[:, bass.ds(i, 1), r, :].rearrange("p i n -> p (i n)"), base[:, r, :], ALU.add))
                st.wait()
                st.done(nc.vector.tensor_tensor(s_prod[:], pick[:, bass.ds(i, 1), r, :, :].rearrange("p i k n -> p (i k) n"),
                                                s_at[:].unsqueeze(1).to_broadcast([P, K4, NE]), ALU.mult))
                st.wait()
                st.done(nc.vector.tensor_reduce(s_f[:], s_prod[:], AX.X, ALU.add))
                st.wait()
                if not is_static(i) or i >= 2:
                    dve.wait_ge(sem[f"{sent}{par}"], own(i - 2, par, 16 * K4))
                nc.vector.tensor_copy(s_idx[:, par, :], s_f[:]).then_inc(sem[f"slot_ready{r}"], 1)
                st.done(nc.vector.tensor_copy(s_all[:, r, bass.ds(i, 1), :].rearrange("p i k -> p (i k)"), s_f[:]))
                st.wait()

            tiles_of(dve, lambda i, par: find_slots(0, i, par, "sent"))

            def turned_tiles(r, rows, halves):
                def body(j, d):
                    dve.wait_ge(sem[f"m_turn{r}"], j + 1)
                    if not is_static(j) or j >= 2:
                        dve.wait_ge(sem[f"m_mm{r}"], j - 1)
                    nc.vector.tensor_copy(m_xT[0:rows, d % 2, 0:halves * P], bank[d % 2][0:rows, 0:halves * P]).then_inc(sem[f"m_xt{r}"], 1)
                matmuls_of(dve, body)

            def index_back(r, i, par):
                if not is_static(i) or i >= 2:
                    dve.wait_ge(sem[f"got{par}_{r}"], own(i - 2, par, 16 * K4))
                nc.vector.tensor_copy(g_idx[:, par, :], s_all[:, r - 1, bass.ds(i, 1), :].rearrange("p i k -> p (i k)")).then_inc(sem[f"back_ready{r}"], 1)

            sums = [None, Steps(dve, "sum_steps1", K4), Steps(dve, "sum_steps2", K4 + 1)]

            def sum_back(r, i, par, width, free):
                st = sums[r]
                st.start(i)
                dve.wait_ge(sem[f"got{par}_{r}"], own(i, par, 16 * K4))
                if not is_static(i) or i >= 2:
                    dve.wait_ge(sem[f"{free}{par}"], own(i - 2, par, 16 * (K4 if r == 1 else 1)))
                for k in range(K4):
                    w = weights[:, bass.ds(i, 1), r - 1, k:k + 1].rearrange("p i k -> p (i k)")
                    if k == 0:
                        ins = nc.vector.tensor_scalar(g_sum[:, par, 0:width], g_in[:, par, 0, 0:width], w, None, ALU.mult)
                    else:
                        st.wait()
                        ins = nc.vector.scalar_tensor_tensor(g_sum[:, par, 0:width], g_in[:, par, k, 0:width], w,
                                                             g_sum[:, par, 0:width], ALU.mult, ALU.add)
                    st.done(ins)
                if r == 2:
                    st.wait()
                    dve.wait_ge(sem[f"res_in{par}"], own(i, par, 16))
                    st.done(nc.vector.tensor_tensor(g_sum[:, par, :], g_sum[:, par, :], t_h[:, par, :], ALU.add))
                st.wait()
                nc.vector.sem_inc(sem[f"summed{r}"], 1)

            turned_tiles(0, HALF, 2)

            def middle(i, par):
                find_slots(1, i, par, "resent")
                sum_back(1, i, par, R, "resent")

            dve.wait_ge(sem["sent0"], 16 * K4 * 9)
            dve.wait_ge(sem["sent1"], 16 * K4 * 8)
            tiles_ahead(dve, lambda i, par: index_back(1, i, par), middle)
            turned_tiles(1, P, 1)
            tiles_ahead(dve, lambda i, par: index_back(2, i, par), lambda i, par: sum_back(2, i, par, D, "out_done"))


_INS = ["a_x", "l_x", "text_ids", "w_shift_a", "w_shift_l", "w_mid_a", "w_mid_l", "tok_vec", "tok_bias", "vocab",
        "w_qkv", "qk_bias", "row_vec", "w_proj", "f_know", "r_know", "w_route", "route_bias", "emb"]


def lay_out(x, x_txt, L0_tok_W, L0_tok_b, L0_tok_gamma, L0_tok_beta, L0_txt_weight, L0_attn_qkv_w,
            L0_attn_qkv_b, L0_attn_proj_w, L0_attn_proj_b, L0_ffn_f_know, L0_ffn_r_know, L0_ffn_W_fk,
            L0_ffn_b_fk, L0_ffn_W_rk, L0_ffn_b_rk, L0_ffn_emb_fk, L0_ffn_emb_rk):
    n8 = IMAGE // 8
    blocks = x.reshape(BATCH, CHANNELS, n8, 8, n8, 8).transpose(3, 5, 1, 0, 2, 4).reshape(BLOCK_F, BATCH, n8, n8)
    ring = [(i - 1) % n8 for i in range(HALO)]
    blocks = blocks[:, :, ring][:, :, :, ring]
    pairs = blocks.reshape(BLOCK_F, PAIRS, 2, HALO, HALO).transpose(1, 0, 2, 3, 4)
    a_x = pairs[:, :P]
    l_x = np.concatenate([pairs[:, P:, :, :, 0::2], pairs[:, P:, :, :, 1::2]], axis=1)
    w = L0_tok_W.reshape(D, 5, 2, 8, 2, 8, CHANNELS).transpose(1, 2, 4, 3, 5, 6, 0).reshape(5, 2, 2, BLOCK_F, D)
    shifted = np.zeros((4, 4, BLOCK_F, D), w.dtype)
    for s, (ra, ca) in enumerate([(2, 2), (2, 0), (0, 2), (0, 0)]):
        shifted[ra:ra + 2, ca:ca + 2] = w[s + 1]
    w_shift_a = shifted[:, :, :P].reshape(16, P, D).transpose(1, 0, 2)
    w_shift_l = shifted[:, :, P:].reshape(8, P, D).transpose(1, 0, 2)
    w_mid_a = w[0][:, :, :P].reshape(4, P, D).transpose(1, 0, 2)
    w_mid_l = np.concatenate([w[0][:, 1, P:], w[0][:, 0, P:]], axis=1).transpose(1, 0, 2)
    rows = lambda *v: np.broadcast_to(np.stack(v)[None], (P, len(v), D))
    split = lambda m: m.reshape(2, HALF, -1).transpose(1, 0, 2)
    return {
        "a_x": a_x, "l_x": l_x, "text_ids": x_txt.astype(np.int32).reshape(8, P).T,
        "w_shift_a": w_shift_a, "w_shift_l": w_shift_l, "w_mid_a": w_mid_a, "w_mid_l": w_mid_l,
        "tok_vec": rows(L0_tok_gamma, L0_tok_beta), "tok_bias": L0_tok_b.reshape(2, HALF).T, "vocab": L0_txt_weight,
        "w_qkv": split(L0_attn_qkv_w.T), "qk_bias": L0_attn_qkv_b[:2 * D].reshape(4, HALF).T,
        "row_vec": rows(L0_attn_qkv_b[2 * D:], L0_attn_proj_b), "w_proj": split(L0_attn_proj_w.T),
        "f_know": L0_ffn_f_know, "r_know": L0_ffn_r_know,
        "w_route": split(np.concatenate([L0_ffn_W_fk, L0_ffn_W_rk], axis=1)),
        "route_bias": np.concatenate([L0_ffn_b_fk, L0_ffn_b_rk])[:, None],
        "emb": np.stack([L0_ffn_emb_fk, L0_ffn_emb_rk], axis=1),
    }


def kernel(**inputs):
    import concourse.bacc as _bacc
    from concourse import mybir as _mybir
    from concourse.bass_utils import run_bass_kernel_spmd as _run

    laid = lay_out(**{k: np.asarray(v) for k, v in inputs.items()})
    nc = _bacc.Bacc("TRN2", target_bir_lowering=False, num_devices=1)
    arrays, args = {}, []
    for name in _INS:
        a = np.ascontiguousarray(laid[name])
        arrays[f"in_{name}"] = a
        args.append(nc.dram_tensor(f"in_{name}", a.shape, _mybir.dt.from_np(a.dtype), kind="ExternalInput").ap())
    args.append(nc.dram_tensor("out", (BATCH, S, D), F32, kind="ExternalOutput").ap())
    build(nc, *args)
    r = _run(nc, [arrays], core_ids=[0])
    return r.results[0]["out"]
```

```python
from contextlib import ExitStack

import numpy as np

import concourse.bass as bass
from concourse import mybir

F32 = mybir.dt.float32
BF16 = mybir.dt.bfloat16
I32 = mybir.dt.int32
U32 = mybir.dt.uint32
U16 = mybir.dt.uint16
ALU = mybir.AluOpType
ACT = mybir.ActivationFunctionType
AX = mybir.AxisListType

BATCH, CHANNELS, IMAGE, PATCH = 32, 3, 96, 16
D = 192
HALF = D // 2
HALO = 2 * (IMAGE // PATCH) + 2
GRID = IMAGE // PATCH
NPATCH = GRID * GRID
NTEXT = 32
S = NPATCH + NTEXT
T = BATCH * S
PAIRS = BATCH // 2
BLOCK_F = 8 * 8 * CHANNELS
HEADS, HD, TOPK = 12, 16, 32
HH = HEADS // 2
ROWS = HH * S // 4
EPS = 1e-5
SCALE = 0.25
TAKEN = -3.0e38
BIG = 1.0e30
NE, R, DS, K4 = 128, 128, 64, 4
P = 128
NT = T // P
TILES = T * K4 // P + NE
SLOTS = TILES * P
FIRST, LAST = 4, 26
N_ZERO = 28
ZERO_W = TILES * D // N_ZERO
DEPTH = 4


def build(nc, a_x, l_x, text_ids, w_shift_a, w_shift_l, w_mid_a, w_mid_l, tok_vec, tok_bias, vocab,
          w_qkv, qk_bias, row_vec, w_proj, f_know, r_know, w_route, route_bias, emb, out):
    ctx = ExitStack()
    with ctx:
        def sb(name, shape, dt=F32):
            return ctx.enter_context(nc.sbuf_tensor(name, shape, dt))

        sem = {}

        def S_(name):
            sem[name] = ctx.enter_context(nc.semaphore(name))

        def dram(name, shape, dt=F32):
            return nc.dram_tensor(name, shape, dt, kind="Internal").ap()

        h0 = dram("h0", [T, D])
        h1 = dram("h1", [T, D])
        xn2 = dram("xn2", [T, D])
        slots_x = dram("slots_x", [SLOTS, D])
        slots_h = dram("slots_h", [SLOTS, R])
        slots_g = slots_x.rearrange("s d -> (s d)")[0:SLOTS * R].rearrange("(s r) -> s r", r=R)
        slots_y = dram("slots_y", [SLOTS, D])

        ident = sb("ident", [P, P])
        ones_f = sb("ones_f", [P, P])
        ones_b = sb("ones_b", [P, P], BF16)
        upper_b = sb("upper_b", [P, P], BF16)
        upper_f = sb("upper_f", [P, P])
        upper_in = sb("upper_in", [P, P])
        eps_col = sb("eps_col", [P, 1])
        minus_half = sb("minus_half", [P, 1])
        iota_e = sb("iota_e", [P, NE])
        iota_t = sb("iota_t", [P, TILES])
        head_mask = sb("head_mask", [HALF, HH])
        wa = sb("wa", [P, 16, D])
        wl = sb("wl", [P, 8, D])
        wma = sb("wma", [P, 4, D])
        wml = sb("wml", [P, 2, D])
        tok_row = sb("tok_row", [P, 2, D])
        tok_b = sb("tok_b", [HALF, 2])
        qkv = sb("qkv", [HALF, 2, 3 * D])
        qk_b = sb("qk_b", [HALF, 4])
        row_b = sb("row_b", [P, 2, D])
        wp = sb("wp", [HALF, 2, D])
        w_rt = sb("w_rt", [HALF, 2, P])
        rt_b = sb("rt_b", [P, 1])
        emb_n = sb("emb_n", [P, 2, DS])
        emb_t = sb("emb_t", [P, 2 * NE])
        zero = sb("zero", [P, ZERO_W])

        ids = sb("ids", [P, 8], I32)
        text = sb("text", [P, 8, D])
        xa = sb("xa", [P, 2, HALO, HALO])
        xl = sb("xl", [P, 2, HALO, HALO // 2])
        tokT = sb("tokT", [HALF, 2, 2 * NPATCH])
        tok = sb("tok", [2 * NPATCH, D])
        tok2 = sb("tok2", [2 * NPATCH, D])
        tstat = sb("tstat", [2 * NPATCH, 8])
        tmv = sb("tmv", [2 * NPATCH, 4])

        hb = sb("hb", [S, 2, D])
        hbr = sb("hbr", [S, 2, D])
        hbp = sb("hbp", [S, 2, D])
        stat = sb("stat", [S, 8])
        mv = sb("mv", [S, 4])
        xn = sb("xn", [S, D])
        xnT = sb("xnT", [HALF, 2, 2, S])
        qk = sb("qk", [HALF, 2, 4, S])
        ek = sb("ek", [HALF, 2, S], BF16)
        qbd = sb("qbd", [HALF, 2, HH, S])
        eqbd = sb("eqbd", [HALF, 2, HH, S], BF16)
        v = sb("v", [S, 2, D])
        o = sb("o", [S, D])
        work = sb("work", [ROWS, 2, 8, S])
        tru = sb("tru", [ROWS, 2, 8, S])
        top8 = sb("top8", [ROWS, 8, 8])
        sc1 = sb("sc1", [ROWS, 2, 8, S])
        sc2 = sb("sc2", [ROWS, 8, S])
        smax = sb("smax", [ROWS, 8])
        ssum = sb("ssum", [ROWS, 8])
        srec = sb("srec", [ROWS, 8])
        pT = sb("pT", [S, 2, HH * S])
        oT = sb("oT", [HALF, 2, S])
        h1b = sb("h1b", [S, 2, D])

        t_h = sb("t_h", [P, 2, D])
        t_stat = sb("t_stat", [P, 8])
        t_mv = sb("t_mv", [P, 4])
        t_xn = sb("t_xn", [P, 2, D])
        t_xT = sb("t_xT", [HALF, 2, P])
        t_q = sb("t_q", [P, P])
        t_e = sb("t_e", [P, 2, NE])
        t_p = sb("t_p", [P, 2, NE])
        t_m = sb("t_m", [P, 8])
        t_top = sb("t_top", [P, 2, 8])
        t_idx = sb("t_idx", [P, 2, 8], U32)
        t_idf = sb("t_idf", [P, 2, 8])
        weights = sb("weights", [P, NT, 2, K4])
        pick = sb("pick", [P, NT, 2, K4, NE], BF16)
        place = sb("place", [P, NT, 2, NE])
        count = sb("count", [P, 2, NE])
        emb_s = sb("emb_s", [P, 2, DS])
        emb_m = sb("emb_m", [P, 8])
        ntile_i = sb("ntile_i", [P, 4], I32)
        ntile = sb("ntile", [P, 2])
        ntile_b = sb("ntile_b", [P, 2, NE])
        base = sb("base", [P, 2, NE])
        ends = sb("ends", [P, 2])
        ended = sb("ended", [P, 2, TILES])
        tile_e = sb("tile_e", [P, 2 * TILES], I32)
        s_at = sb("s_at", [P, NE])
        s_prod = sb("s_prod", [P, K4, NE])
        s_f = sb("s_f", [P, K4])
        s_idx = sb("s_idx", [P, 2, K4], I32)
        s_all = sb("s_all", [P, 2, NT, K4], I32)
        g_idx = sb("g_idx", [P, 2, K4], I32)
        g_in = sb("g_in", [P, 2, K4, D])
        g_sum = sb("g_sum", [P, 2, D])
        m_w = sb("m_w", [P, DEPTH, 2 * P])
        m_x = sb("m_x", [P, DEPTH, D])
        m_xT = sb("m_xT", [P, 2, 2 * P])
        m_y = sb("m_y", [P, DEPTH, D])

        bank = [ctx.enter_context(nc.psum_tensor(f"bank{i}", [P, 512], F32)) for i in range(8)]
        ps_pred = bank[0:2]
        ps_true = bank[2:4]
        ps_front, ps_vp, ps_pt, ps_eo = bank[4], bank[5], bank[6], bank[7]

        for name in (
            "consts", "weights_in", "biases_in", "mid_in", "zeroed", "slots_zeroed", "ids_in", "text_in", "text_out",
            "c_memset", "c_select", "c_iota", "w_sum",
            "x_in", "emb_mm", "emb_turned", "emb_copied", "emb_bias", "emb_stat", "emb_aggr", "emb_rstd", "emb_eps", "ln_eps", "emb_norm", "emb_gamma", "emb_done", "emb_out",
            "hb_in0", "hb_in1", "hbr_in0", "hbr_in1", "ln_stat", "ln_aggr", "ln_rstd", "ln_done", "hbp_done", "xt_mm", "xt_copied", "qk_mm", "v_mm",
            "qk_copied", "ek_done", "qbd_done", "eqbd_done", "v_done", "score_mm", "score_copied",
            "topk", "dve_steps", "gap_done", "masked", "smax_done", "shifted", "exp_done", "ssum_done", "srec_done", "prob_done",
            "pt_mm", "pt_copied", "o_mm", "o_copied", "ot_mm", "ot_copied", "proj_mm", "h1_done", "h1_out0", "h1_out1",
            "emb_sq", "emb_ss", "emb_root", "emb_eps2", "emb_rec", "emb_scaled", "emb_flip", "emb_ready",
            "t_in0", "t_in1", "t_stat", "t_aggr", "t_eps", "t_rstd", "t_norm", "xn_out0", "xn_out1", "t_turn", "t_xt", "t_qmm",
            "t_qd", "t_logit", "t_max", "t_shift", "t_exp", "route", "t_pick", "t_pos", "t_placed", "fresh", "base_steps",
            "count_turn", "base_mm", "ends_mm", "ended_mm", "tiles_known",
            "slot_steps0", "slot_steps1", "slot_ready0", "slot_ready1", "stg_in0", "stg_in1", "sent0", "sent1", "back_ready1", "back_ready2",
            "got0_1", "got1_1", "got0_2", "got1_2", "sum_steps1", "sum_steps2", "summed1", "summed2",
            "resent0", "resent1", "res_in0", "res_in1", "out_done0", "out_done1", "pool_steps",
            *[f"m_in{r}{d}" for r in range(2) for d in range(DEPTH)],
            *[f"m_out{r}{d}" for r in range(2) for d in range(DEPTH)],
            *[f"{n}{r}" for r in range(2) for n in ("m_turn", "m_xt", "m_mm", "m_done")],
        ):
            S_(name)

        block = ctx.enter_context(nc.Block())

        def own16(b, par):
            return b * 8 + (16 - 8 * par)

        def slots_of(eng, slot):
            for b in range(FIRST):
                slot(b, b % 2)
            with eng.Fori(FIRST, LAST, 2) as b:
                slot(b, 0)
                slot(b + 1, 1)
            for b in range(LAST, BATCH + 2):
                slot(b, b % 2)

        def pair(b, par, ahead):
            return (b - par) // 2 + ahead

        def is_static(b):
            return isinstance(b, int)

        def runs(b, lo, hi):
            return not is_static(b) or lo <= b <= hi

        def tiles_of(eng, body):
            body(0, 0)
            body(1, 1)
            with eng.Fori(2, NT - 2, 2) as i:
                body(i, 0)
                body(i + 1, 1)
            body(NT - 1, 0)

        def tiles_ahead(eng, ahead, body):
            ahead(0, 0)
            ahead(1, 1)
            body(0, 0)
            ahead(2, 0)
            body(1, 1)
            with eng.Fori(2, NT - 2, 2) as i:
                ahead(i + 1, 1)
                body(i, 0)
                ahead(i + 2, 0)
                body(i + 1, 1)
            body(NT - 1, 0)

        def own(i, par, each):
            return i * (each // 2) + (each - each // 2 * par)

        def matmuls_of(eng, body):
            for d in range(DEPTH):
                body(d, d)
            with eng.Fori(DEPTH, TILES - DEPTH, DEPTH) as j:
                for d in range(DEPTH):
                    body(j + d, d)
            for d in range(DEPTH):
                body(TILES - DEPTH + d, d)

        def own_m(j, d, each):
            return j * (each // DEPTH) + (each - each // DEPTH * d)

        class Steps:

            def __init__(self, eng, name, per_tile):
                self.eng, self.sem, self.per, self.at, self.base = eng, sem[name], per_tile, per_tile, 0

            def start(self, i):
                assert self.at == self.per, self.at
                self.base, self.at = i * self.per, 0

            def done(self, ins):
                ins.then_inc(self.sem, 1)
                self.at += 1

            def wait(self):
                self.eng.wait_ge(self.sem, self.base + self.at)

        h0_pairs = h0.rearrange("(q s) d -> q s d", s=S)

        @block.sync
        def _(sp):
            sp.dma_start(ids[:], text_ids).then_inc(sem["ids_in"], 16)
            sp.dma_start(wa[:], w_shift_a).then_inc(sem["weights_in"], 16)
            sp.dma_start(wl[:], w_shift_l).then_inc(sem["weights_in"], 16)
            sp.dma_start(wma[:], w_mid_a).then_inc(sem["mid_in"], 16)
            sp.dma_start(wml[:], w_mid_l).then_inc(sem["mid_in"], 16)

            def load_images(p):
                sp.wait_ge(sem["emb_mm"], p)
                sp.dma_start(xa[:], a_x[p] if is_static(p) else a_x[bass.ds(p, 1)].squeeze(0)).then_inc(sem["x_in"], 16)
                sp.dma_start(xl[:], l_x[p] if is_static(p) else l_x[bass.ds(p, 1)].squeeze(0)).then_inc(sem["x_in"], 16)

            def store_patches(p):
                sp.wait_ge(sem["emb_done"], p + 1)
                for j in range(2):
                    row = (2 * p + j) * S
                    sp.dma_start(h0[bass.ds(row, NPATCH), :], tok2[j * NPATCH:(j + 1) * NPATCH, :]).then_inc(sem["emb_out"], 16)

            def load_h0(b, par):
                sp.wait_ge(sem["emb_out"], 32 * (b // 2 + 1) if is_static(b) else (b - par) * 16 + 32)
                if runs(b, 2, BATCH):
                    sp.wait_ge(sem["ln_done"], b - 1)
                sp.dma_start(hb[:, par, :], h0[bass.ds(b * S, S), :]).then_inc(sem[f"hb_in{par}"], 16)

            def load_residual(b, par):
                if runs(b, 2, BATCH):
                    sp.wait_ge(sem["hbp_done"], b - 1)
                sp.dma_start(hbr[:, par, :], h0[bass.ds(b * S, S), :]).then_inc(sem[f"hbr_in{par}"], 16)

            load_images(0)
            sp.dma_start(tok_row[:], tok_vec).then_inc(sem["biases_in"], 16)
            sp.dma_start(tok_b[:], tok_bias).then_inc(sem["biases_in"], 16)
            sp.dma_start(qkv[:], w_qkv).then_inc(sem["biases_in"], 16)
            sp.dma_start(qk_b[:], qk_bias).then_inc(sem["biases_in"], 16)
            sp.dma_start(row_b[:], row_vec).then_inc(sem["biases_in"], 16)
            sp.dma_start(wp[:], w_proj).then_inc(sem["biases_in"], 16)
            sp.dma_start(w_rt[:], w_route).then_inc(sem["biases_in"], 16)
            sp.dma_start(rt_b[:], route_bias).then_inc(sem["biases_in"], 16)
            sp.dma_start(emb_n[:], emb).then_inc(sem["biases_in"], 16)
            load_images(1)
            store_patches(0)
            sp.wait_ge(sem["text_out"], 16 * 32)
            load_h0(0, 0)
            load_h0(1, 1)
            load_images(2)
            store_patches(1)
            load_h0(2, 0)
            sp.wait_ge(sem["zeroed"], 1)

            def store_h1(b, par):
                sp.wait_ge(sem["h1_done"], b + 1)
                sp.dma_start(h1[bass.ds(b * S, S), :], h1b[:, par, :]).then_inc(sem[f"h1_out{par}"], 16)

            slots_flat = slots_x.rearrange("(p s) d -> p (s d)", p=P)

            def slot(b, par):
                if runs(b, 0, BATCH - 1):
                    load_residual(b, par)
                if par == 0 and runs(b, 0, BATCH - 4):
                    load_h0(b + 3, 1)
                if runs(b, 2, BATCH - 3):
                    sp.dma_start(slots_flat[:, bass.ds((b - 2) * ZERO_W, ZERO_W)], zero[:]).then_inc(sem["slots_zeroed"], 16)
                if runs(b, 3, BATCH + 1):
                    store_h1(b - 3, 1 - par)
                if par == 0 and runs(b, 0, BATCH - 8):
                    load_images(pair(b, 0, 3))
                if par == 1 and runs(b, 0, BATCH - 5):
                    store_patches(pair(b, 1, 2))
                if par == 1 and runs(b, 0, BATCH - 4):
                    load_h0(b + 3, 0)

            slots_of(sp, slot)
            store_h1(BATCH - 1, 1)

            for par in range(2):
                sp.wait_ge(sem[f"h1_out{par}"], 16 * (BATCH // 2))

            def load_h1(i, par):
                if not is_static(i) or i >= 2:
                    sp.wait_ge(sem["t_norm"], i - 1)
                sp.dma_start(t_h[:, par, :], h1[bass.ds(i * P, P), :]).then_inc(sem[f"t_in{par}"], 16)

            def store_xn(i, par):
                sp.wait_ge(sem["t_norm"], i + 1)
                sp.dma_start(xn2[bass.ds(i * P, P), :], t_xn[:, par, :]).then_inc(sem[f"xn_out{par}"], 16)

            load_h1(0, 0)
            load_h1(1, 1)
            with sp.Fori(0, NT - 3, 2) as i:
                store_xn(i, 0)
                load_h1(i + 2, 0)
                store_xn(i + 1, 1)
                load_h1(i + 3, 1)
            store_xn(NT - 3, 0)
            load_h1(NT - 1, 0)
            store_xn(NT - 2, 1)
            store_xn(NT - 1, 0)

            sp.wait_ge(sem["xn_out0"], 16 * 9)
            sp.wait_ge(sem["xn_out1"], 16 * 8)
            sp.wait_ge(sem["t_turn"], NT)

            def load_xn(i, par):
                if not is_static(i) or i >= 2:
                    sp.wait_ge(sem[f"sent{par}"], own(i - 2, par, 16 * K4))
                sp.dma_start(t_xn[:, par, :], xn2[bass.ds(i * P, P), :]).then_inc(sem[f"stg_in{par}"], 16)

            load_xn(0, 0)
            load_xn(1, 1)
            with sp.Fori(2, NT - 1, 2) as i:
                load_xn(i, 0)
                load_xn(i + 1, 1)
            load_xn(NT - 1, 0)

            def load_tiles(r, matrices, rows, arrays, width):
                def body(j, d):
                    if not is_static(j) or j >= DEPTH:
                        sp.wait_ge(sem[f"m_mm{r}"], j - DEPTH + 1)
                    e = sp.value_load(tile_e[0:1, bass.ds(j + r * TILES, 1)], min_val=0, max_val=NE - 1)
                    sp.dma_start(m_w[0:rows, d, 0:matrices.shape[2]], matrices[bass.ds(e, 1)].rearrange("e p f -> (e p) f")).then_inc(sem[f"m_in{r}{d}"], 16)
                    sp.dma_start(m_x[:, d, 0:width], arrays[bass.ds(j * P, P), :]).then_inc(sem[f"m_in{r}{d}"], 16)
                matmuls_of(sp, body)

            sp.wait_ge(sem["tiles_known"], 1)
            sp.wait_ge(sem["slots_zeroed"], 16 * N_ZERO)
            sp.wait_ge(sem["sent0"], 16 * K4 * 9)
            sp.wait_ge(sem["sent1"], 16 * K4 * 8)
            load_tiles(0, f_know.rearrange("e (p c) r -> e p (c r)", c=2), HALF, slots_x, D)
            sp.wait_ge(sem["resent0"], 16 * K4 * 9)
            sp.wait_ge(sem["resent1"], 16 * K4 * 8)
            load_tiles(1, r_know, P, slots_g, R)

            out_rows = out.rearrange("b s d -> (b s) d")

            def load_res(i, par):
                if not is_static(i) or i >= 2:
                    sp.wait_ge(sem["summed2"], i - 1)
                sp.dma_start(t_h[:, par, :], h1[bass.ds(i * P, P), :]).then_inc(sem[f"res_in{par}"], 16)

            def store_out(i, par):
                sp.wait_ge(sem["summed2"], i + 1)
                sp.dma_start(out_rows[bass.ds(i * P, P), :], g_sum[:, par, :]).then_inc(sem[f"out_done{par}"], 16)

            load_res(0, 0)
            load_res(1, 1)
            with sp.Fori(0, NT - 3, 2) as i:
                store_out(i, 0)
                load_res(i + 2, 0)
                store_out(i + 1, 1)
                load_res(i + 3, 1)
            store_out(NT - 3, 0)
            load_res(NT - 1, 0)
            store_out(NT - 2, 1)
            store_out(NT - 1, 0)
            sp.wait_ge(sem["out_done0"], 16 * 9)
            sp.wait_ge(sem["out_done1"], 16 * 8)

        @block.gpsimd
        def _(pool):
            nc.gpsimd.memset(ident[:], 0.0)
            nc.gpsimd.memset(minus_half[:], -0.5)
            nc.gpsimd.memset(eps_col[:], EPS)
            nc.gpsimd.memset(ones_f[:], 1.0)
            nc.gpsimd.memset(ones_b[:], 1.0)
            nc.gpsimd.memset(upper_b[:], 1.0)
            nc.gpsimd.memset(upper_f[:], 1.0)
            nc.gpsimd.memset(upper_in[:], 1.0)
            nc.gpsimd.memset(head_mask[:], 1.0).then_inc(sem["c_memset"], 1)
            pool.wait_ge(sem["c_memset"], 1)
            nc.gpsimd.affine_select(out=ident[:], in_=ident[:], compare_op=ALU.not_equal, fill=1.0, base=0,
                                    pattern=[[-1, P]], channel_multiplier=1)
            for m in (upper_b, upper_f):
                nc.gpsimd.affine_select(out=m[:], in_=m[:], compare_op=ALU.is_ge, fill=0.0, base=-1,
                                        pattern=[[1, P]], channel_multiplier=-1)
            nc.gpsimd.affine_select(out=upper_in[:], in_=upper_in[:], compare_op=ALU.is_ge, fill=0.0, base=0,
                                    pattern=[[1, P]], channel_multiplier=-1)
            nc.gpsimd.affine_select(out=head_mask[:], in_=head_mask[:], compare_op=ALU.is_ge, fill=0.0, base=0,
                                    pattern=[[-HD, HH]], channel_multiplier=1).then_inc(sem["c_select"], 1)
            pool.wait_ge(sem["c_select"], 1)
            nc.gpsimd.affine_select(out=head_mask[:], in_=head_mask[:], compare_op=ALU.is_ge, fill=0.0, base=HD - 1,
                                    pattern=[[HD, HH]], channel_multiplier=-1)
            nc.gpsimd.iota(iota_e[:], pattern=[[1, NE]], base=0, channel_multiplier=0,
                           allow_small_or_imprecise_dtypes=True)
            nc.gpsimd.iota(iota_t[:], pattern=[[1, TILES]], base=0, channel_multiplier=0,
                           allow_small_or_imprecise_dtypes=True).then_inc(sem["consts"], 1)

            pool.wait_ge(sem["ids_in"], 16)
            for g in range(8):
                nc.gpsimd.indirect_dma_start(text[:, g, :], None, vocab,
                                             bass.IndirectOffsetOnAxis(ids[:, g:g + 1], 0)).then_inc(sem["text_in"], 16)
            pool.wait_ge(sem["text_in"], 16 * 8)
            for g in range(8):
                for j in range(4):
                    pool.dma_start(h0_pairs[4 * g + j, NPATCH:S, :], text[32 * j:32 * j + 32, g, :]).then_inc(sem["text_out"], 16)

            def residual(b, par):
                pool.wait_ge(sem[f"hbr_in{par}"], own16(b, par))
                if runs(b, 2, BATCH):
                    pool.wait_ge(sem["h1_done"], b - 1)
                nc.gpsimd.tensor_tensor(hbp[:, par, :], hbr[:, par, :], row_b[0:S, 1, :], ALU.add).then_inc(sem["hbp_done"], 1)

            def spread(b, par):
                pool.wait_ge(sem["qk_copied"], b + 1)
                if runs(b, 1, BATCH):
                    pool.wait_ge(sem["score_mm"], b)
                for g in range(2):
                    last = nc.gpsimd.tensor_tensor(
                        qbd[:, g], qk[:, par, g, :].unsqueeze(1).to_broadcast([HALF, HH, S]),
                        head_mask[:].unsqueeze(2).to_broadcast([HALF, HH, S]), ALU.mult)
                last.then_inc(sem["qbd_done"], 1)

            def embed_rstd(p):
                pool.wait_ge(sem["emb_aggr"], p + 1)
                nc.gpsimd.tensor_tensor(tmv[:, 2:3], tmv[:, 1:2], eps_col[0:tmv.shape[0], :], ALU.add).then_inc(sem["emb_eps"], 1)
                pool.wait_ge(sem["emb_eps"], p + 1)
                nc.gpsimd.tensor_tensor(tmv[:, 3:4], tmv[:, 2:3], minus_half[0:tmv.shape[0], :], ALU.pow).then_inc(sem["emb_rstd"], 1)

            def embed_affine(p):
                n = 2 * NPATCH
                pool.wait_ge(sem["emb_norm"], p + 1)
                nc.gpsimd.tensor_tensor(tok[:], tok[:], tok_row[0:n, 0, :], ALU.mult).then_inc(sem["emb_gamma"], 1)
                pool.wait_ge(sem["emb_gamma"], p + 1)
                if runs(p, 1, PAIRS):
                    pool.wait_ge(sem["emb_out"], p * 32)
                nc.gpsimd.tensor_tensor(tok2[:], tok[:], tok_row[0:n, 1, :], ALU.add).then_inc(sem["emb_done"], 1)

            def rstd(b):
                pool.wait_ge(sem["ln_aggr"], b + 1)
                nc.gpsimd.tensor_tensor(mv[:, 2:3], mv[:, 1:2], eps_col[0:mv.shape[0], :], ALU.add).then_inc(sem["ln_eps"], 1)
                pool.wait_ge(sem["ln_eps"], b + 1)
                nc.gpsimd.tensor_tensor(mv[:, 3:4], mv[:, 2:3], minus_half[0:mv.shape[0], :], ALU.pow).then_inc(sem["ln_rstd"], 1)

            pool.wait_ge(sem["biases_in"], 16 * 9)
            embed_rstd(0)
            embed_affine(0)
            rstd(0)
            embed_rstd(1)
            embed_affine(1)
            spread(0, 0)
            rstd(1)

            def slot(b, par):
                if runs(b, 1, BATCH):
                    pool.wait_ge(sem["gap_done"], b)
                    if runs(b, 3, BATCH):
                        pool.wait_ge(sem["pt_mm"], 2 * b - 4)
                    nc.gpsimd.tensor_tensor(sc1[:, 1 - par], work[:, 1 - par], tru[:, 1 - par], ALU.add).then_inc(sem["masked"], 1)
                if runs(b, 0, BATCH - 2):
                    spread(b + 1, 1 - par)
                if runs(b, 1, BATCH):
                    pool.wait_ge(sem["smax_done"], b)
                    nc.gpsimd.tensor_tensor(sc2[:], sc1[:, 1 - par], smax[:].unsqueeze(2).to_broadcast([ROWS, 8, S]),
                                            ALU.subtract).then_inc(sem["shifted"], 1)
                    pool.wait_ge(sem["srec_done"], b)
                    nc.gpsimd.tensor_tensor(sc1[:, 1 - par], sc2[:], srec[:].unsqueeze(2).to_broadcast([ROWS, 8, S]),
                                            ALU.mult).then_inc(sem["prob_done"], 1)
                if par == 1 and runs(b, 0, BATCH - 5):
                    embed_rstd(pair(b, 1, 2))
                if runs(b, 0, BATCH - 3):
                    rstd(b + 2)
                if par == 1 and runs(b, 0, BATCH - 5):
                    embed_affine(pair(b, 1, 2))
                if runs(b, 1, BATCH):
                    residual(b - 1, 1 - par)

            slots_of(pool, slot)

            def t_rstd(i, par):
                pool.wait_ge(sem["t_aggr"], i + 1)
                nc.gpsimd.tensor_tensor(t_mv[:, 2:3], t_mv[:, 1:2], eps_col[:], ALU.add).then_inc(sem["t_eps"], 1)
                pool.wait_ge(sem["t_eps"], i + 1)
                nc.gpsimd.tensor_tensor(t_mv[:, 3:4], t_mv[:, 2:3], minus_half[:], ALU.pow).then_inc(sem["t_rstd"], 1)

            tiles_of(pool, t_rstd)

            pool.wait_ge(sem["slots_zeroed"], 16 * N_ZERO)

            def scatter(src, dst, width, idx, par, done):
                nc.gpsimd.sem_inc(sem["pool_steps"], 1)
                for k in range(K4):
                    nc.gpsimd.indirect_dma_start(dst, bass.IndirectOffsetOnAxis(idx[:, par, k:k + 1], 0),
                                                 src[:, par, 0:width], None).then_inc(sem[f"{done}{par}"], 16)

            def send(i, par):
                pool.wait_ge(sem["slot_ready0"], i + 1)
                pool.wait_ge(sem[f"stg_in{par}"], own(i, par, 16))
                scatter(t_xn, slots_x, D, s_idx, par, "sent")

            tiles_of(pool, send)

            def fetch(r, src, width):
                def body(i, par):
                    pool.wait_ge(sem[f"back_ready{r}"], i + 1)
                    nc.gpsimd.sem_inc(sem["pool_steps"], 1)
                    for k in range(K4):
                        nc.gpsimd.indirect_dma_start(g_in[:, par, k, 0:width], None, src,
                                                     bass.IndirectOffsetOnAxis(g_idx[:, par, k:k + 1], 0)).then_inc(sem[f"got{par}_{r}"], 16)
                return body

            def resend(i, par):
                pool.wait_ge(sem["slot_ready1"], i + 1)
                pool.wait_ge(sem["summed1"], i + 1)
                scatter(g_sum, slots_g, R, s_idx, par, "resent")

            for d in range(DEPTH):
                pool.wait_ge(sem[f"m_out0{d}"], 16 * (TILES // DEPTH))
            tiles_ahead(pool, fetch(1, slots_h, R), resend)
            for d in range(DEPTH):
                pool.wait_ge(sem[f"m_out1{d}"], 16 * (TILES // DEPTH))
            tiles_of(pool, fetch(2, slots_y, D))

        @block.scalar
        def _(act):
            def copy_xt(b, par):
                act.wait_ge(sem["xt_mm"], b + 1)
                if runs(b, 2, BATCH):
                    act.wait_ge(sem["v_mm"], b - 1)
                nc.scalar.activation(xnT[:, par], ps_front[0:HALF, 0:2 * S].rearrange("p (c s) -> p c s", c=2),
                                     ACT.Copy).then_inc(sem["xt_copied"], 1)

            def embed_bias(p):
                act.wait_ge(sem["emb_mm"], p + 1)
                if runs(p, 1, PAIRS):
                    act.wait_ge(sem["emb_turned"], p)
                for e in range(2):
                    last = nc.scalar.activation(tokT[:, e, :], ps_eo[0:HALF, e * 2 * NPATCH:(e + 1) * 2 * NPATCH],
                                                ACT.Identity, bias=tok_b[:, e:e + 1])
                last.then_inc(sem["emb_bias"], 1)

            def embed_copy(p):
                act.wait_ge(sem["emb_turned"], p + 1)
                act.wait_ge(sem["emb_done"], p)
                nc.scalar.activation(tok[:], ps_pt[0:2 * NPATCH, 0:D], ACT.Copy).then_inc(sem["emb_copied"], 1)

            def copy_qk(b, par):
                act.wait_ge(sem["qk_mm"], b + 1)
                for o in range(4):
                    last = nc.scalar.activation(qk[:, par, o, :], ps_front[0:HALF, (2 + o) * S:(3 + o) * S],
                                                ACT.Identity, bias=qk_b[:, o:o + 1])
                last.then_inc(sem["qk_copied"], 1)

            def copy_scores(b, par):
                if runs(b, 2, BATCH):
                    act.wait_ge(sem["masked"], b - 1)
                act.wait_ge(sem["score_mm"], b + 1)
                for g in range(2):
                    nc.scalar.activation(work[:, par, 4 * g:4 * g + 4, :],
                                         ps_pred[g][0:ROWS, 0:4 * S].rearrange("p (c s) -> p c s", c=4), ACT.Copy)
                for g in range(2):
                    last = nc.scalar.activation(tru[:, par, 4 * g:4 * g + 4, :],
                                                ps_true[g][0:ROWS, 0:4 * S].rearrange("p (c s) -> p c s", c=4), ACT.Copy)
                last.then_inc(sem["score_copied"], 1)

            act.wait_ge(sem["biases_in"], 16 * 9)
            embed_bias(0)
            embed_copy(0)
            embed_bias(1)
            copy_xt(0, 0)
            copy_qk(0, 0)
            embed_copy(1)
            copy_scores(0, 0)

            def copy_pt(b, g):
                act.wait_ge(sem["pt_mm"], b * 2 + g + 1)
                if g == 0 and runs(b, 1, BATCH):
                    act.wait_ge(sem["o_mm"], b)
                nc.scalar.activation(pT[:, g, :], ps_pt[0:S, 0:HH * S], ACT.Copy).then_inc(sem["pt_copied"], 1)

            def slot(b, par):
                front = runs(b, 0, BATCH - 2)
                attended = runs(b, 2, BATCH + 1)
                if attended:
                    copy_pt(b - 2, 0)
                if front:
                    copy_xt(b + 1, 1 - par)
                if attended:
                    copy_pt(b - 2, 1)
                if front:
                    copy_qk(b + 1, 1 - par)
                if attended:
                    act.wait_ge(sem["o_mm"], b - 1)
                    if runs(b, 3, BATCH + 1):
                        act.wait_ge(sem["ot_mm"], b - 2)
                    nc.scalar.activation(o[:], ps_eo[0:S, D:2 * D], ACT.Copy).then_inc(sem["o_copied"], 1)
                if par == 1 and runs(b, 0, BATCH - 5):
                    embed_copy(pair(b, 1, 2))
                if runs(b, 1, BATCH):
                    act.wait_ge(sem["shifted"], b)
                    nc.scalar.activation(sc2[:], sc2[:], ACT.Exp, scale=SCALE).then_inc(sem["exp_done"], 1)
                if attended:
                    act.wait_ge(sem["ot_mm"], b - 1)
                    if runs(b, 3, BATCH + 1):
                        act.wait_ge(sem["proj_mm"], b - 2)
                    nc.scalar.activation(oT[:], ps_front[0:HALF, 0:2 * S].rearrange("p (c s) -> p c s", c=2),
                                         ACT.Copy).then_inc(sem["ot_copied"], 1)
                if front:
                    copy_scores(b + 1, 1 - par)
                if par == 0 and runs(b, 0, BATCH - 6):
                    embed_bias(pair(b, 0, 2))

            slots_of(act, slot)

            act.wait_ge(sem["emb_ss"], 1)
            nc.scalar.activation(emb_m[:, 2:4], emb_m[:, 0:2], ACT.Sqrt).then_inc(sem["emb_root"], 1)

            def t_turned(i, par):
                act.wait_ge(sem["t_turn"], i + 1)
                nc.scalar.activation(t_xT[:], bank[0][0:HALF, 0:2 * P].rearrange("p (c s) -> p c s", c=2), ACT.Copy).then_inc(sem["t_xt"], 1)
                act.wait_ge(sem["t_qmm"], i + 1)
                nc.scalar.activation(t_q[:], bank[1][:, 0:P], ACT.Identity, bias=rt_b[:, 0:1]).then_inc(sem["t_qd"], 1)

            def t_exped(i, par):
                act.wait_ge(sem["t_shift"], i + 1)
                nc.scalar.activation(t_e[:], t_e[:], ACT.Exp).then_inc(sem["t_exp"], 1)

            tiles_ahead(act, t_turned, t_exped)

            def keep_tiles(r, arrays, width):
                def body(j, d):
                    act.wait_ge(sem[f"m_mm{r}"], j + 1)
                    if not is_static(j) or j >= DEPTH:
                        act.wait_ge(sem[f"m_out{r}{d}"], own_m(j - DEPTH, d, 16))
                    nc.scalar.activation(m_y[:, d, 0:width], bank[2 + d % 2][:, 0:width], ACT.Copy).then_inc(sem[f"m_done{r}"], 1)
                    act.wait_ge(sem[f"m_done{r}"], j + 1)
                    act.dma_start(arrays[bass.ds(j * P, P), :], m_y[:, d, 0:width]).then_inc(sem[f"m_out{r}{d}"], 16)
                matmuls_of(act, body)

            keep_tiles(0, slots_h, R)
            for d in range(DEPTH):
                act.wait_ge(sem[f"m_out0{d}"], 16 * (TILES // DEPTH))
            keep_tiles(1, slots_y, D)

        @block.tensor
        def _(pe):
            def embed(p, e):
                pe.wait_ge(sem["x_in"], (p + 1) * 32)
                pe.wait_ge(sem["emb_bias"], p)
                half = ps_eo[0:HALF, e * 2 * NPATCH:(e + 1) * 2 * NPATCH]
                for a in range(4):
                    for c in range(4):
                        nc.tensor.matmul(half, wa[:, 4 * a + c, e * HALF:(e + 1) * HALF],
                                         xa[:, :, a:a + 2 * GRID - 1:2, c:c + 2 * GRID - 1:2],
                                         start=(a == 0 and c == 0), stop=False)
                    for c in range(2):
                        last = nc.tensor.matmul(half, wl[:, 2 * a + c, e * HALF:(e + 1) * HALF],
                                                xl[:, :, a:a + 2 * GRID - 1:2, c:c + GRID],
                                                start=False, stop=(a == 3 and c == 1))
                if e == 1:
                    last.then_inc(sem["emb_mm"], 1)

            def embed_turn(p, b):
                pe.wait_ge(sem["emb_bias"], p + 1)
                if runs(p, 1, PAIRS):
                    pe.wait_ge(sem["emb_copied"], p)
                if runs(b, 2, BATCH):
                    pe.wait_ge(sem["pt_copied"], 2 * b - 2)
                for e in range(2):
                    last = nc.tensor.transpose(ps_pt[0:2 * NPATCH, e * HALF:(e + 1) * HALF],
                                               tokT[:, e, :], ident[0:HALF, 0:HALF])
                last.then_inc(sem["emb_turned"], 1)

            def turn_norm(b):
                pe.wait_ge(sem["ln_done"], b + 1)
                if runs(b, 1, BATCH):
                    pe.wait_ge(sem["qk_copied"], b)
                if runs(b, 4, BATCH):
                    pe.wait_ge(sem["ot_copied"], b - 3)
                for c in range(2):
                    last = nc.tensor.transpose(ps_front[0:HALF, c * S:(c + 1) * S], xn[:, c * HALF:(c + 1) * HALF],
                                               ident[0:S, 0:S])
                last.then_inc(sem["xt_mm"], 1)

            def queries_keys(b, par):
                pe.wait_ge(sem["xt_copied"], b + 1)
                for o in range(4):
                    for c in range(2):
                        last = nc.tensor.matmul(ps_front[0:HALF, (2 + o) * S:(3 + o) * S],
                                                qkv[:, c, o * HALF:(o + 1) * HALF], xnT[:, par, c, :],
                                                start=(c == 0), stop=(c == 1))
                last.then_inc(sem["qk_mm"], 1)

            def values(b, par):
                if runs(b, 1, BATCH):
                    pe.wait_ge(sem["v_done"], b)
                if runs(b, 3, BATCH):
                    pe.wait_ge(sem["h1_done"], b - 2)
                for c in range(2):
                    last = nc.tensor.matmul(ps_vp[0:S, 0:D], xnT[:, par, c, :], qkv[:, c, 2 * D:3 * D],
                                            start=(c == 0), stop=(c == 1))
                last.then_inc(sem["v_mm"], 1)

            def scores(b, par):
                pe.wait_ge(sem["eqbd_done"], b + 1)
                if runs(b, 1, BATCH):
                    pe.wait_ge(sem["score_copied"], b)
                for bank2, lhs in ((ps_pred, eqbd), (ps_true, qbd)):
                    for g in range(2):
                        flat = lhs[:, g].rearrange("p h s -> p (h s)")
                        rhs = ek[:, g, :] if lhs is eqbd else qk[:, par, 2 + g, :]
                        for c in range(4):
                            last = nc.tensor.matmul(bank2[g][0:ROWS, c * S:(c + 1) * S], flat[:, c * ROWS:(c + 1) * ROWS],
                                                    rhs, start=True, stop=True)
                last.then_inc(sem["score_mm"], 1)

            def turn_probs(b, par, g):
                if g == 0:
                    pe.wait_ge(sem["prob_done"], b + 1)
                    if par == 0 and runs(b, 0, BATCH - 6):
                        pe.wait_ge(sem["emb_copied"], pair(b, par, 3))
                    if runs(b, 1, BATCH):
                        pe.wait_ge(sem["pt_copied"], 2 * b)
                else:
                    pe.wait_ge(sem["pt_copied"], 2 * b + 1)
                for c in range(4):
                    last = nc.tensor.transpose(ps_pt[0:S, c * ROWS:(c + 1) * ROWS], sc1[:, par, 4 * g + c, :],
                                               ident[0:ROWS, 0:ROWS])
                last.then_inc(sem["pt_mm"], 1)

            def attend(b, par):
                pe.wait_ge(sem["pt_copied"], 2 * b + 2)
                pe.wait_ge(sem["v_done"], b + 1)
                if runs(b, 1, BATCH):
                    pe.wait_ge(sem["o_copied"], b)
                if par == 1 and runs(b, 0, BATCH - 7):
                    pe.wait_ge(sem["emb_bias"], pair(b, par, 4))
                for g in range(2):
                    for h in range(HH):
                        col = (HH * g + h) * HD
                        last = nc.tensor.matmul(ps_eo[0:S, D + col:D + col + HD], pT[:, g, h * S:(h + 1) * S],
                                                v[:, par, col:col + HD], start=True, stop=True)
                last.then_inc(sem["o_mm"], 1)

            def turn_out(b):
                pe.wait_ge(sem["o_copied"], b + 1)
                pe.wait_ge(sem["qk_copied"], b + 4 if runs(b, 0, BATCH - 4) else BATCH)
                for c in range(2):
                    last = nc.tensor.transpose(ps_front[0:HALF, c * S:(c + 1) * S], o[:, c * HALF:(c + 1) * HALF],
                                               ident[0:S, 0:S])
                last.then_inc(sem["ot_mm"], 1)

            def project_out(b):
                pe.wait_ge(sem["ot_copied"], b + 1)
                if is_static(b) and b >= BATCH - 2:
                    pe.wait_ge(sem["v_done"], BATCH)
                    pe.wait_ge(sem["h1_done"], b)
                for g in range(2):
                    last = nc.tensor.matmul(ps_vp[0:S, D:2 * D], oT[:, g, :], wp[:, g, :], start=(g == 0), stop=(g == 1))
                last.then_inc(sem["proj_mm"], 1)

            pe.wait_ge(sem["consts"], 1)
            pe.wait_ge(sem["biases_in"], 16 * 9)
            pe.wait_ge(sem["w_sum"], 1)
            embed(0, 0)
            embed(0, 1)
            embed_turn(0, 0)
            embed(1, 0)
            embed(1, 1)
            turn_norm(0)
            queries_keys(0, 0)
            embed_turn(1, 0)
            scores(0, 0)
            embed(2, 0)

            def slot(b, par):
                front = runs(b, 0, BATCH - 2)
                attended = runs(b, 2, BATCH + 1)
                if attended:
                    turn_probs(b - 2, par, 0)
                if front:
                    turn_norm(b + 1)
                if attended:
                    turn_probs(b - 2, par, 1)
                if front:
                    queries_keys(b + 1, 1 - par)
                if attended:
                    attend(b - 2, par)
                if par == 1 and runs(b, 0, BATCH - 5):
                    embed_turn(pair(b, 1, 2), b)
                if runs(b, 0, BATCH - 1):
                    values(b, par)
                if attended:
                    turn_out(b - 2)
                if par == 0 and runs(b, 0, BATCH - 6):
                    embed(pair(b, 0, 2), 1)
                if par == 1 and runs(b, 0, BATCH - 7):
                    embed(pair(b, 1, 3), 0)
                if front:
                    scores(b + 1, 1 - par)
                if attended:
                    project_out(b - 2)

            slots_of(pe, slot)

            pe.wait_ge(sem["emb_scaled"], 1)
            nc.tensor.transpose(bank[5][:, 0:P], emb_s[:].rearrange("p r d -> p (r d)"), ident[:]).then_inc(sem["emb_flip"], 1)
            pe.wait_ge(sem["emb_ready"], 1)

            def t_logits(i, par):
                pe.wait_ge(sem["t_norm"], i + 1)
                if not is_static(i) or i >= 1:
                    pe.wait_ge(sem["t_xt"], i)
                for c in range(2):
                    last = nc.tensor.transpose(bank[0][0:HALF, c * P:(c + 1) * P], t_xn[:, par, c * HALF:(c + 1) * HALF], ident[:])
                last.then_inc(sem["t_turn"], 1)
                pe.wait_ge(sem["t_xt"], i + 1)
                if not is_static(i) or i >= 1:
                    pe.wait_ge(sem["t_qd"], i)
                for c in range(2):
                    last = nc.tensor.matmul(bank[1][:, 0:P], w_rt[:, c, :], t_xT[:, c, :], start=(c == 0), stop=(c == 1))
                last.then_inc(sem["t_qmm"], 1)
                pe.wait_ge(sem["t_qd"], i + 1)
                if not is_static(i) or i >= 1:
                    pe.wait_ge(sem["t_shift"], i)
                nc.tensor.matmul(bank[2][:, 0:2 * NE], t_q[:], emb_t[:], start=True, stop=True).then_inc(sem["t_logit"], 1)

            def t_position(i, par):
                pe.wait_ge(sem["t_pick"], i + 1)
                if not is_static(i) or i >= 1:
                    pe.wait_ge(sem["t_placed"], i)
                for b2, m in ((3, upper_b), (4, ones_b)):
                    for k in range(K4):
                        last = nc.tensor.matmul(bank[b2][:, 0:2 * NE].rearrange("p (r n) -> p r n", r=2), m[:],
                                                pick[:, bass.ds(i, 1), :, k, :].rearrange("p i r n -> p (i r) n"),
                                                start=(k == 0), stop=(k == K4 - 1))
                last.then_inc(sem["t_pos"], 1)

            tiles_ahead(pe, t_logits, t_position)

            pe.wait_ge(sem["t_placed"], NT)
            for r in range(2):
                last = nc.tensor.transpose(bank[0][:, r * P:(r + 1) * P], count[:, r, :], ident[:])
            last.then_inc(sem["count_turn"], 1)
            pe.wait_ge(sem["base_steps"], 4)
            for r in range(2):
                last = nc.tensor.matmul(bank[1][:, r * NE:(r + 1) * NE], ntile_b[:, r, :], upper_f[:], start=True, stop=True)
            last.then_inc(sem["base_mm"], 1)
            nc.tensor.matmul(bank[2][:, 0:2], upper_in[:], ntile[:], start=True, stop=True).then_inc(sem["ends_mm"], 1)
            pe.wait_ge(sem["base_steps"], 8)
            nc.tensor.matmul(bank[3][:, 0:2 * TILES], ones_f[:], ended[:].rearrange("p r t -> p (r t)"), start=True, stop=True).then_inc(sem["ended_mm"], 1)

            def multiply_tiles(r, rows, halves, width):
                def turn(j, d):
                    pe.wait_ge(sem[f"m_in{r}{d}"], own_m(j, d, 32))
                    if not is_static(j) or j >= 2:
                        pe.wait_ge(sem[f"m_xt{r}"], j - 1)
                    for c in range(halves):
                        last = nc.tensor.transpose(bank[d % 2][0:rows, c * P:(c + 1) * P], m_x[:, d, c:halves * rows:halves], ident[:])
                    last.then_inc(sem[f"m_turn{r}"], 1)

                def multiply(j, d):
                    pe.wait_ge(sem[f"m_xt{r}"], j + 1)
                    if not is_static(j) or j >= 2:
                        pe.wait_ge(sem[f"m_done{r}"], j - 1)
                    for c in range(halves):
                        last = nc.tensor.matmul(bank[2 + d % 2][:, 0:width], m_xT[0:rows, d % 2, c * P:(c + 1) * P],
                                                m_w[0:rows, d, c * width:(c + 1) * width], start=(c == 0), stop=(c == halves - 1))
                    last.then_inc(sem[f"m_mm{r}"], 1)

                turn(0, 0)
                for d in range(DEPTH):
                    turn(d + 1, (d + 1) % DEPTH)
                    multiply(d, d)
                with pe.Fori(DEPTH, TILES - DEPTH, DEPTH) as j:
                    for d in range(DEPTH):
                        turn(j + d + 1, (d + 1) % DEPTH)
                        multiply(j + d, d)
                for d in range(DEPTH):
                    j = TILES - DEPTH + d
                    if d < DEPTH - 1:
                        turn(j + 1, d + 1)
                    multiply(j, d)

            pe.wait_ge(sem["tiles_known"], 1)
            multiply_tiles(0, HALF, 2, R)
            multiply_tiles(1, P, 1, D)

        @block.vector
        def _(dve):
            def plain():
                dve.sem_inc(sem["dve_steps"], 1)

            def embed_norm(p):
                dve.wait_ge(sem["emb_copied"], p + 1)
                nc.vector.bn_stats(tstat[:, 0:6], tok[:]).then_inc(sem["emb_stat"], 1)
                dve.wait_ge(sem["emb_stat"], p + 1)
                plain()
                nc.vector.bn_aggr(tmv[:, 0:2], tstat[:, 0:6]).then_inc(sem["emb_aggr"], 1)

            def embed_scale(p):
                dve.wait_ge(sem["emb_rstd"], p + 1)
                nc.vector.tensor_scalar(tok[:], tok[:], tmv[:, 0:1], tmv[:, 3:4], ALU.subtract, ALU.mult).then_inc(sem["emb_norm"], 1)

            def norm(b, par):
                dve.wait_ge(sem[f"hb_in{par}"], own16(b, par))
                nc.vector.bn_stats(stat[:, 0:6], hb[:, par, :]).then_inc(sem["ln_stat"], 1)
                dve.wait_ge(sem["ln_stat"], b + 1)
                plain()
                nc.vector.bn_aggr(mv[:, 0:2], stat[:, 0:6]).then_inc(sem["ln_aggr"], 1)

            def scale(b, par):
                dve.wait_ge(sem["ln_rstd"], b + 1)
                if runs(b, 1, BATCH):
                    dve.wait_ge(sem["xt_mm"], b)
                nc.vector.tensor_scalar(xn[:], hb[:, par, :], mv[:, 0:1], mv[:, 3:4], ALU.subtract, ALU.mult).then_inc(sem["ln_done"], 1)

            def quantise(b, par):
                dve.wait_ge(sem["qk_copied"], b + 1)
                if runs(b, 1, BATCH):
                    dve.wait_ge(sem["score_mm"], b)
                nc.vector.tensor_scalar(ek[:].bitcast(U16), qk[:, par, 2:4, :].bitcast(U16)[:, :, 1::2], 0xFF80, None,
                                        ALU.bitwise_and).then_inc(sem["ek_done"], 1)
                dve.wait_ge(sem["qbd_done"], b + 1)
                nc.vector.tensor_scalar(eqbd[:].rearrange("p g h s -> p (g h s)").bitcast(U16),
                                        qbd[:].rearrange("p g h s -> p (g h s)").bitcast(U16)[:, 1::2], 0xFF80, None,
                                        ALU.bitwise_and).then_inc(sem["eqbd_done"], 1)

            def add_bias_v(b, par):
                dve.wait_ge(sem["v_mm"], b + 1)
                if runs(b, 2, BATCH):
                    dve.wait_ge(sem["o_mm"], b - 1)
                    dve.wait_ge(sem["proj_mm"], b - 1)
                nc.vector.tensor_tensor(v[:, par, :], ps_vp[0:S, 0:D], row_b[0:S, 0, :], ALU.add).then_inc(sem["v_done"], 1)

            def take8(b, par, r):
                base = 16 * b + 4 * r
                for half in range(2):
                    if r > 0:
                        dve.wait_ge(sem["topk"], base - 1 + half)
                        plain()
                    for c in range(4 * half, 4 * half + 4):
                        last = nc.vector.max(top8[:, c, :], work[:, par, c, :])
                    last.then_inc(sem["topk"], 1)
                for half in range(2):
                    dve.wait_ge(sem["topk"], base + 1 + half)
                    plain()
                    for c in range(4 * half, 4 * half + 4):
                        last = nc.vector.match_replace(work[:, par, c, :], top8[:, c, :], work[:, par, c, :], TAKEN)
                    last.then_inc(sem["topk"], 1)

            def finish(b, par):
                dve.wait_ge(sem["proj_mm"], b + 1)
                dve.wait_ge(sem["hbp_done"], b + 1)
                if runs(b, 2, BATCH):
                    dve.wait_ge(sem[f"h1_out{par}"], own16(b - 2, par))
                nc.vector.tensor_tensor(h1b[:, par, :], ps_vp[0:S, D:2 * D], hbp[:, par, :], ALU.add).then_inc(sem["h1_done"], 1)

            nc.vector.memset(zero[:], 0.0).then_inc(sem["zeroed"], 1)
            dve.wait_ge(sem["weights_in"], 32)
            dve.wait_ge(sem["mid_in"], 32)
            for a in range(2):
                nc.vector.tensor_tensor(wa[:, 5 + 4 * a:7 + 4 * a, :], wa[:, 5 + 4 * a:7 + 4 * a, :], wma[:, 2 * a:2 * a + 2, :], ALU.add)
                nc.vector.tensor_tensor(wl[64:P, 2 + 2 * a, :], wl[64:P, 2 + 2 * a, :], wml[64:P, a, :], ALU.add)
                last = nc.vector.tensor_tensor(wl[0:64, 3 + 2 * a, :], wl[0:64, 3 + 2 * a, :], wml[0:64, a, :], ALU.add)
            last.then_inc(sem["w_sum"], 1)
            dve.wait_ge(sem["biases_in"], 16 * 9)
            embed_norm(0)
            embed_scale(0)
            norm(0, 0)
            scale(0, 0)
            embed_norm(1)
            embed_scale(1)
            quantise(0, 0)
            norm(1, 1)
            scale(1, 1)

            def slot(b, par):
                take = runs(b, 0, BATCH - 1)
                front = runs(b, 0, BATCH - 2)
                back = runs(b, 1, BATCH)
                embeds = par == 1 and runs(b, 0, BATCH - 5)
                if back:
                    dve.wait_ge(sem["topk"], b * 16)
                    nc.vector.tensor_scalar(work[:, 1 - par], work[:, 1 - par], TAKEN / 2, -BIG, ALU.is_gt, ALU.mult).then_inc(sem["gap_done"], 1)
                if take:
                    dve.wait_ge(sem["score_copied"], b + 1)
                    plain()
                    take8(b, par, 0)
                if runs(b, 3, BATCH + 1):
                    finish(b - 3, 1 - par)
                if back:
                    add_bias_v(b - 1, 1 - par)
                if back:
                    dve.wait_ge(sem["masked"], b)
                    nc.vector.tensor_reduce(smax[:], sc1[:, 1 - par], AX.X, ALU.max).then_inc(sem["smax_done"], 1)
                if take:
                    take8(b, par, 1)
                if front:
                    quantise(b + 1, 1 - par)
                if back:
                    dve.wait_ge(sem["exp_done"], b)
                    nc.vector.tensor_reduce(ssum[:], sc2[:], AX.X, ALU.add).then_inc(sem["ssum_done"], 1)
                    dve.wait_ge(sem["ssum_done"], b)
                    nc.vector.reciprocal(srec[:], ssum[:]).then_inc(sem["srec_done"], 1)
                if embeds:
                    embed_norm(pair(b, 1, 2))
                if runs(b, 0, BATCH - 3):
                    norm(b + 2, par)
                if take:
                    take8(b, par, 2)
                if runs(b, 0, BATCH - 3):
                    scale(b + 2, par)
                if embeds:
                    embed_scale(pair(b, 1, 2))
                if take:
                    take8(b, par, 3)
                if is_static(b) and b == BATCH + 1:
                    finish(b - 2, par)

            slots_of(dve, slot)

            nc.vector.memset(emb_t[:], 0.0).then_inc(sem["fresh"], 1)
            nc.vector.memset(count[:], 0.0).then_inc(sem["fresh"], 1)
            nc.vector.tensor_tensor(emb_s[:], emb_n[:], emb_n[:], ALU.mult).then_inc(sem["emb_sq"], 1)
            dve.wait_ge(sem["emb_sq"], 1)
            nc.vector.tensor_reduce(emb_m[:, 0:2], emb_s[:], AX.X, ALU.add).then_inc(sem["emb_ss"], 1)
            dve.wait_ge(sem["emb_root"], 1)
            nc.vector.tensor_scalar(emb_m[:, 4:6], emb_m[:, 2:4], 1e-8, None, ALU.add).then_inc(sem["emb_eps2"], 1)
            dve.wait_ge(sem["emb_eps2"], 1)
            nc.vector.reciprocal(emb_m[:, 6:8], emb_m[:, 4:6]).then_inc(sem["emb_rec"], 1)
            dve.wait_ge(sem["emb_rec"], 1)
            for r in range(2):
                last = nc.vector.tensor_scalar(emb_s[:, r, :], emb_n[:, r, :], emb_m[:, 6 + r:7 + r], None, ALU.mult)
            last.then_inc(sem["emb_scaled"], 1)
            dve.wait_ge(sem["emb_flip"], 1)
            dve.wait_ge(sem["fresh"], 2)
            nc.vector.tensor_copy(emb_t[0:DS, 0:NE], bank[5][0:DS, 0:P])
            nc.vector.tensor_copy(emb_t[DS:P, NE:2 * NE], bank[5][DS:P, 0:P]).then_inc(sem["emb_ready"], 1)

            def t_norm(i, par):
                dve.wait_ge(sem[f"t_in{par}"], own(i, par, 16))
                nc.vector.bn_stats(t_stat[:, 0:6], t_h[:, par, :]).then_inc(sem["t_stat"], 1)
                dve.wait_ge(sem["t_stat"], i + 1)
                plain()
                nc.vector.bn_aggr(t_mv[:, 0:2], t_stat[:, 0:6]).then_inc(sem["t_aggr"], 1)
                dve.wait_ge(sem["t_rstd"], i + 1)
                if not is_static(i) or i >= 2:
                    dve.wait_ge(sem["t_turn"], i - 1)
                    dve.wait_ge(sem[f"xn_out{par}"], own(i - 2, par, 16))
                nc.vector.tensor_scalar(t_xn[:, par, :], t_h[:, par, :], t_mv[:, 0:1], t_mv[:, 3:4], ALU.subtract, ALU.mult).then_inc(sem["t_norm"], 1)

            route = Steps(dve, "route", 9)

            def t_route(i, par):
                route.start(i)
                logits = bank[2][:, 0:2 * NE].rearrange("p (r n) -> p r n", r=2)
                dve.wait_ge(sem["t_logit"], i + 1)
                nc.vector.tensor_reduce(t_m[:, 0:2], logits, AX.X, ALU.max).then_inc(sem["t_max"], 1)
                dve.wait_ge(sem["t_max"], i + 1)
                nc.vector.tensor_tensor(t_e[:], logits, t_m[:, 0:2].unsqueeze(2).to_broadcast([P, 2, NE]), ALU.subtract).then_inc(sem["t_shift"], 1)
                dve.wait_ge(sem["t_exp"], i + 1)
                route.done(nc.vector.tensor_reduce(t_m[:, 2:4], t_e[:], AX.X, ALU.add))
                route.wait()
                route.done(nc.vector.reciprocal(t_m[:, 4:6], t_m[:, 2:4]))
                route.wait()
                route.done(nc.vector.tensor_tensor(t_p[:], t_e[:], t_m[:, 4:6].unsqueeze(2).to_broadcast([P, 2, NE]), ALU.mult))
                route.wait()
                plain()
                nc.vector.max(t_top[:, 0, :], t_p[:, 0, :])
                route.done(nc.vector.max(t_top[:, 1, :], t_p[:, 1, :]))
                route.wait()
                plain()
                nc.vector.max_index(t_idx[:, 0, :], t_top[:, 0, :], t_p[:, 0, :])
                nc.vector.max_index(t_idx[:, 1, :], t_top[:, 1, :], t_p[:, 1, :])
                route.done(nc.vector.tensor_reduce(t_m[:, 6:8], t_top[:, :, 0:K4], AX.X, ALU.add))
                route.wait()
                route.done(nc.vector.tensor_scalar(t_m[:, 2:4], t_m[:, 6:8], 1e-8, None, ALU.add))
                nc.vector.tensor_copy(t_idf[:], t_idx[:])
                route.wait()
                route.done(nc.vector.reciprocal(t_m[:, 4:6], t_m[:, 2:4]))
                route.wait()
                route.done(nc.vector.tensor_tensor(weights[:, bass.ds(i, 1), :, :].rearrange("p i r k -> p (i r) k"), t_top[:, :, 0:K4],
                                                   t_m[:, 4:6].unsqueeze(2).to_broadcast([P, 2, K4]), ALU.mult))
                for r in range(2):
                    last = nc.vector.tensor_tensor(pick[:, bass.ds(i, 1), r, :, :].rearrange("p i k n -> p (i k) n"),
                                                   iota_e[:].unsqueeze(1).to_broadcast([P, K4, NE]),
                                                   t_idf[:, r, 0:K4].unsqueeze(2).to_broadcast([P, K4, NE]), ALU.is_equal)
                last.then_inc(sem["t_pick"], 1)
                dve.wait_ge(sem["t_pos"], i + 1)
                route.wait()
                nc.vector.tensor_tensor(place[:, bass.ds(i, 1), :, :].rearrange("p i r n -> p (i r) n"),
                                        bank[3][:, 0:2 * NE].rearrange("p (r n) -> p r n", r=2), count[:], ALU.add)
                route.done(nc.vector.tensor_tensor(count[:], bank[4][:, 0:2 * NE].rearrange("p (r n) -> p r n", r=2), count[:], ALU.add))
                route.wait()
                nc.vector.sem_inc(sem["t_placed"], 1)

            tiles_ahead(dve, t_norm, t_route)

            steps = Steps(dve, "base_steps", 9)
            steps.start(0)
            dve.wait_ge(sem["count_turn"], 1)
            steps.done(nc.vector.tensor_scalar(ntile_i[:, 0:2], bank[0][:, 0:2 * P:P], float(P - 1), None, ALU.add))
            steps.wait()
            steps.done(nc.vector.tensor_scalar(ntile_i[:, 2:4], ntile_i[:, 0:2], 7, None, ALU.logical_shift_right))
            steps.wait()
            steps.done(nc.vector.tensor_copy(ntile[:], ntile_i[:, 2:4]))
            steps.wait()
            steps.done(nc.vector.tensor_copy(ntile_b[:], ntile[:].unsqueeze(2).to_broadcast([P, 2, NE])))
            dve.wait_ge(sem["base_mm"], 1)
            steps.done(nc.vector.tensor_scalar(base[:].rearrange("p r n -> p (r n)"), bank[1][:, 0:2 * NE], float(P), None, ALU.mult))
            dve.wait_ge(sem["ends_mm"], 1)
            steps.done(nc.vector.tensor_copy(ends[:], bank[2][:, 0:2]))
            steps.wait()
            for r in range(2):
                steps.done(nc.vector.tensor_scalar(ended[:, r, :], iota_t[:], ends[:, r:r + 1], None, ALU.is_ge))
            dve.wait_ge(sem["ended_mm"], 1)
            steps.done(nc.vector.tensor_scalar(tile_e[:], bank[3][:, 0:2 * TILES], float(NE - 1), None, ALU.min))
            steps.wait()
            nc.vector.sem_inc(sem["tiles_known"], 1)

            slot_steps = [Steps(dve, "slot_steps0", 4), Steps(dve, "slot_steps1", 4)]

            def find_slots(r, i, par, sent):
                st = slot_steps[r]
                st.start(i)
                st.done(nc.vector.tensor_tensor(s_at[:], place[:, bass.ds(i, 1), r, :].rearrange("p i n -> p (i n)"), base[:, r, :], ALU.add))
                st.wait()
                st.done(nc.vector.tensor_tensor(s_prod[:], pick[:, bass.ds(i, 1), r, :, :].rearrange("p i k n -> p (i k) n"),
                                                s_at[:].unsqueeze(1).to_broadcast([P, K4, NE]), ALU.mult))
                st.wait()
                st.done(nc.vector.tensor_reduce(s_f[:], s_prod[:], AX.X, ALU.add))
                st.wait()
                if not is_static(i) or i >= 2:
                    dve.wait_ge(sem[f"{sent}{par}"], own(i - 2, par, 16 * K4))
                nc.vector.tensor_copy(s_idx[:, par, :], s_f[:]).then_inc(sem[f"slot_ready{r}"], 1)
                st.done(nc.vector.tensor_copy(s_all[:, r, bass.ds(i, 1), :].rearrange("p i k -> p (i k)"), s_f[:]))
                st.wait()

            tiles_of(dve, lambda i, par: find_slots(0, i, par, "sent"))

            def turned_tiles(r, rows, halves):
                def body(j, d):
                    dve.wait_ge(sem[f"m_turn{r}"], j + 1)
                    if not is_static(j) or j >= 2:
                        dve.wait_ge(sem[f"m_mm{r}"], j - 1)
                    nc.vector.tensor_copy(m_xT[0:rows, d % 2, 0:halves * P], bank[d % 2][0:rows, 0:halves * P]).then_inc(sem[f"m_xt{r}"], 1)
                matmuls_of(dve, body)

            def index_back(r, i, par):
                if not is_static(i) or i >= 2:
                    dve.wait_ge(sem[f"got{par}_{r}"], own(i - 2, par, 16 * K4))
                nc.vector.tensor_copy(g_idx[:, par, :], s_all[:, r - 1, bass.ds(i, 1), :].rearrange("p i k -> p (i k)")).then_inc(sem[f"back_ready{r}"], 1)

            sums = [None, Steps(dve, "sum_steps1", K4), Steps(dve, "sum_steps2", K4 + 1)]

            def sum_back(r, i, par, width, free):
                st = sums[r]
                st.start(i)
                dve.wait_ge(sem[f"got{par}_{r}"], own(i, par, 16 * K4))
                if not is_static(i) or i >= 2:
                    dve.wait_ge(sem[f"{free}{par}"], own(i - 2, par, 16 * (K4 if r == 1 else 1)))
                for k in range(K4):
                    w = weights[:, bass.ds(i, 1), r - 1, k:k + 1].rearrange("p i k -> p (i k)")
                    if k == 0:
                        ins = nc.vector.tensor_scalar(g_sum[:, par, 0:width], g_in[:, par, 0, 0:width], w, None, ALU.mult)
                    else:
                        st.wait()
                        ins = nc.vector.scalar_tensor_tensor(g_sum[:, par, 0:width], g_in[:, par, k, 0:width], w,
                                                             g_sum[:, par, 0:width], ALU.mult, ALU.add)
                    st.done(ins)
                if r == 2:
                    st.wait()
                    dve.wait_ge(sem[f"res_in{par}"], own(i, par, 16))
                    st.done(nc.vector.tensor_tensor(g_sum[:, par, :], g_sum[:, par, :], t_h[:, par, :], ALU.add))
                st.wait()
                nc.vector.sem_inc(sem[f"summed{r}"], 1)

            turned_tiles(0, HALF, 2)

            def middle(i, par):
                find_slots(1, i, par, "resent")
                sum_back(1, i, par, R, "resent")

            dve.wait_ge(sem["sent0"], 16 * K4 * 9)
            dve.wait_ge(sem["sent1"], 16 * K4 * 8)
            tiles_ahead(dve, lambda i, par: index_back(1, i, par), middle)
            turned_tiles(1, P, 1)
            tiles_ahead(dve, lambda i, par: index_back(2, i, par), lambda i, par: sum_back(2, i, par, D, "out_done"))


_INS = ["a_x", "l_x", "text_ids", "w_shift_a", "w_shift_l", "w_mid_a", "w_mid_l", "tok_vec", "tok_bias", "vocab",
        "w_qkv", "qk_bias", "row_vec", "w_proj", "f_know", "r_know", "w_route", "route_bias", "emb"]


def lay_out(x, x_txt, L0_tok_W, L0_tok_b, L0_tok_gamma, L0_tok_beta, L0_txt_weight, L0_attn_qkv_w,
            L0_attn_qkv_b, L0_attn_proj_w, L0_attn_proj_b, L0_ffn_f_know, L0_ffn_r_know, L0_ffn_W_fk,
            L0_ffn_b_fk, L0_ffn_W_rk, L0_ffn_b_rk, L0_ffn_emb_fk, L0_ffn_emb_rk):
    n8 = IMAGE // 8
    blocks = x.reshape(BATCH, CHANNELS, n8, 8, n8, 8).transpose(3, 5, 1, 0, 2, 4).reshape(BLOCK_F, BATCH, n8, n8)
    ring = [(i - 1) % n8 for i in range(HALO)]
    blocks = blocks[:, :, ring][:, :, :, ring]
    pairs = blocks.reshape(BLOCK_F, PAIRS, 2, HALO, HALO).transpose(1, 0, 2, 3, 4)
    a_x = pairs[:, :P]
    l_x = np.concatenate([pairs[:, P:, :, :, 0::2], pairs[:, P:, :, :, 1::2]], axis=1)
    w = L0_tok_W.reshape(D, 5, 2, 8, 2, 8, CHANNELS).transpose(1, 2, 4, 3, 5, 6, 0).reshape(5, 2, 2, BLOCK_F, D)
    shifted = np.zeros((4, 4, BLOCK_F, D), w.dtype)
    for s, (ra, ca) in enumerate([(2, 2), (2, 0), (0, 2), (0, 0)]):
        shifted[ra:ra + 2, ca:ca + 2] = w[s + 1]
    w_shift_a = shifted[:, :, :P].reshape(16, P, D).transpose(1, 0, 2)
    w_shift_l = shifted[:, :, P:].reshape(8, P, D).transpose(1, 0, 2)
    w_mid_a = w[0][:, :, :P].reshape(4, P, D).transpose(1, 0, 2)
    w_mid_l = np.concatenate([w[0][:, 1, P:], w[0][:, 0, P:]], axis=1).transpose(1, 0, 2)
    rows = lambda *v: np.broadcast_to(np.stack(v)[None], (P, len(v), D))
    split = lambda m: m.reshape(2, HALF, -1).transpose(1, 0, 2)
    return {
        "a_x": a_x, "l_x": l_x, "text_ids": x_txt.astype(np.int32).reshape(8, P).T,
        "w_shift_a": w_shift_a, "w_shift_l": w_shift_l, "w_mid_a": w_mid_a, "w_mid_l": w_mid_l,
        "tok_vec": rows(L0_tok_gamma, L0_tok_beta), "tok_bias": L0_tok_b.reshape(2, HALF).T, "vocab": L0_txt_weight,
        "w_qkv": split(L0_attn_qkv_w.T), "qk_bias": L0_attn_qkv_b[:2 * D].reshape(4, HALF).T,
        "row_vec": rows(L0_attn_qkv_b[2 * D:], L0_attn_proj_b), "w_proj": split(L0_attn_proj_w.T),
        "f_know": L0_ffn_f_know, "r_know": L0_ffn_r_know,
        "w_route": split(np.concatenate([L0_ffn_W_fk, L0_ffn_W_rk], axis=1)),
        "route_bias": np.concatenate([L0_ffn_b_fk, L0_ffn_b_rk])[:, None],
        "emb": np.stack([L0_ffn_emb_fk, L0_ffn_emb_rk], axis=1),
    }


def kernel(**inputs):
    import concourse.bacc as _bacc
    from concourse import mybir as _mybir
    from concourse.bass_utils import run_bass_kernel_spmd as _run

    laid = lay_out(**{k: np.asarray(v) for k, v in inputs.items()})
    nc = _bacc.Bacc("TRN2", target_bir_lowering=False, num_devices=1)
    arrays, args = {}, []
    for name in _INS:
        a = np.ascontiguousarray(laid[name])
        arrays[f"in_{name}"] = a
        args.append(nc.dram_tensor(f"in_{name}", a.shape, _mybir.dt.from_np(a.dtype), kind="ExternalInput").ap())
    args.append(nc.dram_tensor("out", (BATCH, S, D), F32, kind="ExternalOutput").ap())
    build(nc, *args)
    r = _run(nc, [arrays], core_ids=[0])
    return r.results[0]["out"]
```

```python
from contextlib import ExitStack

import numpy as np

import concourse.bass as bass
from concourse import mybir

F32 = mybir.dt.float32
BF16 = mybir.dt.bfloat16
I32 = mybir.dt.int32
U32 = mybir.dt.uint32
U16 = mybir.dt.uint16
ALU = mybir.AluOpType
ACT = mybir.ActivationFunctionType
AX = mybir.AxisListType

BATCH, CHANNELS, IMAGE, PATCH = 32, 3, 96, 16
D = 192
HALF = D // 2
HALO = 2 * (IMAGE // PATCH) + 2
GRID = IMAGE // PATCH
NPATCH = GRID * GRID
NTEXT = 32
S = NPATCH + NTEXT
T = BATCH * S
QUADS = BATCH // 4
BLOCK_F = 8 * 8 * CHANNELS
HEADS, HD, TOPK = 12, 16, 32
HH = HEADS // 2
ROWS = HH * S // 4
EPS = 1e-5
SCALE = 0.25
TAKEN = -3.0e38
BIG = 1.0e30
NE, R, DS, K4 = 128, 128, 64, 4
P = 128
NT = T // P
TILES = T * K4 // P + NE
SLOTS = TILES * P
PT = HEADS * (HD + 1)
FIRST, LAST = 4, 24
N_ZERO = 28
ZERO_W = TILES * D // N_ZERO
GROUP = 4
GROUPS = TILES // GROUP
DEPTH = 4


def build(nc, a_x, l_x, text_ids, w_shift_a, w_shift_l, w_mid_a, w_mid_l, tok_vec, tok_bias, vocab,
          w_qkv, qk_bias, row_vec, w_proj, f_know, r_know, w_route, route_bias, emb, out):
    ctx = ExitStack()
    with ctx:
        def sb(name, shape, dt=F32):
            return ctx.enter_context(nc.sbuf_tensor(name, shape, dt))

        sem = {}

        def S_(name):
            sem[name] = ctx.enter_context(nc.semaphore(name))

        def dram(name, shape, dt=F32):
            return nc.dram_tensor(name, shape, dt, kind="Internal").ap()

        h0 = dram("h0", [T, D])
        h1 = dram("h1", [T, D])
        xn2 = dram("xn2", [T, D])
        slots_x = dram("slots_x", [SLOTS, D])
        slots_h = dram("slots_h", [SLOTS, R])
        slots_g = slots_x.rearrange("s d -> (s d)")[0:SLOTS * R].rearrange("(s r) -> s r", r=R)
        slots_y = dram("slots_y", [SLOTS, D])

        ident = sb("ident", [P, P])
        ones_f = sb("ones_f", [P, P])
        ones_b = sb("ones_b", [P, P], BF16)
        upper_b = sb("upper_b", [P, P], BF16)
        upper_f = sb("upper_f", [P, P])
        upper_in = sb("upper_in", [P, P])
        eps_col = sb("eps_col", [P, 1])
        minus_half = sb("minus_half", [P, 1])
        minus_one = sb("minus_one", [P, 1])
        iota_e = sb("iota_e", [P, NE])
        iota_t = sb("iota_t", [P, TILES])
        head_mask = sb("head_mask", [HALF, HH])
        early = sb("early", [P, 38 * D])
        wa = early[:, 0:16 * D].rearrange("p (s d) -> p s d", d=D)
        wl = early[:, 16 * D:24 * D].rearrange("p (s d) -> p s d", d=D)
        wma = early[:, 24 * D:28 * D].rearrange("p (s d) -> p s d", d=D)
        wml = early[:, 28 * D:30 * D].rearrange("p (s d) -> p s d", d=D)
        text = early[:, 30 * D:38 * D].rearrange("p (s d) -> p s d", d=D)
        m_w = early[:, 0:DEPTH * GROUP * 2 * P].rearrange("p (g t f) -> p g t f", g=DEPTH, t=GROUP)
        m_x = early[:, DEPTH * GROUP * 2 * P:DEPTH * GROUP * (2 * P + D)].rearrange("p (g t f) -> p g t f", g=DEPTH, t=GROUP)
        tok_row = sb("tok_row", [P, 2, D])
        tok_b = sb("tok_b", [HALF, 2])
        qkv = sb("qkv", [HALF, 2, 3 * D])
        qk_b = sb("qk_b", [HALF, 4])
        row_b = sb("row_b", [P, 2, D])
        wp = sb("wp", [HALF, 2, D])
        w_rt = sb("w_rt", [HALF, 2, P])
        rt_b = sb("rt_b", [P, 1])
        emb_n = sb("emb_n", [P, 2, DS])
        emb_t = sb("emb_t", [P, 2 * NE])
        zero = sb("zero", [P, ZERO_W])

        ids = sb("ids", [P, 8], I32)
        xa = sb("xa", [P, 4, HALO, HALO])
        xl = sb("xl", [P, 4, HALO, HALO // 2])
        tokT = sb("tokT", [HALF, 2, 4 * NPATCH])
        tok = sb("tok", [2 * NPATCH, D])
        tok2 = sb("tok2", [2 * NPATCH, D])
        tstat = sb("tstat", [2 * NPATCH, 8])
        tmv = sb("tmv", [2 * NPATCH, 4])

        hb = sb("hb", [S, 2, D])
        hbr = sb("hbr", [S, 2, D])
        hbp = sb("hbp", [S, 2, D])
        stat = sb("stat", [S, 8])
        mv = sb("mv", [S, 6])
        xn = sb("xn", [S, D])
        xnT = sb("xnT", [HALF, 2, 2, S])
        qk = sb("qk", [HALF, 2, 4, S])
        ek = sb("ek", [HALF, 2, S], BF16)
        qbd = sb("qbd", [HALF, 2, HH, S])
        eqbd = sb("eqbd", [HALF, 2, HH, S], BF16)
        v = sb("v", [S, 2, HEADS, HD + 1])
        o = sb("o", [S, D])
        work = sb("work", [ROWS, 2, 8, S])
        tru = sb("tru", [ROWS, 2, 8, S])
        top8 = sb("top8", [ROWS, 8, 8])
        sc1 = sb("sc1", [ROWS, 2, 8, S])
        sc2 = sb("sc2", [ROWS, 8, S])
        smax = sb("smax", [ROWS, 8])
        srec = sb("srec", [S, HEADS])
        pT = sb("pT", [S, 2, HH * S])
        oT = sb("oT", [HALF, 2, S])
        h1b = sb("h1b", [S, 2, D])

        t_h = sb("t_h", [P, 2, D])
        t_stat = sb("t_stat", [P, 8])
        t_mv = sb("t_mv", [P, 4])
        t_xn = sb("t_xn", [P, 2, D])
        t_xT = sb("t_xT", [HALF, 2, P])
        t_q = sb("t_q", [P, P])
        t_e = sb("t_e", [P, 2, 2, NE])
        t_p = sb("t_p", [P, 2, NE])
        t_m = sb("t_m", [P, 2, 2])
        t_s = sb("t_s", [P, 10])
        t_top = sb("t_top", [P, 2, 8])
        t_idx = sb("t_idx", [P, 2, 8], U32)
        t_idf = sb("t_idf", [P, 2, 8])
        weights = sb("weights", [P, NT, 2, K4])
        pick = sb("pick", [P, NT, 2, K4, NE], BF16)
        place = sb("place", [P, NT, 2, NE])
        count = sb("count", [P, 2, NE])
        emb_s = sb("emb_s", [P, 2, DS])
        emb_m = sb("emb_m", [P, 8])
        ntile_i = sb("ntile_i", [P, 4], I32)
        ntile = sb("ntile", [P, 2])
        ntile_b = sb("ntile_b", [P, 2, NE])
        base = sb("base", [P, 2, NE])
        ends = sb("ends", [P, 2])
        ended = sb("ended", [P, 2, TILES])
        tile_e = sb("tile_e", [P, 2 * TILES], I32)
        s_at = sb("s_at", [P, NE])
        s_prod = sb("s_prod", [P, K4, NE])
        s_f = sb("s_f", [P, K4])
        s_idx = sb("s_idx", [P, 2, K4], I32)
        s_all = sb("s_all", [P, 2, NT, K4], I32)
        g_idx = sb("g_idx", [P, 2, K4], I32)
        g_in = sb("g_in", [P, 2, K4, D])
        g_sum = sb("g_sum", [P, 2, D])
        m_xT = sb("m_xT", [P, 2, 2 * P])
        m_y = sb("m_y", [P, DEPTH, GROUP, D])

        bank = [ctx.enter_context(nc.psum_tensor(f"bank{i}", [P, 512], F32)) for i in range(8)]
        ps_pred = bank[0:2]
        ps_true = bank[2:4]
        ps_front, ps_vp, ps_pt, ps_eo = bank[4], bank[5], bank[6], bank[7]

        for name in (
            "consts", "weights_in", "biases_in", "mid_in", "zeroed", "slots_zeroed", "ids_in", "text_in", "text_out",
            "c_memset", "c_select", "c_iota", "w_sum",
            "x_in", "emb_mm", "emb_turned", "emb_copied", "emb_bias", "emb_stat", "emb_aggr", "emb_rstd", "emb_eps", "ln_eps", "ln_eps2", "emb_norm", "emb_gamma", "emb_done", "emb_out",
            "hb_in0", "hb_in1", "hbr_in0", "hbr_in1", "ln_stat", "ln_aggr", "ln_rstd", "ln_done", "hbp_done", "xt_mm", "xt_copied", "qk_mm", "v_mm",
            "qk_copied", "ek_done", "qbd_done", "eqbd_done", "v_done", "score_mm", "score_copied",
            "topk", "dve_steps", "gap_done", "masked", "smax_done", "shifted", "exp_done", "srec_done", 
            "pt_mm", "pt_copied", "o_mm", "o_done", "ot_mm", "ot_copied", "proj_mm", "h1_done", "h1_out0", "h1_out1",
            "emb_sq", "emb_ss", "emb_root", "emb_plus", "emb_rec", "emb_scaled", "emb_flip", "emb_ready",
            "t_in0", "t_in1", "t_stat", "t_aggr", "t_eps", "t_rstd", "t_norm", "xn_out0", "xn_out1", "t_turn", "t_xt", "t_qmm",
            "t_qd", "t_logit", "t_max", "t_shift", "t_exp", "route", "t_pick", "t_pos", "t_placed", "fresh", "base_steps",
            "count_turn", "base_mm", "ends_mm", "ended_mm", "tiles_known",
            "slot_steps0", "slot_steps1", "slot_ready0", "slot_ready1", "stg_in0", "stg_in1", "sent0", "sent1", "back_ready1", "back_ready2",
            "got0_1", "got1_1", "got0_2", "got1_2", "sum_steps1", "sum_steps2", "summed1", "summed2",
            "resent0", "resent1", "res_in0", "res_in1", "out_done0", "out_done1", "pool_steps",
            *[f"{n}{r}{d}" for r in range(2) for d in range(DEPTH) for n in ("m_in", "m_out")],
            *[f"{n}{r}" for r in range(2) for n in ("m_turn", "m_xt", "m_mm", "m_done")],
        ):
            S_(name)

        block = ctx.enter_context(nc.Block())

        def own16(b, par):
            return b * 8 + (16 - 8 * par)

        def slots_of(eng, slot):
            for b in range(FIRST):
                slot(b, b % 4)
            with eng.Fori(FIRST, LAST, 4) as b:
                for m in range(4):
                    slot(b + m, m)
            for b in range(LAST, BATCH + 2):
                slot(b, b % 4)

        def pair(b, m, ahead):
            return (b - m % 2) // 2 + ahead

        def quad(b, m, ahead):
            return (b - m) // 4 + ahead

        def is_static(b):
            return isinstance(b, int)

        def runs(b, lo, hi):
            return not is_static(b) or lo <= b <= hi

        def tiles_of(eng, body):
            body(0, 0)
            body(1, 1)
            with eng.Fori(2, NT - 2, 2) as i:
                body(i, 0)
                body(i + 1, 1)
            body(NT - 1, 0)

        def tiles_ahead(eng, ahead, body):
            ahead(0, 0)
            ahead(1, 1)
            body(0, 0)
            ahead(2, 0)
            body(1, 1)
            with eng.Fori(2, NT - 2, 2) as i:
                ahead(i + 1, 1)
                body(i, 0)
                ahead(i + 2, 0)
                body(i + 1, 1)
            body(NT - 1, 0)

        def route_tiles(eng, body):
            body(0, 0)
            body(1, 1)
            with eng.Fori(2, NT - 4, 2) as i:
                body(i, 0)
                body(i + 1, 1)
            for i in range(NT - 3, NT):
                body(i, i % 2)

        def own(i, par, each):
            return i * (each // 2) + (each - each // 2 * par)

        def groups_of(eng, body):
            for d in range(DEPTH):
                body(d, d)
            with eng.Fori(DEPTH, GROUPS - DEPTH, DEPTH) as j:
                for d in range(DEPTH):
                    body(j + d, d)
            body(GROUPS - 1, 0)

        def own_d(j, d, each):
            return j * (each // DEPTH) + (each - each // DEPTH * d)

        class Steps:

            def __init__(self, eng, name, per_tile):
                self.eng, self.sem, self.per, self.at, self.base = eng, sem[name], per_tile, per_tile, 0

            def start(self, i):
                assert self.at == self.per, self.at
                self.base, self.at = i * self.per, 0

            def done(self, ins):
                ins.then_inc(self.sem, 1)
                self.at += 1

            def wait(self):
                self.eng.wait_ge(self.sem, self.base + self.at)

        h0_pairs = h0.rearrange("(q s) d -> q s d", s=S)

        @block.sync
        def _(sp):
            sp.dma_start(ids[:], text_ids).then_inc(sem["ids_in"], 16)

            def load_images(p):
                sp.wait_ge(sem["emb_mm"], p)
                sp.dma_start(xa[:], a_x[p] if is_static(p) else a_x[bass.ds(p, 1)].squeeze(0)).then_inc(sem["x_in"], 16)
                sp.dma_start(xl[:], l_x[p] if is_static(p) else l_x[bass.ds(p, 1)].squeeze(0)).then_inc(sem["x_in"], 16)

            load_images(0)
            sp.dma_start(wa[:], w_shift_a).then_inc(sem["weights_in"], 16)
            sp.dma_start(wl[:], w_shift_l).then_inc(sem["weights_in"], 16)
            sp.dma_start(wma[:], w_mid_a).then_inc(sem["mid_in"], 16)
            sp.dma_start(wml[:], w_mid_l).then_inc(sem["mid_in"], 16)

            def store_patches(p):
                sp.wait_ge(sem["emb_done"], p + 1)
                for j in range(2):
                    row = (2 * p + j) * S
                    sp.dma_start(h0[bass.ds(row, NPATCH), :], tok2[j * NPATCH:(j + 1) * NPATCH, :]).then_inc(sem["emb_out"], 16)

            def load_h0(b, par):
                sp.wait_ge(sem["emb_out"], 32 * (b // 2 + 1) if is_static(b) else (b - par) * 16 + 32)
                if runs(b, 2, BATCH):
                    sp.wait_ge(sem["ln_done"], b - 1)
                sp.dma_start(hb[:, par, :], h0[bass.ds(b * S, S), :]).then_inc(sem[f"hb_in{par}"], 16)

            def load_residual(b, par):
                if runs(b, 2, BATCH):
                    sp.wait_ge(sem["hbp_done"], b - 1)
                sp.dma_start(hbr[:, par, :], h0[bass.ds(b * S, S), :]).then_inc(sem[f"hbr_in{par}"], 16)

            sp.dma_start(tok_row[:], tok_vec).then_inc(sem["biases_in"], 16)
            sp.dma_start(tok_b[:], tok_bias).then_inc(sem["biases_in"], 16)
            sp.dma_start(qkv[:], w_qkv).then_inc(sem["biases_in"], 16)
            sp.dma_start(qk_b[:], qk_bias).then_inc(sem["biases_in"], 16)
            sp.dma_start(row_b[:], row_vec).then_inc(sem["biases_in"], 16)
            sp.dma_start(wp[:], w_proj).then_inc(sem["biases_in"], 16)
            sp.dma_start(w_rt[:], w_route).then_inc(sem["biases_in"], 16)
            sp.dma_start(rt_b[:], route_bias).then_inc(sem["biases_in"], 16)
            sp.dma_start(emb_n[:], emb).then_inc(sem["biases_in"], 16)

            def store_text(g):
                for j in range(4):
                    sp.dma_start(h0_pairs[4 * g + j, NPATCH:S, :], text[32 * j:32 * j + 32, g, :]).then_inc(sem["text_out"], 16)

            sp.wait_ge(sem["text_in"], 16 * 8)
            for g in range(4):
                store_text(g)
            load_images(1)
            store_patches(0)
            sp.wait_ge(sem["text_out"], 16 * 16)
            load_h0(0, 0)
            load_h0(1, 1)
            store_patches(1)
            load_h0(2, 0)
            sp.wait_ge(sem["zeroed"], 2)

            def store_h1(b, par):
                sp.wait_ge(sem["h1_done"], b + 1)
                sp.dma_start(h1[bass.ds(b * S, S), :], h1b[:, par, :]).then_inc(sem[f"h1_out{par}"], 16)

            slots_flat = slots_x.rearrange("(p s) d -> p (s d)", p=P)

            def slot(b, m):
                par = m % 2
                if runs(b, 0, BATCH - 1):
                    load_residual(b, par)
                if par == 0 and runs(b, 0, BATCH - 4):
                    load_h0(b + 3, 1)
                if runs(b, 2, BATCH - 3):
                    sp.dma_start(slots_flat[:, bass.ds((b - 2) * ZERO_W, ZERO_W)], zero[:]).then_inc(sem["slots_zeroed"], 16)
                if runs(b, 3, BATCH + 1):
                    store_h1(b - 3, 1 - par)
                if m == 0 and runs(b, 0, BATCH - 12):
                    load_images(quad(b, m, 2))
                if par == 1 and runs(b, 0, BATCH - 5):
                    store_patches(pair(b, m, 2))
                if par == 1 and runs(b, 0, BATCH - 4):
                    load_h0(b + 3, 0)
                if is_static(b) and b < FIRST:
                    store_text(4 + b)
                if is_static(b) and b == FIRST - 1:
                    sp.wait_ge(sem["text_out"], 16 * 32)

            slots_of(sp, slot)
            store_h1(BATCH - 1, 1)

            for par in range(2):
                sp.wait_ge(sem[f"h1_out{par}"], 16 * (BATCH // 2))

            def load_h1(i, par):
                if not is_static(i) or i >= 2:
                    sp.wait_ge(sem["t_norm"], i - 1)
                sp.dma_start(t_h[:, par, :], h1[bass.ds(i * P, P), :]).then_inc(sem[f"t_in{par}"], 16)

            def store_xn(i, par):
                sp.wait_ge(sem["t_norm"], i + 1)
                sp.dma_start(xn2[bass.ds(i * P, P), :], t_xn[:, par, :]).then_inc(sem[f"xn_out{par}"], 16)

            load_h1(0, 0)
            load_h1(1, 1)
            with sp.Fori(0, NT - 3, 2) as i:
                store_xn(i, 0)
                load_h1(i + 2, 0)
                store_xn(i + 1, 1)
                load_h1(i + 3, 1)
            store_xn(NT - 3, 0)
            load_h1(NT - 1, 0)
            store_xn(NT - 2, 1)
            store_xn(NT - 1, 0)

            sp.wait_ge(sem["xn_out0"], 16 * 9)
            sp.wait_ge(sem["xn_out1"], 16 * 8)
            sp.wait_ge(sem["t_turn"], NT)

            def load_xn(i, par):
                if not is_static(i) or i >= 2:
                    sp.wait_ge(sem[f"sent{par}"], own(i - 2, par, 16 * K4))
                sp.dma_start(t_xn[:, par, :], xn2[bass.ds(i * P, P), :]).then_inc(sem[f"stg_in{par}"], 16)

            load_xn(0, 0)
            load_xn(1, 1)
            with sp.Fori(2, NT - 1, 2) as i:
                load_xn(i, 0)
                load_xn(i + 1, 1)
            load_xn(NT - 1, 0)

            def load_tiles(r, matrices, rows, arrays, width):
                def body(j, d):
                    numbers = nc.values_load_multi_w_load_instructions(
                        tile_e[0:1, bass.ds(j * GROUP + r * TILES, GROUP)], engines=[mybir.EngineType.SP], min_val=0, max_val=NE - 1)[1]
                    if not is_static(j) or j >= DEPTH:
                        sp.wait_ge(sem[f"m_mm{r}"], (j - DEPTH + 1) * GROUP)
                    sp.dma_start(m_x[:, d, :, 0:width], arrays[bass.ds(j * (GROUP * P), GROUP * P), :].rearrange(
                        "(t p) d -> p t d", p=P)).then_inc(sem[f"m_in{r}{d}"], 16)
                    for t, e in enumerate(numbers):
                        sp.dma_start(m_w[0:rows, d, t, 0:matrices.shape[2]],
                                     matrices[bass.ds(e, 1)].rearrange("e p f -> (e p) f")).then_inc(sem[f"m_in{r}{d}"], 16)
                groups_of(sp, body)

            sp.wait_ge(sem["tiles_known"], 1)
            sp.wait_ge(sem["slots_zeroed"], 16 * N_ZERO)
            sp.wait_ge(sem["sent0"], 16 * K4 * 9)
            sp.wait_ge(sem["sent1"], 16 * K4 * 8)
            load_tiles(0, f_know.rearrange("e (p c) r -> e p (c r)", c=2), HALF, slots_x, D)
            sp.wait_ge(sem["resent0"], 16 * K4 * 9)
            sp.wait_ge(sem["resent1"], 16 * K4 * 8)
            load_tiles(1, r_know, P, slots_g, R)

            out_rows = out.rearrange("b s d -> (b s) d")

            def load_res(i, par):
                if not is_static(i) or i >= 2:
                    sp.wait_ge(sem["summed2"], i - 1)
                sp.dma_start(t_h[:, par, :], h1[bass.ds(i * P, P), :]).then_inc(sem[f"res_in{par}"], 16)

            def store_out(i, par):
                sp.wait_ge(sem["summed2"], i + 1)
                sp.dma_start(out_rows[bass.ds(i * P, P), :], g_sum[:, par, :]).then_inc(sem[f"out_done{par}"], 16)

            load_res(0, 0)
            load_res(1, 1)
            with sp.Fori(0, NT - 3, 2) as i:
                store_out(i, 0)
                load_res(i + 2, 0)
                store_out(i + 1, 1)
                load_res(i + 3, 1)
            store_out(NT - 3, 0)
            load_res(NT - 1, 0)
            store_out(NT - 2, 1)
            store_out(NT - 1, 0)
            sp.wait_ge(sem["out_done0"], 16 * 9)
            sp.wait_ge(sem["out_done1"], 16 * 8)

        @block.gpsimd
        def _(pool):
            nc.gpsimd.memset(ident[:], 0.0)
            nc.gpsimd.memset(minus_half[:], -0.5)
            nc.gpsimd.memset(minus_one[:], -1.0)
            nc.gpsimd.memset(eps_col[:], EPS)
            nc.gpsimd.memset(ones_f[:], 1.0)
            nc.gpsimd.memset(ones_b[:], 1.0)
            nc.gpsimd.memset(upper_b[:], 1.0)
            nc.gpsimd.memset(upper_f[:], 1.0)
            nc.gpsimd.memset(upper_in[:], 1.0)
            nc.gpsimd.memset(head_mask[:], 1.0).then_inc(sem["c_memset"], 1)
            pool.wait_ge(sem["c_memset"], 1)
            nc.gpsimd.affine_select(out=ident[:], in_=ident[:], compare_op=ALU.not_equal, fill=1.0, base=0,
                                    pattern=[[-1, P]], channel_multiplier=1)
            for m in (upper_b, upper_f):
                nc.gpsimd.affine_select(out=m[:], in_=m[:], compare_op=ALU.is_ge, fill=0.0, base=-1,
                                        pattern=[[1, P]], channel_multiplier=-1)
            nc.gpsimd.affine_select(out=upper_in[:], in_=upper_in[:], compare_op=ALU.is_ge, fill=0.0, base=0,
                                    pattern=[[1, P]], channel_multiplier=-1)
            nc.gpsimd.affine_select(out=head_mask[:], in_=head_mask[:], compare_op=ALU.is_ge, fill=0.0, base=0,
                                    pattern=[[-HD, HH]], channel_multiplier=1).then_inc(sem["c_select"], 1)
            pool.wait_ge(sem["c_select"], 1)
            nc.gpsimd.affine_select(out=head_mask[:], in_=head_mask[:], compare_op=ALU.is_ge, fill=0.0, base=HD - 1,
                                    pattern=[[HD, HH]], channel_multiplier=-1)
            nc.gpsimd.iota(iota_e[:], pattern=[[1, NE]], base=0, channel_multiplier=0,
                           allow_small_or_imprecise_dtypes=True)
            nc.gpsimd.iota(iota_t[:], pattern=[[1, TILES]], base=0, channel_multiplier=0,
                           allow_small_or_imprecise_dtypes=True).then_inc(sem["consts"], 1)

            pool.wait_ge(sem["ids_in"], 16)
            for g in range(8):
                nc.gpsimd.indirect_dma_start(text[:, g, :], None, vocab,
                                             bass.IndirectOffsetOnAxis(ids[:, g:g + 1], 0)).then_inc(sem["text_in"], 16)

            def residual(b, par):
                pool.wait_ge(sem[f"hbr_in{par}"], own16(b, par))
                if runs(b, 2, BATCH):
                    pool.wait_ge(sem["h1_done"], b - 1)
                nc.gpsimd.tensor_tensor(hbp[:, par, :], hbr[:, par, :], row_b[0:S, 1, :], ALU.add).then_inc(sem["hbp_done"], 1)

            def spread(b, par):
                pool.wait_ge(sem["qk_copied"], b + 1)
                if runs(b, 1, BATCH):
                    pool.wait_ge(sem["score_mm"], b)
                for g in range(2):
                    last = nc.gpsimd.tensor_tensor(
                        qbd[:, g], qk[:, par, g, :].unsqueeze(1).to_broadcast([HALF, HH, S]),
                        head_mask[:].unsqueeze(2).to_broadcast([HALF, HH, S]), ALU.mult)
                last.then_inc(sem["qbd_done"], 1)

            def embed_rstd(p):
                n = 2 * NPATCH
                pool.wait_ge(sem["emb_aggr"], p + 1)
                nc.gpsimd.tensor_tensor(tmv[:, 2:3], tmv[:, 1:2], eps_col[0:n, :], ALU.add).then_inc(sem["emb_eps"], 1)
                pool.wait_ge(sem["emb_eps"], p + 1)
                nc.gpsimd.tensor_tensor(tmv[:, 3:4], tmv[:, 2:3], minus_half[0:n, :], ALU.pow).then_inc(sem["emb_rstd"], 1)

            def embed_affine(p):
                n = 2 * NPATCH
                pool.wait_ge(sem["emb_norm"], p + 1)
                nc.gpsimd.tensor_tensor(tok[:], tok[:], tok_row[0:n, 0, :], ALU.mult).then_inc(sem["emb_gamma"], 1)
                pool.wait_ge(sem["emb_gamma"], p + 1)
                if runs(p, 1, BATCH):
                    pool.wait_ge(sem["emb_out"], p * 32)
                nc.gpsimd.tensor_tensor(tok2[:], tok[:], tok_row[0:n, 1, :], ALU.add).then_inc(sem["emb_done"], 1)

            def rstd(b):
                n = mv.shape[0]
                pool.wait_ge(sem["ln_aggr"], b + 1)
                nc.gpsimd.tensor_tensor(mv[:, 4:5], mv[:, 0:1], minus_one[0:n, :], ALU.mult)
                nc.gpsimd.tensor_tensor(mv[:, 2:3], mv[:, 1:2], eps_col[0:n, :], ALU.add).then_inc(sem["ln_eps"], 1)
                pool.wait_ge(sem["ln_eps"], b + 1)
                nc.gpsimd.tensor_tensor(mv[:, 3:4], mv[:, 2:3], minus_half[0:n, :], ALU.pow).then_inc(sem["ln_eps2"], 1)
                pool.wait_ge(sem["ln_eps2"], b + 1)
                nc.gpsimd.tensor_tensor(mv[:, 5:6], mv[:, 4:5], mv[:, 3:4], ALU.mult).then_inc(sem["ln_rstd"], 1)

            pool.wait_ge(sem["biases_in"], 16 * 9)
            embed_rstd(0)
            embed_affine(0)
            rstd(0)
            embed_rstd(1)
            embed_affine(1)
            spread(0, 0)
            rstd(1)

            def slot(b, m):
                par = m % 2
                if runs(b, 1, BATCH):
                    pool.wait_ge(sem["gap_done"], b)
                    if runs(b, 3, BATCH):
                        pool.wait_ge(sem["pt_mm"], 2 * b - 4)
                    nc.gpsimd.tensor_tensor(sc1[:, 1 - par], work[:, 1 - par], tru[:, 1 - par], ALU.add).then_inc(sem["masked"], 1)
                if runs(b, 0, BATCH - 2):
                    spread(b + 1, 1 - par)
                if runs(b, 1, BATCH):
                    pool.wait_ge(sem["smax_done"], b)
                    if runs(b, 2, BATCH):
                        pool.wait_ge(sem["exp_done"], b - 1)
                    nc.gpsimd.tensor_tensor(sc2[:], sc1[:, 1 - par], smax[:].unsqueeze(2).to_broadcast([ROWS, 8, S]),
                                            ALU.subtract).then_inc(sem["shifted"], 1)
                if runs(b, 0, BATCH - 3):
                    rstd(b + 2)
                if runs(b, 1, BATCH):
                    residual(b - 1, 1 - par)
                if par == 1 and runs(b, 0, BATCH - 5):
                    embed_rstd(pair(b, m, 2))
                    embed_affine(pair(b, m, 2))

            slots_of(pool, slot)

            def t_rstd(i, par):
                pool.wait_ge(sem["t_aggr"], i + 1)
                nc.gpsimd.tensor_tensor(t_mv[:, 2:3], t_mv[:, 1:2], eps_col[:], ALU.add).then_inc(sem["t_eps"], 1)
                pool.wait_ge(sem["t_eps"], i + 1)
                nc.gpsimd.tensor_tensor(t_mv[:, 3:4], t_mv[:, 2:3], minus_half[:], ALU.pow).then_inc(sem["t_rstd"], 1)

            tiles_of(pool, t_rstd)

            pool.wait_ge(sem["slots_zeroed"], 16 * N_ZERO)

            def scatter(src, dst, width, idx, par, done):
                nc.gpsimd.sem_inc(sem["pool_steps"], 1)
                for k in range(K4):
                    nc.gpsimd.indirect_dma_start(dst, bass.IndirectOffsetOnAxis(idx[:, par, k:k + 1], 0),
                                                 src[:, par, 0:width], None).then_inc(sem[f"{done}{par}"], 16)

            def send(i, par):
                pool.wait_ge(sem["slot_ready0"], i + 1)
                pool.wait_ge(sem[f"stg_in{par}"], own(i, par, 16))
                scatter(t_xn, slots_x, D, s_idx, par, "sent")

            tiles_of(pool, send)

            def fetch(r, src, width):
                def body(i, par):
                    pool.wait_ge(sem[f"back_ready{r}"], i + 1)
                    nc.gpsimd.sem_inc(sem["pool_steps"], 1)
                    for k in range(K4):
                        nc.gpsimd.indirect_dma_start(g_in[:, par, k, 0:width], None, src,
                                                     bass.IndirectOffsetOnAxis(g_idx[:, par, k:k + 1], 0)).then_inc(sem[f"got{par}_{r}"], 16)
                return body

            def resend(i, par):
                pool.wait_ge(sem["slot_ready1"], i + 1)
                pool.wait_ge(sem["summed1"], i + 1)
                scatter(g_sum, slots_g, R, s_idx, par, "resent")

            for d in range(DEPTH):
                pool.wait_ge(sem[f"m_out0{d}"], 16 * len(range(d, GROUPS, DEPTH)))
            tiles_ahead(pool, fetch(1, slots_h, R), resend)
            for d in range(DEPTH):
                pool.wait_ge(sem[f"m_out1{d}"], 16 * len(range(d, GROUPS, DEPTH)))
            tiles_of(pool, fetch(2, slots_y, D))

        @block.scalar
        def _(act):
            def copy_xt(b, par):
                act.wait_ge(sem["xt_mm"], b + 1)
                if runs(b, 2, BATCH):
                    act.wait_ge(sem["v_mm"], b - 1)
                nc.scalar.activation(xnT[:, par], ps_front[0:HALF, 0:2 * S].rearrange("p (c s) -> p c s", c=2),
                                     ACT.Copy).then_inc(sem["xt_copied"], 1)

            def embed_bias(p):
                act.wait_ge(sem["emb_mm"], p + 1)
                if runs(p, 1, QUADS):
                    act.wait_ge(sem["emb_turned"], 2 * p)
                for e in range(2):
                    last = nc.scalar.activation(tokT[:, e, :], ps_eo[0:HALF, e * 4 * NPATCH:(e + 1) * 4 * NPATCH],
                                                ACT.Identity, bias=tok_b[:, e:e + 1])
                last.then_inc(sem["emb_bias"], 1)

            def embed_copy(p):
                act.wait_ge(sem["emb_turned"], p + 1)
                act.wait_ge(sem["emb_done"], p)
                nc.scalar.activation(tok[:], ps_pt[0:2 * NPATCH, PT:PT + D], ACT.Copy).then_inc(sem["emb_copied"], 1)

            def copy_qk(b, par):
                act.wait_ge(sem["qk_mm"], b + 1)
                for o in range(4):
                    last = nc.scalar.activation(qk[:, par, o, :], ps_front[0:HALF, (2 + o) * S:(3 + o) * S],
                                                ACT.Identity, bias=qk_b[:, o:o + 1])
                last.then_inc(sem["qk_copied"], 1)

            def copy_scores(b, par):
                if runs(b, 2, BATCH):
                    act.wait_ge(sem["masked"], b - 1)
                act.wait_ge(sem["score_mm"], b + 1)
                for g in range(2):
                    nc.scalar.activation(work[:, par, 4 * g:4 * g + 4, :],
                                         ps_pred[g][0:ROWS, 0:4 * S].rearrange("p (c s) -> p c s", c=4), ACT.Copy)
                for g in range(2):
                    last = nc.scalar.activation(tru[:, par, 4 * g:4 * g + 4, :],
                                                ps_true[g][0:ROWS, 0:4 * S].rearrange("p (c s) -> p c s", c=4), ACT.Copy)
                last.then_inc(sem["score_copied"], 1)

            def scale(b, par):
                act.wait_ge(sem["ln_rstd"], b + 1)
                if runs(b, 1, BATCH):
                    act.wait_ge(sem["xt_mm"], b)
                nc.scalar.activation(xn[:], hb[:, par, :], ACT.Identity, bias=mv[:, 5:6], scale=mv[:, 3:4]).then_inc(sem["ln_done"], 1)

            act.wait_ge(sem["biases_in"], 16 * 9)
            embed_bias(0)
            embed_copy(0)
            scale(0, 0)
            copy_xt(0, 0)
            copy_qk(0, 0)
            embed_copy(1)
            copy_scores(0, 0)
            scale(1, 1)

            def copy_pt(b, g):
                act.wait_ge(sem["pt_mm"], b * 2 + g + 1)
                if g == 0 and runs(b, 1, BATCH):
                    act.wait_ge(sem["o_mm"], b)
                nc.scalar.activation(pT[:, g, :], ps_pt[0:S, 0:HH * S], ACT.Copy).then_inc(sem["pt_copied"], 1)

            def slot(b, m):
                par = m % 2
                front = runs(b, 0, BATCH - 2)
                attended = runs(b, 2, BATCH + 1)
                if attended:
                    copy_pt(b - 2, 0)
                if front:
                    copy_xt(b + 1, 1 - par)
                if attended:
                    copy_pt(b - 2, 1)
                if front:
                    copy_qk(b + 1, 1 - par)
                if runs(b, 1, BATCH):
                    act.wait_ge(sem["shifted"], b)
                    nc.scalar.activation(sc1[:, 1 - par], sc2[:], ACT.Exp, scale=SCALE).then_inc(sem["exp_done"], 1)
                if attended:
                    act.wait_ge(sem["ot_mm"], b - 1)
                    if runs(b, 3, BATCH + 1):
                        act.wait_ge(sem["proj_mm"], b - 2)
                    nc.scalar.activation(oT[:], ps_front[0:HALF, 0:2 * S].rearrange("p (c s) -> p c s", c=2),
                                         ACT.Copy).then_inc(sem["ot_copied"], 1)
                if par == 1 and runs(b, 0, BATCH - 5):
                    embed_copy(pair(b, m, 2))
                if runs(b, 0, BATCH - 3):
                    scale(b + 2, par)
                if front:
                    copy_scores(b + 1, 1 - par)
                if m == 0 and runs(b, 0, BATCH - 8):
                    embed_bias(quad(b, m, 1))

            slots_of(act, slot)

            act.wait_ge(sem["emb_ss"], 1)
            nc.scalar.activation(emb_m[:, 2:4], emb_m[:, 0:2], ACT.Sqrt).then_inc(sem["emb_root"], 1)

            def t_turned(i, par):
                act.wait_ge(sem["t_turn"], i + 1)
                nc.scalar.activation(t_xT[:], bank[0][0:HALF, 0:2 * P].rearrange("p (c s) -> p c s", c=2), ACT.Copy).then_inc(sem["t_xt"], 1)
                act.wait_ge(sem["t_qmm"], i + 1)
                nc.scalar.activation(t_q[:], bank[1][:, 0:P], ACT.Identity, bias=rt_b[:, 0:1]).then_inc(sem["t_qd"], 1)

            def t_exped(i, par):
                act.wait_ge(sem["t_shift"], i + 1)
                nc.scalar.activation(t_e[:, par], t_e[:, par], ACT.Exp).then_inc(sem["t_exp"], 1)

            def t_front(i, par):
                t_turned(i, par)
                t_exped(i, par)

            tiles_of(act, t_front)

            def keep_tiles(r, arrays, width):
                def body(j, d):
                    if not is_static(j) or j >= DEPTH:
                        act.wait_ge(sem[f"m_out{r}{d}"], own_d(j - DEPTH, d, 16))
                    for t in range(GROUP):
                        act.wait_ge(sem[f"m_mm{r}"], j * GROUP + t + 1)
                        nc.scalar.activation(m_y[:, d, t, 0:width], bank[2 + t % 2][:, 0:width], ACT.Copy).then_inc(sem[f"m_done{r}"], 1)
                    act.wait_ge(sem[f"m_done{r}"], (j + 1) * GROUP)
                    act.dma_start(arrays[bass.ds(j * (GROUP * P), GROUP * P), :].rearrange("(t p) d -> p t d", p=P),
                                  m_y[:, d, :, 0:width]).then_inc(sem[f"m_out{r}{d}"], 16)
                groups_of(act, body)

            keep_tiles(0, slots_h, R)
            for d in range(DEPTH):
                act.wait_ge(sem[f"m_out0{d}"], 16 * len(range(d, GROUPS, DEPTH)))
            keep_tiles(1, slots_y, D)

        @block.tensor
        def _(pe):
            def embed(p, k):
                if k == 0:
                    pe.wait_ge(sem["x_in"], (p + 1) * 32)
                    pe.wait_ge(sem["emb_bias"], p)
                e = k // 2
                half = ps_eo[0:HALF, e * 4 * NPATCH:(e + 1) * 4 * NPATCH]
                for a in range(2 * (k % 2), 2 * (k % 2) + 2):
                    for c in range(4):
                        nc.tensor.matmul(half, wa[:, 4 * a + c, e * HALF:(e + 1) * HALF],
                                         xa[:, :, a:a + 2 * GRID - 1:2, c:c + 2 * GRID - 1:2],
                                         start=(a == 0 and c == 0), stop=False)
                    for c in range(2):
                        last = nc.tensor.matmul(half, wl[:, 2 * a + c, e * HALF:(e + 1) * HALF],
                                                xl[:, :, a:a + 2 * GRID - 1:2, c:c + GRID],
                                                start=False, stop=(a == 3 and c == 1))
                if k == 3:
                    last.then_inc(sem["emb_mm"], 1)

            def embed_turn(p, b, q, second):
                pe.wait_ge(sem["emb_bias"], q + 1)
                if runs(p, 1, BATCH):
                    pe.wait_ge(sem["emb_copied"], p)
                if runs(b, 2, BATCH):
                    pe.wait_ge(sem["o_done"], b - 1)
                for e in range(2):
                    last = nc.tensor.transpose(ps_pt[0:2 * NPATCH, PT + e * HALF:PT + (e + 1) * HALF],
                                               tokT[:, e, second * 2 * NPATCH:(second + 1) * 2 * NPATCH], ident[0:HALF, 0:HALF])
                last.then_inc(sem["emb_turned"], 1)

            def turn_norm(b):
                pe.wait_ge(sem["ln_done"], b + 1)
                if runs(b, 1, BATCH):
                    pe.wait_ge(sem["qk_copied"], b)
                if runs(b, 4, BATCH):
                    pe.wait_ge(sem["ot_copied"], b - 3)
                for c in range(2):
                    last = nc.tensor.transpose(ps_front[0:HALF, c * S:(c + 1) * S], xn[:, c * HALF:(c + 1) * HALF],
                                               ident[0:S, 0:S])
                last.then_inc(sem["xt_mm"], 1)

            def queries_keys(b, par):
                pe.wait_ge(sem["xt_copied"], b + 1)
                for o in range(4):
                    for c in range(2):
                        last = nc.tensor.matmul(ps_front[0:HALF, (2 + o) * S:(3 + o) * S],
                                                qkv[:, c, o * HALF:(o + 1) * HALF], xnT[:, par, c, :],
                                                start=(c == 0), stop=(c == 1))
                last.then_inc(sem["qk_mm"], 1)

            def values(b, par):
                if runs(b, 1, BATCH):
                    pe.wait_ge(sem["v_done"], b)
                if runs(b, 3, BATCH):
                    pe.wait_ge(sem["h1_done"], b - 2)
                for c in range(2):
                    last = nc.tensor.matmul(ps_vp[0:S, 0:D], xnT[:, par, c, :], qkv[:, c, 2 * D:3 * D],
                                            start=(c == 0), stop=(c == 1))
                last.then_inc(sem["v_mm"], 1)

            def scores(b, par):
                pe.wait_ge(sem["eqbd_done"], b + 1)
                if runs(b, 1, BATCH):
                    pe.wait_ge(sem["score_copied"], b)
                for bank2, lhs in ((ps_pred, eqbd), (ps_true, qbd)):
                    for g in range(2):
                        flat = lhs[:, g].rearrange("p h s -> p (h s)")
                        rhs = ek[:, g, :] if lhs is eqbd else qk[:, par, 2 + g, :]
                        for c in range(4):
                            last = nc.tensor.matmul(bank2[g][0:ROWS, c * S:(c + 1) * S], flat[:, c * ROWS:(c + 1) * ROWS],
                                                    rhs, start=True, stop=True)
                last.then_inc(sem["score_mm"], 1)

            def turn_probs(b, par, g):
                if g == 0:
                    pe.wait_ge(sem["exp_done"], b + 1)
                    if par == 0 and runs(b, 0, BATCH - 6):
                        pe.wait_ge(sem["emb_copied"], pair(b, par, 3))
                    if runs(b, 1, BATCH):
                        pe.wait_ge(sem["o_done"], b)
                else:
                    pe.wait_ge(sem["pt_copied"], 2 * b + 1)
                for c in range(4):
                    last = nc.tensor.transpose(ps_pt[0:S, c * ROWS:(c + 1) * ROWS], sc1[:, par, 4 * g + c, :],
                                               ident[0:ROWS, 0:ROWS])
                last.then_inc(sem["pt_mm"], 1)

            def attend(b, par):
                pe.wait_ge(sem["pt_copied"], 2 * b + 2)
                pe.wait_ge(sem["v_done"], b + 1)
                for g in range(2):
                    for h in range(HH):
                        head = HH * g + h
                        last = nc.tensor.matmul(ps_pt[0:S, head * (HD + 1):(head + 1) * (HD + 1)], pT[:, g, h * S:(h + 1) * S],
                                                v[:, par, head, :], start=True, stop=True)
                last.then_inc(sem["o_mm"], 1)

            def turn_out(b):
                pe.wait_ge(sem["o_done"], b + 1)
                pe.wait_ge(sem["qk_copied"], b + 4 if runs(b, 0, BATCH - 4) else BATCH)
                for c in range(2):
                    last = nc.tensor.transpose(ps_front[0:HALF, c * S:(c + 1) * S], o[:, c * HALF:(c + 1) * HALF],
                                               ident[0:S, 0:S])
                last.then_inc(sem["ot_mm"], 1)

            def project_out(b):
                pe.wait_ge(sem["ot_copied"], b + 1)
                if is_static(b) and b >= BATCH - 2:
                    pe.wait_ge(sem["v_done"], BATCH)
                    pe.wait_ge(sem["h1_done"], b)
                for g in range(2):
                    last = nc.tensor.matmul(ps_vp[0:S, D:2 * D], oT[:, g, :], wp[:, g, :], start=(g == 0), stop=(g == 1))
                last.then_inc(sem["proj_mm"], 1)

            pe.wait_ge(sem["consts"], 1)
            pe.wait_ge(sem["w_sum"], 1)
            for k in range(4):
                embed(0, k)
            pe.wait_ge(sem["biases_in"], 16 * 9)
            embed_turn(0, 0, 0, 0)
            embed(1, 0)
            turn_norm(0)
            queries_keys(0, 0)
            embed_turn(1, 0, 0, 1)
            embed(1, 1)
            scores(0, 0)
            embed(1, 2)

            def slot(b, m):
                par = m % 2
                front = runs(b, 0, BATCH - 2)
                attended = runs(b, 2, BATCH + 1)
                if attended:
                    turn_probs(b - 2, par, 0)
                if front:
                    turn_norm(b + 1)
                if attended:
                    turn_probs(b - 2, par, 1)
                if front:
                    queries_keys(b + 1, 1 - par)
                if attended:
                    attend(b - 2, par)
                if runs(b, 0, BATCH - 1):
                    values(b, par)
                if runs(b, 0, BATCH - 8):
                    embed(quad(b, m, 1 if m == 0 else 2), (m + 3) % 4)
                if attended:
                    turn_out(b - 2)
                if par == 1 and runs(b, 0, BATCH - 5):
                    embed_turn(pair(b, m, 2), b, quad(b, m, 1), m // 2)
                if front:
                    scores(b + 1, 1 - par)
                if attended:
                    project_out(b - 2)

            slots_of(pe, slot)

            pe.wait_ge(sem["emb_scaled"], 1)
            nc.tensor.transpose(bank[5][:, 0:P], emb_s[:].rearrange("p r d -> p (r d)"), ident[:]).then_inc(sem["emb_flip"], 1)
            pe.wait_ge(sem["emb_ready"], 1)

            def t_turn(i, par):
                pe.wait_ge(sem["t_norm"], i + 1)
                if not is_static(i) or i >= 1:
                    pe.wait_ge(sem["t_xt"], i)
                for c in range(2):
                    last = nc.tensor.transpose(bank[0][0:HALF, c * P:(c + 1) * P], t_xn[:, par, c * HALF:(c + 1) * HALF], ident[:])
                last.then_inc(sem["t_turn"], 1)

            def t_logits(i):
                pe.wait_ge(sem["t_xt"], i + 1)
                if not is_static(i) or i >= 1:
                    pe.wait_ge(sem["t_qd"], i)
                for c in range(2):
                    last = nc.tensor.matmul(bank[1][:, 0:P], w_rt[:, c, :], t_xT[:, c, :], start=(c == 0), stop=(c == 1))
                last.then_inc(sem["t_qmm"], 1)
                pe.wait_ge(sem["t_qd"], i + 1)
                if not is_static(i) or i >= 1:
                    pe.wait_ge(sem["t_shift"], i)
                nc.tensor.matmul(bank[2][:, 0:2 * NE], t_q[:], emb_t[:], start=True, stop=True).then_inc(sem["t_logit"], 1)

            def t_position(i):
                pe.wait_ge(sem["t_pick"], i + 1)
                if not is_static(i) or i >= 1:
                    pe.wait_ge(sem["t_placed"], i)
                for b2, m in ((3, upper_b), (4, ones_b)):
                    for k in range(K4):
                        last = nc.tensor.matmul(bank[b2][:, 0:2 * NE].rearrange("p (r n) -> p r n", r=2), m[:],
                                                pick[:, bass.ds(i, 1), :, k, :].rearrange("p i r n -> p (i r) n"),
                                                start=(k == 0), stop=(k == K4 - 1))
                last.then_inc(sem["t_pos"], 1)

            def t_front(i, par):
                t_turn(i, par)
                t_logits(i)

            def t_both(i, par):
                if not is_static(i) or i >= 1:
                    t_position(i - 1)
                if not (is_static(i) and i + 2 >= NT):
                    t_front(i + 2, par)

            t_front(0, 0)
            t_front(1, 1)
            route_tiles(pe, t_both)
            t_position(NT - 1)

            pe.wait_ge(sem["t_placed"], NT)
            for r in range(2):
                last = nc.tensor.transpose(bank[0][:, r * P:(r + 1) * P], count[:, r, :], ident[:])
            last.then_inc(sem["count_turn"], 1)
            pe.wait_ge(sem["base_steps"], 4)
            for r in range(2):
                last = nc.tensor.matmul(bank[1][:, r * NE:(r + 1) * NE], ntile_b[:, r, :], upper_f[:], start=True, stop=True)
            last.then_inc(sem["base_mm"], 1)
            nc.tensor.matmul(bank[2][:, 0:2], upper_in[:], ntile[:], start=True, stop=True).then_inc(sem["ends_mm"], 1)
            pe.wait_ge(sem["base_steps"], 8)
            nc.tensor.matmul(bank[3][:, 0:2 * TILES], ones_f[:], ended[:].rearrange("p r t -> p (r t)"), start=True, stop=True).then_inc(sem["ended_mm"], 1)

            def multiply_tiles(r, rows, halves, width):
                def turn(j, d, t):
                    if t == 0:
                        pe.wait_ge(sem[f"m_in{r}{d}"], own_d(j, d, 16 * (GROUP + 1)))
                    if not is_static(j) or j * GROUP + t >= 2:
                        pe.wait_ge(sem[f"m_xt{r}"], j * GROUP + t - 1)
                    for c in range(halves):
                        last = nc.tensor.transpose(bank[t % 2][0:rows, c * P:(c + 1) * P], m_x[:, d, t, c:halves * rows:halves], ident[:])
                    last.then_inc(sem[f"m_turn{r}"], 1)

                def multiply(j, d, t):
                    pe.wait_ge(sem[f"m_xt{r}"], j * GROUP + t + 1)
                    if not is_static(j) or j * GROUP + t >= 2:
                        pe.wait_ge(sem[f"m_done{r}"], j * GROUP + t - 1)
                    for c in range(halves):
                        last = nc.tensor.matmul(bank[2 + t % 2][:, 0:width], m_xT[0:rows, t % 2, c * P:(c + 1) * P],
                                                m_w[0:rows, d, t, c * width:(c + 1) * width], start=(c == 0), stop=(c == halves - 1))
                    last.then_inc(sem[f"m_mm{r}"], 1)

                def body(j, d):
                    for t in range(GROUP - 1):
                        turn(j, d, t + 1)
                        multiply(j, d, t)
                    if not (is_static(j) and j == GROUPS - 1):
                        turn(j + 1, (d + 1) % DEPTH, 0)
                    multiply(j, d, GROUP - 1)

                turn(0, 0, 0)
                groups_of(pe, body)

            pe.wait_ge(sem["tiles_known"], 1)
            multiply_tiles(0, HALF, 2, R)
            multiply_tiles(1, P, 1, D)

        @block.vector
        def _(dve):
            def plain():
                dve.sem_inc(sem["dve_steps"], 1)

            def embed_norm(p):
                dve.wait_ge(sem["emb_copied"], p + 1)
                nc.vector.bn_stats(tstat[:, 0:6], tok[:]).then_inc(sem["emb_stat"], 1)
                dve.wait_ge(sem["emb_stat"], p + 1)
                plain()
                nc.vector.bn_aggr(tmv[:, 0:2], tstat[:, 0:6]).then_inc(sem["emb_aggr"], 1)

            def embed_scale(p):
                dve.wait_ge(sem["emb_rstd"], p + 1)
                nc.vector.tensor_scalar(tok[:], tok[:], tmv[:, 0:1], tmv[:, 3:4], ALU.subtract, ALU.mult).then_inc(sem["emb_norm"], 1)

            def norm(b, par):
                dve.wait_ge(sem[f"hb_in{par}"], own16(b, par))
                nc.vector.bn_stats(stat[:, 0:6], hb[:, par, :]).then_inc(sem["ln_stat"], 1)
                dve.wait_ge(sem["ln_stat"], b + 1)
                plain()
                nc.vector.bn_aggr(mv[:, 0:2], stat[:, 0:6]).then_inc(sem["ln_aggr"], 1)

            def quantise(b, par):
                dve.wait_ge(sem["qk_copied"], b + 1)
                if runs(b, 1, BATCH):
                    dve.wait_ge(sem["score_mm"], b)
                nc.vector.tensor_scalar(ek[:].bitcast(U16), qk[:, par, 2:4, :].bitcast(U16)[:, :, 1::2], 0xFF80, None,
                                        ALU.bitwise_and).then_inc(sem["ek_done"], 1)
                dve.wait_ge(sem["qbd_done"], b + 1)
                nc.vector.tensor_scalar(eqbd[:].rearrange("p g h s -> p (g h s)").bitcast(U16),
                                        qbd[:].rearrange("p g h s -> p (g h s)").bitcast(U16)[:, 1::2], 0xFF80, None,
                                        ALU.bitwise_and).then_inc(sem["eqbd_done"], 1)

            def add_bias_v(b, par):
                dve.wait_ge(sem["v_mm"], b + 1)
                if runs(b, 2, BATCH):
                    dve.wait_ge(sem["o_mm"], b - 1)
                    dve.wait_ge(sem["proj_mm"], b - 1)
                nc.vector.tensor_tensor(v[:, par, :, 0:HD], ps_vp[0:S, 0:D].rearrange("p (h c) -> p h c", h=HEADS),
                                        row_b[0:S, 0, :].rearrange("p (h c) -> p h c", h=HEADS), ALU.add).then_inc(sem["v_done"], 1)

            def take8(b, par, r):
                base = 16 * b + 4 * r
                for half in range(2):
                    if r > 0:
                        dve.wait_ge(sem["topk"], base - 1 + half)
                        plain()
                    for c in range(4 * half, 4 * half + 4):
                        last = nc.vector.max(top8[:, c, :], work[:, par, c, :])
                    last.then_inc(sem["topk"], 1)
                for half in range(2):
                    dve.wait_ge(sem["topk"], base + 1 + half)
                    plain()
                    for c in range(4 * half, 4 * half + 4):
                        last = nc.vector.match_replace(work[:, par, c, :], top8[:, c, :], work[:, par, c, :], TAKEN)
                    last.then_inc(sem["topk"], 1)

            def finish(b, par):
                dve.wait_ge(sem["proj_mm"], b + 1)
                dve.wait_ge(sem["hbp_done"], b + 1)
                if runs(b, 2, BATCH):
                    dve.wait_ge(sem[f"h1_out{par}"], own16(b - 2, par))
                nc.vector.tensor_tensor(h1b[:, par, :], ps_vp[0:S, D:2 * D], hbp[:, par, :], ALU.add).then_inc(sem["h1_done"], 1)

            nc.vector.memset(zero[:], 0.0).then_inc(sem["zeroed"], 1)
            nc.vector.memset(v[:], 1.0).then_inc(sem["zeroed"], 1)
            dve.wait_ge(sem["zeroed"], 2)
            dve.wait_ge(sem["weights_in"], 32)
            dve.wait_ge(sem["mid_in"], 32)
            for a in range(2):
                nc.vector.tensor_tensor(wa[:, 5 + 4 * a:7 + 4 * a, :], wa[:, 5 + 4 * a:7 + 4 * a, :], wma[:, 2 * a:2 * a + 2, :], ALU.add)
                nc.vector.tensor_tensor(wl[64:P, 2 + 2 * a, :], wl[64:P, 2 + 2 * a, :], wml[64:P, a, :], ALU.add)
                last = nc.vector.tensor_tensor(wl[0:64, 3 + 2 * a, :], wl[0:64, 3 + 2 * a, :], wml[0:64, a, :], ALU.add)
            last.then_inc(sem["w_sum"], 1)
            dve.wait_ge(sem["biases_in"], 16 * 9)
            embed_norm(0)
            embed_scale(0)
            norm(0, 0)
            embed_norm(1)
            embed_scale(1)
            quantise(0, 0)
            norm(1, 1)

            def slot(b, m):
                par = m % 2
                take = runs(b, 0, BATCH - 1)
                front = runs(b, 0, BATCH - 2)
                back = runs(b, 1, BATCH)
                attended = runs(b, 2, BATCH + 1)
                embeds = par == 1 and runs(b, 0, BATCH - 5)
                if back:
                    dve.wait_ge(sem["topk"], b * 16)
                    nc.vector.tensor_scalar(work[:, 1 - par], work[:, 1 - par], TAKEN / 2, -BIG, ALU.is_gt, ALU.mult).then_inc(sem["gap_done"], 1)
                if runs(b, 3, BATCH + 1):
                    finish(b - 3, 1 - par)
                if back:
                    add_bias_v(b - 1, 1 - par)
                if take:
                    dve.wait_ge(sem["score_copied"], b + 1)
                    plain()
                    take8(b, par, 0)
                if back:
                    dve.wait_ge(sem["masked"], b)
                    nc.vector.tensor_reduce(smax[:], sc1[:, 1 - par], AX.X, ALU.max).then_inc(sem["smax_done"], 1)
                if take:
                    take8(b, par, 1)
                if attended:
                    attended_v = ps_pt[0:S, 0:PT].rearrange("p (h c) -> p h c", h=HEADS)
                    dve.wait_ge(sem["o_mm"], b - 1)
                    nc.vector.reciprocal(srec[:], attended_v[:, :, HD]).then_inc(sem["srec_done"], 1)
                if front:
                    quantise(b + 1, 1 - par)
                if attended:
                    dve.wait_ge(sem["srec_done"], b - 1)
                    if runs(b, 3, BATCH + 1):
                        dve.wait_ge(sem["ot_mm"], b - 2)
                    nc.vector.tensor_tensor(o[:].rearrange("p (h c) -> p h c", h=HEADS), attended_v[:, :, 0:HD],
                                            srec[:].unsqueeze(2).to_broadcast([S, HEADS, HD]), ALU.mult).then_inc(sem["o_done"], 1)
                if runs(b, 0, BATCH - 3):
                    norm(b + 2, par)
                if take:
                    take8(b, par, 2)
                if embeds:
                    embed_norm(pair(b, m, 2))
                if take:
                    take8(b, par, 3)
                if embeds:
                    embed_scale(pair(b, m, 2))
                if is_static(b) and b == BATCH + 1:
                    finish(b - 2, par)

            slots_of(dve, slot)

            nc.vector.memset(emb_t[:], 0.0).then_inc(sem["fresh"], 1)
            nc.vector.memset(count[:], 0.0).then_inc(sem["fresh"], 1)
            nc.vector.tensor_tensor(emb_s[:], emb_n[:], emb_n[:], ALU.mult).then_inc(sem["emb_sq"], 1)
            dve.wait_ge(sem["emb_sq"], 1)
            nc.vector.tensor_reduce(emb_m[:, 0:2], emb_s[:], AX.X, ALU.add).then_inc(sem["emb_ss"], 1)
            dve.wait_ge(sem["emb_root"], 1)
            nc.vector.tensor_scalar(emb_m[:, 4:6], emb_m[:, 2:4], 1e-8, None, ALU.add).then_inc(sem["emb_plus"], 1)
            dve.wait_ge(sem["emb_plus"], 1)
            nc.vector.reciprocal(emb_m[:, 6:8], emb_m[:, 4:6]).then_inc(sem["emb_rec"], 1)
            dve.wait_ge(sem["emb_rec"], 1)
            for r in range(2):
                last = nc.vector.tensor_scalar(emb_s[:, r, :], emb_n[:, r, :], emb_m[:, 6 + r:7 + r], None, ALU.mult)
            last.then_inc(sem["emb_scaled"], 1)
            dve.wait_ge(sem["emb_flip"], 1)
            dve.wait_ge(sem["fresh"], 2)
            nc.vector.tensor_copy(emb_t[0:DS, 0:NE], bank[5][0:DS, 0:P])
            nc.vector.tensor_copy(emb_t[DS:P, NE:2 * NE], bank[5][DS:P, 0:P]).then_inc(sem["emb_ready"], 1)

            def t_stats(i, par):
                dve.wait_ge(sem[f"t_in{par}"], own(i, par, 16))
                nc.vector.bn_stats(t_stat[:, 0:6], t_h[:, par, :]).then_inc(sem["t_stat"], 1)

            def t_aggregate(i):
                dve.wait_ge(sem["t_stat"], i + 1)
                plain()
                nc.vector.bn_aggr(t_mv[:, 0:2], t_stat[:, 0:6]).then_inc(sem["t_aggr"], 1)

            def t_norm(i, par):
                dve.wait_ge(sem["t_rstd"], i + 1)
                if not is_static(i) or i >= 2:
                    dve.wait_ge(sem["t_turn"], i - 1)
                    dve.wait_ge(sem[f"xn_out{par}"], own(i - 2, par, 16))
                nc.vector.tensor_scalar(t_xn[:, par, :], t_h[:, par, :], t_mv[:, 0:1], t_mv[:, 3:4], ALU.subtract, ALU.mult).then_inc(sem["t_norm"], 1)

            logits = bank[2][:, 0:2 * NE].rearrange("p (r n) -> p r n", r=2)

            def t_peak(i, par):
                dve.wait_ge(sem["t_logit"], i + 1)
                nc.vector.tensor_reduce(t_m[:, par, :], logits, AX.X, ALU.max).then_inc(sem["t_max"], 1)

            def t_shift(i, par):
                dve.wait_ge(sem["t_max"], i + 1)
                nc.vector.tensor_tensor(t_e[:, par], logits, t_m[:, par, :].unsqueeze(2).to_broadcast([P, 2, NE]), ALU.subtract).then_inc(sem["t_shift"], 1)

            def t_place(i):
                dve.wait_ge(sem["t_pos"], i + 1)
                if not is_static(i) or i >= 1:
                    dve.wait_ge(sem["t_placed"], i)
                nc.vector.tensor_tensor(place[:, bass.ds(i, 1), :, :].rearrange("p i r n -> p (i r) n"),
                                        bank[3][:, 0:2 * NE].rearrange("p (r n) -> p r n", r=2), count[:], ALU.add)
                nc.vector.tensor_tensor(count[:], bank[4][:, 0:2 * NE].rearrange("p (r n) -> p r n", r=2), count[:], ALU.add).then_inc(sem["t_placed"], 1)

            route = Steps(dve, "route", 8)

            def t_route(i, par):
                after = not (is_static(i) and i + 2 >= NT)
                next_ = not (is_static(i) and i + 1 >= NT)
                route.start(i)
                dve.wait_ge(sem["t_exp"], i + 1)
                route.done(nc.vector.tensor_reduce(t_s[:, 0:2], t_e[:, par], AX.X, ALU.add))
                if after:
                    t_stats(i + 2, par)
                route.wait()
                route.done(nc.vector.reciprocal(t_s[:, 2:4], t_s[:, 0:2]))
                if after:
                    t_aggregate(i + 2)
                route.wait()
                route.done(nc.vector.tensor_tensor(t_p[:], t_e[:, par], t_s[:, 2:4].unsqueeze(2).to_broadcast([P, 2, NE]), ALU.mult))
                if next_:
                    t_peak(i + 1, 1 - par)
                route.wait()
                plain()
                nc.vector.max(t_top[:, 0, :], t_p[:, 0, :])
                route.done(nc.vector.max(t_top[:, 1, :], t_p[:, 1, :]))
                if next_:
                    t_shift(i + 1, 1 - par)
                route.wait()
                plain()
                nc.vector.max_index(t_idx[:, 0, :], t_top[:, 0, :], t_p[:, 0, :])
                nc.vector.max_index(t_idx[:, 1, :], t_top[:, 1, :], t_p[:, 1, :])
                route.done(nc.vector.tensor_reduce(t_s[:, 4:6], t_top[:, :, 0:K4], AX.X, ALU.add))
                if after:
                    t_norm(i + 2, par)
                route.wait()
                nc.vector.tensor_copy(t_idf[:], t_idx[:])
                route.done(nc.vector.tensor_scalar(t_s[:, 6:8], t_s[:, 4:6], 1e-8, None, ALU.add))
                if not is_static(i) or i >= 1:
                    t_place(i - 1)
                route.wait()
                route.done(nc.vector.reciprocal(t_s[:, 8:10], t_s[:, 6:8]))
                for r in range(2):
                    last = nc.vector.tensor_tensor(pick[:, bass.ds(i, 1), r, :, :].rearrange("p i k n -> p (i k) n"),
                                                   iota_e[:].unsqueeze(1).to_broadcast([P, K4, NE]),
                                                   t_idf[:, r, 0:K4].unsqueeze(2).to_broadcast([P, K4, NE]), ALU.is_equal)
                last.then_inc(sem["t_pick"], 1)
                route.wait()
                route.done(nc.vector.tensor_tensor(weights[:, bass.ds(i, 1), :, :].rearrange("p i r k -> p (i r) k"), t_top[:, :, 0:K4],
                                                   t_s[:, 8:10].unsqueeze(2).to_broadcast([P, 2, K4]), ALU.mult))

            for par in range(2):
                t_stats(par, par)
                t_aggregate(par)
                t_norm(par, par)
            t_peak(0, 0)
            t_shift(0, 0)
            route_tiles(dve, t_route)
            t_place(NT - 1)
            dve.wait_ge(sem["t_placed"], NT)

            steps = Steps(dve, "base_steps", 9)
            steps.start(0)
            dve.wait_ge(sem["count_turn"], 1)
            steps.done(nc.vector.tensor_scalar(ntile_i[:, 0:2], bank[0][:, 0:2 * P:P], float(P - 1), None, ALU.add))
            steps.wait()
            steps.done(nc.vector.tensor_scalar(ntile_i[:, 2:4], ntile_i[:, 0:2], 7, None, ALU.logical_shift_right))
            steps.wait()
            steps.done(nc.vector.tensor_copy(ntile[:], ntile_i[:, 2:4]))
            steps.wait()
            steps.done(nc.vector.tensor_copy(ntile_b[:], ntile[:].unsqueeze(2).to_broadcast([P, 2, NE])))
            dve.wait_ge(sem["base_mm"], 1)
            steps.done(nc.vector.tensor_scalar(base[:].rearrange("p r n -> p (r n)"), bank[1][:, 0:2 * NE], float(P), None, ALU.mult))
            dve.wait_ge(sem["ends_mm"], 1)
            steps.done(nc.vector.tensor_copy(ends[:], bank[2][:, 0:2]))
            steps.wait()
            for r in range(2):
                steps.done(nc.vector.tensor_scalar(ended[:, r, :], iota_t[:], ends[:, r:r + 1], None, ALU.is_ge))
            dve.wait_ge(sem["ended_mm"], 1)
            steps.done(nc.vector.tensor_scalar(tile_e[:], bank[3][:, 0:2 * TILES], float(NE - 1), None, ALU.min))
            steps.wait()
            nc.vector.sem_inc(sem["tiles_known"], 1)

            slot_steps = [Steps(dve, "slot_steps0", 4), Steps(dve, "slot_steps1", 4)]

            def find_slots(r, i, par, sent):
                st = slot_steps[r]
                st.start(i)
                st.done(nc.vector.tensor_tensor(s_at[:], place[:, bass.ds(i, 1), r, :].rearrange("p i n -> p (i n)"), base[:, r, :], ALU.add))
                st.wait()
                st.done(nc.vector.tensor_tensor(s_prod[:], pick[:, bass.ds(i, 1), r, :, :].rearrange("p i k n -> p (i k) n"),
                                                s_at[:].unsqueeze(1).to_broadcast([P, K4, NE]), ALU.mult))
                st.wait()
                st.done(nc.vector.tensor_reduce(s_f[:], s_prod[:], AX.X, ALU.add))
                st.wait()
                if not is_static(i) or i >= 2:
                    dve.wait_ge(sem[f"{sent}{par}"], own(i - 2, par, 16 * K4))
                nc.vector.tensor_copy(s_idx[:, par, :], s_f[:]).then_inc(sem[f"slot_ready{r}"], 1)
                st.done(nc.vector.tensor_copy(s_all[:, r, bass.ds(i, 1), :].rearrange("p i k -> p (i k)"), s_f[:]))
                st.wait()

            tiles_of(dve, lambda i, par: find_slots(0, i, par, "sent"))

            def turned_tiles(r, rows, halves):
                def body(j, par):
                    for t in range(GROUP):
                        dve.wait_ge(sem[f"m_turn{r}"], j * GROUP + t + 1)
                        if not is_static(j) or j * GROUP + t >= 2:
                            dve.wait_ge(sem[f"m_mm{r}"], j * GROUP + t - 1)
                        nc.vector.tensor_copy(m_xT[0:rows, t % 2, 0:halves * P], bank[t % 2][0:rows, 0:halves * P]).then_inc(sem[f"m_xt{r}"], 1)
                groups_of(dve, body)

            def index_back(r, i, par):
                if not is_static(i) or i >= 2:
                    dve.wait_ge(sem[f"got{par}_{r}"], own(i - 2, par, 16 * K4))
                nc.vector.tensor_copy(g_idx[:, par, :], s_all[:, r - 1, bass.ds(i, 1), :].rearrange("p i k -> p (i k)")).then_inc(sem[f"back_ready{r}"], 1)

            sums = [None, Steps(dve, "sum_steps1", K4), Steps(dve, "sum_steps2", K4 + 1)]

            def sum_back(r, i, par, width, free):
                st = sums[r]
                st.start(i)
                dve.wait_ge(sem[f"got{par}_{r}"], own(i, par, 16 * K4))
                if not is_static(i) or i >= 2:
                    dve.wait_ge(sem[f"{free}{par}"], own(i - 2, par, 16 * (K4 if r == 1 else 1)))
                for k in range(K4):
                    w = weights[:, bass.ds(i, 1), r - 1, k:k + 1].rearrange("p i k -> p (i k)")
                    if k == 0:
                        ins = nc.vector.tensor_scalar(g_sum[:, par, 0:width], g_in[:, par, 0, 0:width], w, None, ALU.mult)
                    else:
                        st.wait()
                        ins = nc.vector.scalar_tensor_tensor(g_sum[:, par, 0:width], g_in[:, par, k, 0:width], w,
                                                             g_sum[:, par, 0:width], ALU.mult, ALU.add)
                    st.done(ins)
                if r == 2:
                    st.wait()
                    dve.wait_ge(sem[f"res_in{par}"], own(i, par, 16))
                    st.done(nc.vector.tensor_tensor(g_sum[:, par, :], g_sum[:, par, :], t_h[:, par, :], ALU.add))
                st.wait()
                nc.vector.sem_inc(sem[f"summed{r}"], 1)

            turned_tiles(0, HALF, 2)

            def middle(i, par):
                find_slots(1, i, par, "resent")
                sum_back(1, i, par, R, "resent")

            dve.wait_ge(sem["sent0"], 16 * K4 * 9)
            dve.wait_ge(sem["sent1"], 16 * K4 * 8)
            tiles_ahead(dve, lambda i, par: index_back(1, i, par), middle)
            turned_tiles(1, P, 1)
            tiles_ahead(dve, lambda i, par: index_back(2, i, par), lambda i, par: sum_back(2, i, par, D, "out_done"))


_INS = ["a_x", "l_x", "text_ids", "w_shift_a", "w_shift_l", "w_mid_a", "w_mid_l", "tok_vec", "tok_bias", "vocab",
        "w_qkv", "qk_bias", "row_vec", "w_proj", "f_know", "r_know", "w_route", "route_bias", "emb"]


def lay_out(x, x_txt, L0_tok_W, L0_tok_b, L0_tok_gamma, L0_tok_beta, L0_txt_weight, L0_attn_qkv_w,
            L0_attn_qkv_b, L0_attn_proj_w, L0_attn_proj_b, L0_ffn_f_know, L0_ffn_r_know, L0_ffn_W_fk,
            L0_ffn_b_fk, L0_ffn_W_rk, L0_ffn_b_rk, L0_ffn_emb_fk, L0_ffn_emb_rk):
    n8 = IMAGE // 8
    blocks = x.reshape(BATCH, CHANNELS, n8, 8, n8, 8).transpose(3, 5, 1, 0, 2, 4).reshape(BLOCK_F, BATCH, n8, n8)
    ring = [(i - 1) % n8 for i in range(HALO)]
    blocks = blocks[:, :, ring][:, :, :, ring]
    quads = blocks.reshape(BLOCK_F, QUADS, 4, HALO, HALO).transpose(1, 0, 2, 3, 4)
    a_x = quads[:, :P]
    l_x = np.concatenate([quads[:, P:, :, :, 0::2], quads[:, P:, :, :, 1::2]], axis=1)
    w = L0_tok_W.reshape(D, 5, 2, 8, 2, 8, CHANNELS).transpose(1, 2, 4, 3, 5, 6, 0).reshape(5, 2, 2, BLOCK_F, D)
    shifted = np.zeros((4, 4, BLOCK_F, D), w.dtype)
    for s, (ra, ca) in enumerate([(2, 2), (2, 0), (0, 2), (0, 0)]):
        shifted[ra:ra + 2, ca:ca + 2] = w[s + 1]
    w_shift_a = shifted[:, :, :P].reshape(16, P, D).transpose(1, 0, 2)
    w_shift_l = shifted[:, :, P:].reshape(8, P, D).transpose(1, 0, 2)
    w_mid_a = w[0][:, :, :P].reshape(4, P, D).transpose(1, 0, 2)
    w_mid_l = np.concatenate([w[0][:, 1, P:], w[0][:, 0, P:]], axis=1).transpose(1, 0, 2)
    rows = lambda *v: np.broadcast_to(np.stack(v)[None], (P, len(v), D))
    split = lambda m: m.reshape(2, HALF, -1).transpose(1, 0, 2)
    return {
        "a_x": a_x, "l_x": l_x, "text_ids": x_txt.astype(np.int32).reshape(8, P).T,
        "w_shift_a": w_shift_a, "w_shift_l": w_shift_l, "w_mid_a": w_mid_a, "w_mid_l": w_mid_l,
        "tok_vec": rows(L0_tok_gamma, L0_tok_beta), "tok_bias": L0_tok_b.reshape(2, HALF).T, "vocab": L0_txt_weight,
        "w_qkv": split(L0_attn_qkv_w.T), "qk_bias": L0_attn_qkv_b[:2 * D].reshape(4, HALF).T,
        "row_vec": rows(L0_attn_qkv_b[2 * D:], L0_attn_proj_b), "w_proj": split(L0_attn_proj_w.T),
        "f_know": L0_ffn_f_know, "r_know": L0_ffn_r_know,
        "w_route": split(np.concatenate([L0_ffn_W_fk, L0_ffn_W_rk], axis=1)),
        "route_bias": np.concatenate([L0_ffn_b_fk, L0_ffn_b_rk])[:, None],
        "emb": np.stack([L0_ffn_emb_fk, L0_ffn_emb_rk], axis=1),
    }


def kernel(**inputs):
    import concourse.bacc as _bacc
    from concourse import mybir as _mybir
    from concourse.bass_utils import run_bass_kernel_spmd as _run

    laid = lay_out(**{k: np.asarray(v) for k, v in inputs.items()})
    nc = _bacc.Bacc("TRN2", target_bir_lowering=False, num_devices=1)
    arrays, args = {}, []
    for name in _INS:
        a = np.ascontiguousarray(laid[name])
        arrays[f"in_{name}"] = a
        args.append(nc.dram_tensor(f"in_{name}", a.shape, _mybir.dt.from_np(a.dtype), kind="ExternalInput").ap())
    args.append(nc.dram_tensor("out", (BATCH, S, D), F32, kind="ExternalOutput").ap())
    build(nc, *args)
    r = _run(nc, [arrays], core_ids=[0])
    return r.results[0]["out"]
```
